# Optimizing a Trainium2 kernel written in Bass

```python
import numpy as np
import jax
import jax.numpy as jnp

def _softmax(x, axis=-1):
    return jax.nn.softmax(x, axis=axis)

def _gelu(x):
    return jax.nn.gelu(x, approximate=True)

def _silu(x):
    return jax.nn.silu(x)

def _sigmoid(x):
    return jax.nn.sigmoid(x)

def _layernorm(x, axis=-1, eps=1e-05):
    m = jnp.mean(x, axis=axis, keepdims=True)
    v = jnp.var(x, axis=axis, keepdims=True)
    return (x - m) / jnp.sqrt(v + eps)

def _scatter_add(tgt, idx, src, axis=0):
    return tgt.at[idx].add(src)

def _segment_sum(src, seg, n):
    return jax.ops.segment_sum(src, seg, n)
kernel_name = 'mk_recurrent_d1_jaxref_r4_60df3b'

def setup_inputs(seed: int=0):
    np.random.seed(seed)
    _w = jnp.asarray

    def _L0_attn_setup():
        import jax, jax.numpy as jnp
        import numpy as np

        def _rope_cos_sin(m, d, dtype=jnp.float32):
            i = jnp.arange(d // 2, dtype=dtype)
            theta = jnp.power(jnp.asarray(10000.0, dtype), -2.0 * (i - 1.0) / d)
            pos = jnp.arange(m, dtype=dtype)
            ang = pos[:, None] * theta[None, :]
            return (jnp.cos(ang), jnp.sin(ang))

        def _rotate(t, cos, sin):
            te = t[..., 0::2]
            to = t[..., 1::2]
            re = te * cos + to * sin
            ro = -te * sin + to * cos
            return jnp.stack((re, ro), axis=-1).reshape(t.shape)
        key = jax.random.key(seed)
        k1, k2, k3, k4 = jax.random.split(key, 4)
        b, m, d = (4, 512, 256)
        scale = 1.0 / np.sqrt(d)
        return {'x': jax.random.normal(k1, (b, m, d), dtype=jnp.float32), 'w_q': jax.random.normal(k2, (d, d), dtype=jnp.float32) * scale, 'w_k': jax.random.normal(k3, (d, d), dtype=jnp.float32) * scale, 'w_v': jax.random.normal(k4, (d, d), dtype=jnp.float32) * scale}
    _L0_attn_in = _L0_attn_setup()

    def _L0_ffn_setup():
        import jax, jax.numpy as jnp
        import numpy as np
        DIM = 256
        DEPTH = 2
        HEADS = 8
        DIM_HEAD = 64
        WINDOW = 128
        INNER = HEADS * DIM_HEAD
        HID = int(DIM * 4 * 2 / 3)
        B, N = (2, 2048)
        QK_SCALE = 8.0

        def shift_token(t):
            t1, t2 = jnp.split(t, 2, axis=-1)
            t2 = jnp.pad(t2, ((0, 0), (1, 0), (0, 0)))[:, :-1]
            return jnp.concatenate([t1, t2], axis=-1)

        def l2norm(t):
            return t / jnp.clip(jnp.linalg.norm(t, axis=-1, keepdims=True), 1e-12)

        def rotate_half(x):
            x1, x2 = jnp.split(x, 2, axis=-1)
            return jnp.concatenate([-x2, x1], axis=-1)

        def rotary_xpos(q, k):
            n = q.shape[-2]
            half_idx = jnp.arange(0, DIM_HEAD, 2, dtype=jnp.float32)
            inv_freq = 1.0 / 10000.0 ** (half_idx / DIM_HEAD)
            t = jnp.arange(n, dtype=jnp.float32)
            freqs = t[:, None] * inv_freq[None, :]
            freqs = jnp.concatenate([freqs, freqs], axis=-1)
            base = (half_idx + 0.4 * DIM_HEAD) / (1.4 * DIM_HEAD)
            power = (t - n // 2) / float(WINDOW // 2)
            scale = base[None, :] ** power[:, None]
            scale = jnp.concatenate([scale, scale], axis=-1)
            cos, sin = (jnp.cos(freqs), jnp.sin(freqs))
            q = q * cos * scale + rotate_half(q) * sin * scale
            k = k * cos / scale + rotate_half(k) * sin / scale
            return (q, k)

        def local_attention(q, k, v):
            b, h, n, d = q.shape
            w = n // WINDOW
            bq = q.reshape(b, h, w, WINDOW, d) * QK_SCALE
            bk = k.reshape(b, h, w, WINDOW, d)
            bv = v.reshape(b, h, w, WINDOW, d)

            def look_around(t):
                p = jnp.pad(t, ((0, 0), (0, 0), (1, 0), (0, 0), (0, 0)))
                return jnp.concatenate([p[:, :, :w], p[:, :, 1:]], axis=3)
            bk, bv = (look_around(bk), look_around(bv))
            bt = jnp.arange(n).reshape(w, WINDOW)
            btp = jnp.pad(bt, ((1, 0), (0, 0)), constant_values=-1)
            btk = jnp.concatenate([btp[:w], btp[1:]], axis=1)
            sim = jnp.einsum('bhwid,bhwjd->bhwij', bq, bk)
            i = bt[:, :, None]
            j = btk[:, None, :]
            mask = (i < j) | (i > j + WINDOW) | (j == -1)
            sim = jnp.where(mask, -jnp.finfo(sim.dtype).max, sim)
            attn = jax.nn.softmax(sim, axis=-1)
            out = jnp.einsum('bhwij,bhwjd->bhwid', attn, bv)
            return out.reshape(b, h, n, d)

        def _layer(x, wqkv, qs, ksc, wo, lg, lb, w1, b1, w2, b2):
            b, n, _ = x.shape
            h = shift_token(x)
            qkv = h @ wqkv
            q, k, v = jnp.split(qkv, 3, axis=-1)
            to_heads = lambda t: t.reshape(b, n, HEADS, DIM_HEAD).transpose(0, 2, 1, 3)
            q, k, v = (to_heads(q), to_heads(k), to_heads(v))
            q = l2norm(q) * qs
            k = l2norm(k) * ksc
            q, k = rotary_xpos(q, k)
            o = local_attention(q, k, v)
            o = o.transpose(0, 2, 1, 3).reshape(b, n, INNER)
            x = x + o @ wo
            h = shift_token(x)
            mu = h.mean(-1, keepdims=True)
            var = h.var(-1, keepdims=True)
            h = (h - mu) / jnp.sqrt(var + 1e-05) * lg + lb
            h = h @ w1 + b1
            a, g = jnp.split(h, 2, axis=-1)
            h = a * jax.nn.gelu(g, approximate=False)
            x = x + h @ w2 + b2
            return x
        key = jax.random.key(seed)
        ks = jax.random.split(key, 6)
        return {'x': jax.random.normal(ks[0], (B, N, DIM), jnp.float32), 'wqkv': jax.random.normal(ks[1], (DEPTH, DIM, 3 * INNER), jnp.float32) * 0.02, 'q_scale': jnp.ones((DEPTH, DIM_HEAD), jnp.float32), 'k_scale': jnp.ones((DEPTH, DIM_HEAD), jnp.float32), 'wo': jax.random.normal(ks[2], (DEPTH, INNER, DIM), jnp.float32) * 0.02, 'ln_g': jnp.ones((DEPTH, DIM), jnp.float32), 'ln_b': jnp.zeros((DEPTH, DIM), jnp.float32), 'w1': jax.random.normal(ks[3], (DEPTH, DIM, 2 * HID), jnp.float32) * 0.02, 'b1': jnp.zeros((DEPTH, 2 * HID), jnp.float32), 'w2': jax.random.normal(ks[4], (DEPTH, HID, DIM), jnp.float32) * 0.02, 'b2': jnp.zeros((DEPTH, DIM), jnp.float32)}
    _L0_ffn_in = _L0_ffn_setup()
    _d = {'L0_attn_x': _L0_attn_in['x'], 'L0_attn_w_q': _L0_attn_in['w_q'], 'L0_attn_w_k': _L0_attn_in['w_k'], 'L0_attn_w_v': _L0_attn_in['w_v'], 'L0_ffn_wqkv': _L0_ffn_in['wqkv'], 'L0_ffn_q_scale': _L0_ffn_in['q_scale'], 'L0_ffn_k_scale': _L0_ffn_in['k_scale'], 'L0_ffn_wo': _L0_ffn_in['wo'], 'L0_ffn_ln_g': _L0_ffn_in['ln_g'], 'L0_ffn_ln_b': _L0_ffn_in['ln_b'], 'L0_ffn_w1': _L0_ffn_in['w1'], 'L0_ffn_b1': _L0_ffn_in['b1'], 'L0_ffn_w2': _L0_ffn_in['w2'], 'L0_ffn_b2': _L0_ffn_in['b2']}
    _x0 = _d['L0_attn_x']
    _d['L0_attn_x'] = jax.random.normal(jax.random.fold_in(jax.random.key(seed), 1), (8, 512, 256), dtype=_x0.dtype)
    del _x0
    return _d

def reference(L0_attn_x, L0_attn_w_q, L0_attn_w_k, L0_attn_w_v, L0_ffn_wqkv, L0_ffn_q_scale, L0_ffn_k_scale, L0_ffn_wo, L0_ffn_ln_g, L0_ffn_ln_b, L0_ffn_w1, L0_ffn_b1, L0_ffn_w2, L0_ffn_b2):

    def _L0_attn_ref(x, w_q, w_k, w_v):
        import jax, jax.numpy as jnp
        import numpy as np

        def _rope_cos_sin(m, d, dtype=jnp.float32):
            i = jnp.arange(d // 2, dtype=dtype)
            theta = jnp.power(jnp.asarray(10000.0, dtype), -2.0 * (i - 1.0) / d)
            pos = jnp.arange(m, dtype=dtype)
            ang = pos[:, None] * theta[None, :]
            return (jnp.cos(ang), jnp.sin(ang))

        def _rotate(t, cos, sin):
            te = t[..., 0::2]
            to = t[..., 1::2]
            re = te * cos + to * sin
            ro = -te * sin + to * cos
            return jnp.stack((re, ro), axis=-1).reshape(t.shape)
        b, m, d = x.shape
        q = jnp.einsum('bmd,ed->bme', x, w_q)
        k = jnp.einsum('bmd,ed->bme', x, w_k)
        v = jnp.einsum('bmd,ed->bme', x, w_v)
        cos, sin = _rope_cos_sin(m, d, x.dtype)
        q_rot = _rotate(q, cos, sin)
        k_rot = _rotate(k, cos, sin)
        scores = jnp.einsum('bqd,bkd->bqk', q_rot, k_rot) / jnp.sqrt(jnp.asarray(d, x.dtype))
        causal = jnp.tril(jnp.ones((m, m), dtype=bool))
        scores = jnp.where(causal[None], scores, jnp.asarray(-jnp.inf, scores.dtype))
        attn = jax.nn.softmax(scores, axis=-1)
        return jnp.einsum('bqk,bkd->bqd', attn, v)

    def _L0_ffn_ref(x, wqkv, q_scale, k_scale, wo, ln_g, ln_b, w1, b1, w2, b2):
        import jax, jax.numpy as jnp
        import numpy as np
        DIM = 256
        DEPTH = 2
        HEADS = 8
        DIM_HEAD = 64
        WINDOW = 128
        INNER = HEADS * DIM_HEAD
        HID = int(DIM * 4 * 2 / 3)
        B, N = (2, 2048)
        QK_SCALE = 8.0

        def shift_token(t):
            t1, t2 = jnp.split(t, 2, axis=-1)
            t2 = jnp.pad(t2, ((0, 0), (1, 0), (0, 0)))[:, :-1]
            return jnp.concatenate([t1, t2], axis=-1)

        def l2norm(t):
            return t / jnp.clip(jnp.linalg.norm(t, axis=-1, keepdims=True), 1e-12)

        def rotate_half(x):
            x1, x2 = jnp.split(x, 2, axis=-1)
            return jnp.concatenate([-x2, x1], axis=-1)

        def rotary_xpos(q, k):
            n = q.shape[-2]
            half_idx = jnp.arange(0, DIM_HEAD, 2, dtype=jnp.float32)
            inv_freq = 1.0 / 10000.0 ** (half_idx / DIM_HEAD)
            t = jnp.arange(n, dtype=jnp.float32)
            freqs = t[:, None] * inv_freq[None, :]
            freqs = jnp.concatenate([freqs, freqs], axis=-1)
            base = (half_idx + 0.4 * DIM_HEAD) / (1.4 * DIM_HEAD)
            power = (t - n // 2) / float(WINDOW // 2)
            scale = base[None, :] ** power[:, None]
            scale = jnp.concatenate([scale, scale], axis=-1)
            cos, sin = (jnp.cos(freqs), jnp.sin(freqs))
            q = q * cos * scale + rotate_half(q) * sin * scale
            k = k * cos / scale + rotate_half(k) * sin / scale
            return (q, k)

        def local_attention(q, k, v):
            b, h, n, d = q.shape
            w = n // WINDOW
            bq = q.reshape(b, h, w, WINDOW, d) * QK_SCALE
            bk = k.reshape(b, h, w, WINDOW, d)
            bv = v.reshape(b, h, w, WINDOW, d)

            def look_around(t):
                p = jnp.pad(t, ((0, 0), (0, 0), (1, 0), (0, 0), (0, 0)))
                return jnp.concatenate([p[:, :, :w], p[:, :, 1:]], axis=3)
            bk, bv = (look_around(bk), look_around(bv))
            bt = jnp.arange(n).reshape(w, WINDOW)
            btp = jnp.pad(bt, ((1, 0), (0, 0)), constant_values=-1)
            btk = jnp.concatenate([btp[:w], btp[1:]], axis=1)
            sim = jnp.einsum('bhwid,bhwjd->bhwij', bq, bk)
            i = bt[:, :, None]
            j = btk[:, None, :]
            mask = (i < j) | (i > j + WINDOW) | (j == -1)
            sim = jnp.where(mask, -jnp.finfo(sim.dtype).max, sim)
            attn = jax.nn.softmax(sim, axis=-1)
            out = jnp.einsum('bhwij,bhwjd->bhwid', attn, bv)
            return out.reshape(b, h, n, d)

        def _layer(x, wqkv, qs, ksc, wo, lg, lb, w1, b1, w2, b2):
            b, n, _ = x.shape
            h = shift_token(x)
            qkv = h @ wqkv
            q, k, v = jnp.split(qkv, 3, axis=-1)
            to_heads = lambda t: t.reshape(b, n, HEADS, DIM_HEAD).transpose(0, 2, 1, 3)
            q, k, v = (to_heads(q), to_heads(k), to_heads(v))
            q = l2norm(q) * qs
            k = l2norm(k) * ksc
            q, k = rotary_xpos(q, k)
            o = local_attention(q, k, v)
            o = o.transpose(0, 2, 1, 3).reshape(b, n, INNER)
            x = x + o @ wo
            h = shift_token(x)
            mu = h.mean(-1, keepdims=True)
            var = h.var(-1, keepdims=True)
            h = (h - mu) / jnp.sqrt(var + 1e-05) * lg + lb
            h = h @ w1 + b1
            a, g = jnp.split(h, 2, axis=-1)
            h = a * jax.nn.gelu(g, approximate=False)
            x = x + h @ w2 + b2
            return x
        for l in range(DEPTH):
            x = _layer(x, wqkv[l], q_scale[l], k_scale[l], wo[l], ln_g[l], ln_b[l], w1[l], b1[l], w2[l], b2[l])
        return x
    x = L0_attn_x
    xn = _layernorm(x, axis=-1)
    s = _L0_attn_ref(xn, L0_attn_w_q, L0_attn_w_k, L0_attn_w_v)
    g = _silu(_L0_ffn_ref(xn, L0_ffn_wqkv, L0_ffn_q_scale, L0_ffn_k_scale, L0_ffn_wo, L0_ffn_ln_g, L0_ffn_ln_b, L0_ffn_w1, L0_ffn_b1, L0_ffn_w2, L0_ffn_b2))
    x = x + s * g
    return x

_drawn_inputs = setup_inputs


def setup_inputs(seed=0):
    import zlib

    import numpy as np

    out = dict(_drawn_inputs(seed))
    spreads = {'L0_ffn_q_scale': (1.0, 0.6),
     'L0_ffn_k_scale': (1.0, 0.6),
     'L0_ffn_ln_g': (1.0, 0.6),
     'L0_ffn_ln_b': (0.0, 0.8),
     'L0_ffn_b1': (0.0, 0.8),
     'L0_ffn_b2': (0.0, 2.0)}
    factors = {'L0_ffn_wqkv': 7.236, 'L0_ffn_wo': 7.031, 'L0_ffn_w1': 8.0, 'L0_ffn_w2': 8.0}
    for name, (base, spread) in spreads.items():
        noise = np.random.default_rng([zlib.crc32(name.encode()), seed]).standard_normal(out[name].shape)
        drawn = base * np.exp(spread * noise) if base else spread * noise
        out[name] = jnp.asarray(drawn.astype(out[name].dtype))
    for name, factor in factors.items():
        out[name] = (out[name] * factor).astype(out[name].dtype)
    return out
```

```python
from contextlib import ExitStack

import numpy as np

import concourse.bass as bass
from concourse import mybir

ALU = mybir.AluOpType
ACT = mybir.ActivationFunctionType
AX = mybir.AxisListType
F32 = mybir.dt.float32
F32R = mybir.dt.float32r
BF16 = mybir.dt.bfloat16

P = 128
B, N, D = 8, 512, 256
TT = N // P
KD = D // P
HEADS, DH = 8, 64
INNER = HEADS * DH
HID = int(D * 4 * 2 / 3)
HFULL = HID // P
HREM = HID - HFULL * P
HT = HFULL + 1
W1T = 2 * HFULL + 1
GATE0 = 64
LAYERS = 2
QK_SCALE = 8.0
EPS = 1e-5
XW = 2 * (N + 4)
X1 = N + 4
NLE = "natural_log_exp_and_others"


def ge(engine, sem, value):
    if not isinstance(value, int) or value > 0:
        engine.wait_ge(sem, value)


def at(ap, i):
    return ap[:, bass.ds(i, 1)]


def x_view(xT, b):
    return xT[:, bass.ds(b, 1), 0:2 * X1].rearrange("p b (k c) -> p (b k) c", k=KD)[:, :, 0:N]


def h_view(xT, b):
    return xT[:, bass.ds(b, 1), 0:2 * (X1 - 1)].rearrange("p b (k c) -> p (b k) c", k=KD)[:, :, 0:N]


def spread(ap, n):
    return ap.unsqueeze(2).broadcast_to([ap.shape[0], ap.shape[1], n, ap.shape[2]])


def along(ap, n):
    return ap.unsqueeze(2).broadcast_to([ap.shape[0], ap.shape[1], n])


def start_at_zero(nc, semaphores):
    with nc.Block() as block:
        @block.sync
        def _(sp):
            for s in semaphores:
                sp.sem_clear(s)


def attention_block(nc, io, xT, ident, identb, epsc):
    ctx = ExitStack()
    with ctx:
        def sb(name, shape, dt=F32):
            return ctx.enter_context(nc.sbuf_tensor(name, shape, dt))

        def pb(name):
            return ctx.enter_context(nc.psum_tensor(name, [P, 512], F32))

        def sem(name):
            return ctx.enter_context(nc.semaphore("a_" + name))

        QKW = 2 * D
        wst = sb("aw_stage", [P, KD, 3 * D])
        whi = sb("aw_hi", [P, KD, 3 * D], F32R)
        wlo = sb("aw_lo", [P, KD, 3 * D], F32R)
        wraw = sb("aw_raw", [P, 3 * KD, D])
        cosT = sb("a_cos", [P, TT, D])
        sinT = sb("a_sin", [P, TT, D])
        maskT = sb("a_mask", [P, N], BF16)
        x_in = sb("a_x", [P, TT, D])
        stats = sb("a_stats", [P, TT, 6])
        mv = sb("a_mv", [P, TT, 2])
        spare = sb("a_spare", [P, 1])
        lnv = sb("a_lnv", [P, TT])
        rstd = sb("a_rstd", [P, TT])
        xn = sb("a_xn", [P, TT, D])
        hhi = sb("a_hhi", [P, KD, N], F32R)
        hlo = sb("a_hlo", [P, KD, N], F32R)
        raw = sb("a_raw", [P, 2, QKW])
        t2 = sb("a_t2", [P, 2, QKW])
        rot = sb("a_rot", [P, TT, QKW])
        V = sb("a_v", [P, TT, D])
        QK = sb("a_qk", [P, 2 * KD, N])
        Pr = sb("a_p", [P, TT, N])
        PT = sb("a_pt", [P, TT, N])
        mx = sb("a_mx", [P, TT])
        nb = sb("a_nb", [P, TT])
        sums = sb("a_sums", [P, TT])
        rinv = sb("a_rinv", [P, TT])
        O = sb("a_o", [P, TT, D])

        ring = [pb("a_ring0"), pb("a_ring1")]
        psT = pb("a_psT")
        psS = [pb("a_psS0"), pb("a_psS1")]
        psP = [pb("a_psP0"), pb("a_psP1")]
        psO = pb("a_psO")

        names = ("w_in c_in w_tr w_ev w_hi w_lo x_in0 bn agg lnv rstd xn xT_ps xT_hi xT_sb xT_lo "
                 "proj_ps proj_sb t2_done t1_done rot_done qkT_ps qkT_sb s_ps m_red m_bias exp_done "
                 "rinv_done pT_ps pT_sb o_ps o_sb out_dma").split()
        S = {n: sem(n) for n in names}
        start_at_zero(nc, S.values())
        block = ctx.enter_context(nc.Block())
        x_v = io["x"].rearrange("b (t p) d -> b p t d", p=P)
        s_v = io["s"].rearrange("b (t p) d -> b p t d", p=P)
        scale = 1.0 / np.sqrt(D)
        TILES = 2 * TT

        def pipeline(e, step):
            step(0, True, False)
            with e.Fori(1, B) as i:
                step(i, True, True)
            step(B, False, True)

        @block.sync
        def _(sp):
            sp.dma_start(x_in[:, :, :], x_v[0]).then_inc(S["x_in0"], 16)
            for j, w in enumerate(("wq", "wk", "wv")):
                sp.dma_start(wraw[:, KD * j:KD * (j + 1), :], io[w].rearrange("(k p) d -> p k d", p=P)).then_inc(S["w_in"], 16)
            sp.dma_start(cosT[:, :, :], io["acos"]).then_inc(S["c_in"], 16)
            sp.dma_start(sinT[:, :, :], io["asin"]).then_inc(S["c_in"], 16)
            sp.dma_start(maskT[:, :], io["amask"]).then_inc(S["c_in"], 16)

            def step(i, front, back):
                if front and not (isinstance(i, int) and i == B - 1):
                    ge(sp, S["xn"], i + 1)
                    sp.dma_start(at(x_in[:, :, :].unsqueeze(1), 0), x_v[bass.ds(i + 1, 1)].rearrange("b p t d -> p b t d")).then_inc(S["x_in0"], 16)
                if back:
                    ge(sp, S["o_sb"], TT * i)
                    sp.dma_start(s_v[bass.ds(i - 1, 1)].rearrange("b p t d -> p b t d"), O[:, :, :].unsqueeze(1)).then_inc(S["out_dma"], 16)
            step(0, True, False)
            with sp.Fori(1, B - 1) as i:
                step(i, True, True)
            step(B - 1, False, True)
            step(B, False, True)
            sp.wait_ge(S["out_dma"], 16 * B)

        @block.gpsimd
        def _(pool):
            pool.wait_ge(S["c_in"], 48)

            def step(i, front, back):
                if front:
                    for t in range(TT):
                        ge(pool, S["proj_sb"], TILES * i + t + 1)
                        ge(pool, S["rot_done"], TT * i + t - 1)
                        src = raw[:, t % 2, :].rearrange("p (q c s) -> p q c s", q=2, s=2)
                        dst = t2[:, t % 2, :].rearrange("p (q c s) -> p q c s", q=2, s=2)
                        tab = sinT[:, t, :].rearrange("p (c s) -> p c s", s=2).unsqueeze(1).broadcast_to([P, 2, D // 2, 2])
                        pool.tensor_tensor(dst[:, :, :, 0], src[:, :, :, 1], tab[:, :, :, 0], ALU.mult).then_inc(S["t2_done"], 1)
                        pool.tensor_tensor(dst[:, :, :, 1], src[:, :, :, 0], tab[:, :, :, 1], ALU.mult).then_inc(S["t2_done"], 1)
            pipeline(pool, step)

        @block.scalar
        def _(act):
            act.preload_act_table_set(NLE)
            for j in range(3 * KD // 2):
                act.wait_ge(S["w_tr"], j + 1)
                act.activation(wst[:, 0:KD, j * D:(j + 1) * D], ring[j % 2][:, :].rearrange("p (k o) -> p k o", k=KD), ACT.Copy).then_inc(S["w_ev"], 1)
            act.wait_ge(S["w_ev"], 3)
            act.activation(whi[:, :, :], wst[:, :, :], ACT.Copy).then_inc(S["w_hi"], 1)

            def proj(i, t):
                n = TILES * i + t
                ge(act, S["proj_ps"], n + 1)
                if t < TT:
                    ge(act, S["rot_done"], TT * i + t - 1)
                    act.activation(raw[:, t % 2, :], ring[t % 2][:, :], ACT.Copy).then_inc(S["proj_sb"], 1)
                else:
                    act.activation(V[:, t - TT, :], ring[t % 2][:, 0:D], ACT.Copy).then_inc(S["proj_sb"], 1)

            def norm(i):
                ge(act, S["agg"], i + 1)
                act.activation(lnv[:, :], mv[:, :, 1], ACT.Ln, bias=epsc[:, 0:1]).then_inc(S["lnv"], 1)
                ge(act, S["lnv"], i + 1)
                act.activation(rstd[:, :], lnv[:, :], ACT.Exp, scale=-0.5).then_inc(S["rstd"], 1)

            def high(i):
                ge(act, S["xT_ps"], i + 1)
                for k in range(KD):
                    act.activation(hhi[:, k, :], ring[k][:, :], ACT.Copy).then_inc(S["xT_hi"], 1)

            def softmax(i, t):
                w = (t + 1) * P
                ge(act, S["m_bias"], TT * (i - 1) + t + 1)
                act.activation(Pr[:, t, 0:w], psS[t % 2][:, 0:w], ACT.Exp, bias=nb[:, t:t + 1], scale=scale,
                               accum_out=sums[:, t:t + 1]).then_inc(S["exp_done"], 1)

            def out(i, t):
                ge(act, S["o_ps"], TT * (i - 1) + t + 1)
                ge(act, S["rinv_done"], TT * (i - 1) + t + 1)
                if t == 0:
                    ge(act, S["out_dma"], 16 * (i - 1))
                act.activation(O[:, t, :], psO[:, 0:D], ACT.Copy, scale=rinv[:, t:t + 1]).then_inc(S["o_sb"], 1)

            def step(i, front, back):
                if front:
                    norm(i)
                if back:
                    softmax(i, 0)
                    softmax(i, 1)
                if front:
                    high(i)
                    proj(i, 0)
                if back:
                    softmax(i, 2)
                    out(i, 0)
                if front:
                    proj(i, 1)
                if back:
                    softmax(i, 3)
                    out(i, 1)
                if front:
                    proj(i, 2)
                if back:
                    out(i, 2)
                if front:
                    proj(i, 3)
                if back:
                    out(i, 3)
                if front:
                    for t in range(TT):
                        ge(act, S["qkT_ps"], TT * i + t + 1)
                        act.activation(QK[:, :, t * P:(t + 1) * P], psT[:, :].rearrange("p (a c) -> p a c", c=P), ACT.Copy).then_inc(S["qkT_sb"], 1)
                    for t in range(TT, 2 * TT):
                        proj(i, t)
            pipeline(act, step)

        @block.vector
        def _(dve):
            dve.wait_ge(S["w_hi"], 1)
            dve.tensor_tensor(wlo[:, :, :], wst[:, :, :], whi[:, :, :].bitcast(F32), ALU.subtract).then_inc(S["w_lo"], 1)
            dve.wait_ge(S["c_in"], 48)

            def norm(i):
                ge(dve, S["x_in0"], 16 * (i + 1))
                for t in range(TT):
                    dve.bn_stats(stats[:, t, :], x_in[:, t, :]).then_inc(S["bn"], 1)
                ge(dve, S["bn"], TT * (i + 1))
                dve.memset(spare[:, :], 0.0)
                for t in range(TT):
                    last = dve.bn_aggr(mv[:, t, :], stats[:, t, :])
                last.then_inc(S["agg"], 1)
                ge(dve, S["rstd"], i + 1)
                for t in range(TT):
                    last = dve.tensor_scalar(xn[:, t, :], x_in[:, t, :], mv[:, t, 0:1], rstd[:, t:t + 1], ALU.subtract, ALU.mult)
                last.then_inc(S["xn"], 1)

            def low(i):
                ge(dve, S["xT_ps"], i + 1)
                ge(dve, S["xT_hi"], KD * (i + 1))
                for k in range(KD):
                    dve.tensor_tensor(hlo[:, k, :], ring[k][:, :], hhi[:, k, :].bitcast(F32), ALU.subtract).then_inc(S["xT_lo"], 1)
                for k in range(KD):
                    last = dve.tensor_copy(xT[:, bass.ds(i, 1), k * X1:k * X1 + N], ring[k][:, :].unsqueeze(1))
                last.then_inc(S["xT_sb"], 1)

            def rotate(i, t):
                ge(dve, S["proj_sb"], TILES * i + t + 1)
                r = rot[:, t, :].rearrange("p (q d) -> p q d", q=2)
                tab = cosT[:, t, :].unsqueeze(1).broadcast_to([P, 2, D])
                dve.tensor_tensor(r, raw[:, t % 2, :].rearrange("p (q d) -> p q d", q=2), tab, ALU.mult).then_inc(S["t1_done"], 1)
                ge(dve, S["t1_done"], TT * i + t + 1)
                ge(dve, S["t2_done"], 2 * (TT * i + t + 1))
                dve.tensor_tensor(rot[:, t, :], rot[:, t, :], t2[:, t % 2, :], ALU.add).then_inc(S["rot_done"], 1)

            def maxima(i, t):
                n = TT * (i - 1) + t + 1
                ge(dve, S["s_ps"], n)
                dve.reduce_max(mx[:, t:t + 1], psS[t % 2][:, 0:(t + 1) * P], AX.X).then_inc(S["m_red"], 1)
                ge(dve, S["m_red"], n)
                dve.tensor_scalar(nb[:, t:t + 1], mx[:, t:t + 1], -scale, None, ALU.mult).then_inc(S["m_bias"], 1)

            def inverse(i, t):
                ge(dve, S["exp_done"], TT * (i - 1) + t + 1)
                dve.reciprocal(rinv[:, t:t + 1], sums[:, t:t + 1]).then_inc(S["rinv_done"], 1)

            def p_copy(i, t):
                w = (t + 1) * P
                ge(dve, S["pT_ps"], TT * (i - 1) + t + 1)
                dve.tensor_copy(PT[:, t, 0:w], psP[t % 2][:, 0:w]).then_inc(S["pT_sb"], 1)

            def step(i, front, back):
                if front:
                    norm(i)
                if back:
                    maxima(i, 0)
                    maxima(i, 1)
                    inverse(i, 0)
                if front:
                    low(i)
                if back:
                    p_copy(i, 0)
                    inverse(i, 1)
                    maxima(i, 2)
                    p_copy(i, 1)
                if front:
                    rotate(i, 0)
                if back:
                    inverse(i, 2)
                    maxima(i, 3)
                    p_copy(i, 2)
                if front:
                    rotate(i, 1)
                if back:
                    inverse(i, 3)
                    p_copy(i, 3)
                if front:
                    rotate(i, 2)
                    rotate(i, 3)
            pipeline(dve, step)

        @block.tensor
        def _(pe):
            pe.wait_ge(S["w_in"], 48)
            for j in range(3):
                if j >= 2:
                    pe.wait_ge(S["w_ev"], j - 1)
                for k in range(KD):
                    for o in range(KD):
                        last = pe.transpose(ring[j % 2][:, k * D + o * P:k * D + (o + 1) * P],
                                            wraw[:, KD * j + o, k * P:(k + 1) * P], ident[:, :])
                last.then_inc(S["w_tr"], 1)
            pe.wait_ge(S["w_ev"], 3)
            pe.wait_ge(S["w_lo"], 1)

            def x_transposes(i):
                ge(pe, S["xn"], i + 1)
                ge(pe, S["proj_sb"], TILES * i)
                for k in range(KD):
                    for t in range(TT):
                        last = pe.transpose(ring[k][:, t * P:(t + 1) * P], xn[:, t, k * P:(k + 1) * P], ident[:, :])
                last.then_inc(S["xT_ps"], 1)

            def project(i, t):
                c0, w = (0, QKW) if t < TT else (QKW, D)
                tok = slice((t % TT) * P, (t % TT + 1) * P)
                if t < 2:
                    ge(pe, S["xT_lo"], KD * (i + 1))
                    ge(pe, S["xT_sb"], i + 1)
                else:
                    ge(pe, S["proj_sb"], TILES * i + t - 1)
                m = 0
                for k in range(KD):
                    for a, w_ in ((hhi, whi), (hhi, wlo), (hlo, whi)):
                        last = pe.matmul(ring[t % 2][:, 0:w], a[:, k, tok], w_[:, k, c0:c0 + w], start=(m == 0), stop=(m == 3 * KD - 1))
                        m += 1
                last.then_inc(S["proj_ps"], 1)

            def qk_transposes(i, t):
                ge(pe, S["rot_done"], TT * i + t + 1)
                ge(pe, S["qkT_sb"], TT * i + t)
                for a in range(2 * KD):
                    last = pe.transpose(psT[:, a * P:(a + 1) * P], rot[:, t, a * P:(a + 1) * P], ident[:, :])
                last.then_inc(S["qkT_ps"], 1)

            def scores(i, t):
                w = (t + 1) * P
                ge(pe, S["qkT_sb"], TT * i)
                if t >= 2:
                    ge(pe, S["exp_done"], TT * (i - 1) + t - 1)
                pe.matmul(psS[t % 2][:, 0:w], identb[:, :], maskT[:, N - w:N], start=True, stop=False)
                for k in range(KD):
                    last = pe.matmul(psS[t % 2][:, 0:w], QK[:, k, t * P:(t + 1) * P], QK[:, KD + k, 0:w], start=False, stop=(k == KD - 1))
                last.then_inc(S["s_ps"], 1)

            def p_transposes(i, t):
                ge(pe, S["exp_done"], TT * (i - 1) + t + 1)
                if t >= 2:
                    ge(pe, S["pT_sb"], TT * (i - 1) + t - 1)
                for k in range(t + 1):
                    last = pe.transpose(psP[t % 2][:, k * P:(k + 1) * P], Pr[:, t, k * P:(k + 1) * P], ident[:, :])
                last.then_inc(S["pT_ps"], 1)

            def values(i, t):
                ge(pe, S["pT_sb"], TT * (i - 1) + t + 1)
                ge(pe, S["proj_sb"], TILES * i)
                ge(pe, S["o_sb"], TT * (i - 1) + t)
                for k in range(t + 1):
                    last = pe.matmul(psO[:, 0:D], PT[:, t, k * P:(k + 1) * P], V[:, k, :], start=(k == 0), stop=(k == t))
                last.then_inc(S["o_ps"], 1)

            def step(i, front, back):
                if back:
                    scores(i, 0)
                    scores(i, 1)
                if front:
                    x_transposes(i)
                if back:
                    p_transposes(i, 0)
                if front:
                    project(i, 0)
                if back:
                    scores(i, 2)
                    p_transposes(i, 1)
                    values(i, 0)
                if front:
                    project(i, 1)
                if back:
                    scores(i, 3)
                    p_transposes(i, 2)
                    values(i, 1)
                if front:
                    project(i, 2)
                if back:
                    p_transposes(i, 3)
                    values(i, 2)
                if front:
                    project(i, 3)
                if back:
                    values(i, 3)
                if front:
                    for t in range(TT):
                        qk_transposes(i, t)
                    for t in range(TT, 2 * TT):
                        project(i, t)
            pipeline(pe, step)


def layer_block(nc, io, layer, xT, ident, identb, ones, epsc):
    ctx = ExitStack()
    with ctx:
        def sb(name, shape, dt=F32):
            return ctx.enter_context(nc.sbuf_tensor(f"l{layer}_{name}", shape, dt))

        def pb(name, n=1):
            return ctx.enter_context(nc.psum_tensor(f"l{layer}_{name}", [P, 512 * n], F32))

        def sem(name):
            return ctx.enter_context(nc.semaphore(f"l{layer}_{name}"))

        QKW = 2 * INNER
        wq_hi = sb("wq_hi", [P, KD, 3 * INNER], F32R)
        wq_lo = sb("wq_lo", [P, KD, 3 * INNER], F32R)
        w1_hi = sb("w1_hi", [P, KD, W1T * P], F32R)
        w1_lo = sb("w1_lo", [P, KD, W1T * P], F32R)
        wo = sb("wo", [P, INNER // P, D])
        w2 = sb("w2", [P, HT, D])
        gcol = sb("g", [P, KD])
        bcol = sb("b", [P, KD])
        b1raw = sb("b1raw", [P, W1T])
        b1col = sb("b1", [P, W1T])
        b2col = sb("b2", [P, KD])
        scl = sb("scl", [P, 2, DH])
        scls = sb("scls", [P, 2, DH])
        cosT = sb("cos", [P, TT, 2, DH])
        sinT = sb("sin", [P, TT, 2, DH])
        maskT = sb("mask", [P, 2 * P], BF16)
        raw = sb("raw", [P, 2, QKW])
        Pr = raw
        sq = sb("sq", [P, QKW])
        t2 = sb("t2", [P, QKW])
        rot = sb("rot", [P, TT, QKW])
        PT = rot
        ssq = sb("ssq", [P, TT, 2 * HEADS])
        lnq = sb("lnq", [P, TT, 2 * HEADS])
        rn = sb("rn", [P, TT, 2 * HEADS])
        sc8 = sb("sc8", [P, TT, HEADS])
        nsc8 = sb("nsc8", [P, TT, HEADS])
        hhi = sb("hhi", [P, KD, N], F32R)
        hlo = sb("hlo", [P, KD, N], F32R)
        dF = sb("dF", [P, KD, N])
        sqF = sb("sqF", [P, KD, N])
        fhi = sb("fhi", [P, KD, N], F32R)
        flo = sb("flo", [P, KD, N], F32R)
        rstdF = sb("rstdF", [P, N])
        G = sb("G", [P, 2, N])
        U = sb("U", [P, HT, N])
        OT = U
        QT = sb("QT", [P, 2, INNER // P, N])
        stage = QT[:, :, :, :].rearrange("p a b c -> p (a b c)")
        KT = sb("KT", [P, INNER // P, N])
        V = sb("V", [P, TT, INNER])
        mx = sb("mx", [P, 2, TT])
        nb = sb("nb", [P, 2, TT])
        sums = sb("sums", [P, 2, TT])
        rinv = sb("rinv", [P, 2, TT])

        ring = [pb("ring0"), pb("ring1")]
        psS = pb("psS", 2)
        psP = pb("psP", 2)
        psF = [pb("psF0"), pb("psF1")]

        names = ("w_in w_in1 h_ready small tabs w1pad w2pad w2_in wq_hi wq_lo w1_hi w1_lo b1_ps b1_sb zeroed "
                 "h_hi h_lo proj_ps proj_sb sq_done ssq_done t1_done t2_done rot_done clamped lnq_done rn_done "
                 "k_scaled sc_done qT_ps qT_sb kT_ps kT_sb s_ps m_red m_bias exp_done rinv_done p_done pT_ps "
                 "pT_sb0 pT_sb1 o_ps o_sb wo_ps x_attn mean_ps d_done sqF_done var_ps lnF_done rstdF_done hn_done "
                 "f_hi f_lo w1_ps gelu_done u_done w2_ps x_ffn").split()
        S = {n: sem(n) for n in names}
        start_at_zero(nc, S.values())
        block = ctx.enter_context(nc.Block())

        def heads_of(ap, n):
            return ap.rearrange("p (h d) -> p h d", h=n)

        def pipeline(e, step):
            step(0, True, False)
            with e.Fori(1, B) as i:
                step(i, True, True)
            step(B, False, True)

        @block.sync
        def _(sp):
            st = stage[:, 0:KD * 3 * INNER].rearrange("p (k n) -> p k n", k=KD)
            sp.dma_start(st, io["wqkv"][layer].rearrange("(k p) n -> p k n", p=P)).then_inc(S["w_in"], 16)
            sp.dma_start(cosT[:, :, :, :], io["fcos"]).then_inc(S["small"], 16)
            sp.dma_start(sinT[:, :, :, :], io["fsin"]).then_inc(S["small"], 16)
            sp.dma_start(maskT[:, :], io["fmask"]).then_inc(S["small"], 16)
            for j, n in enumerate(("q_scale", "k_scale")):
                row = io[n][layer:layer + 1, :]
                sp.dma_start(scl[:, j, :], row.broadcast_to([P, DH])).then_inc(S["small"], 16)
                for s in range(2):
                    sp.dma_start(scls[:, j, s * DH // 2:(s + 1) * DH // 2],
                                 row[:, (1 - s) * DH // 2:(2 - s) * DH // 2].broadcast_to([P, DH // 2])).then_inc(S["small"], 16)
            for dst, n in ((gcol, "ln_g"), (bcol, "ln_b"), (b2col, "b2")):
                sp.dma_start(dst[:, :], io[n][layer].rearrange("(k p) -> p k", p=P), allow_slow_non_contiguous=True).then_inc(S["small"], 16)
            b1 = io["b1"][layer]
            sp.wait_ge(S["w1pad"], 1)
            for s in range(2):
                full = b1[s * HID:s * HID + HFULL * P].rearrange("(j p) -> p j", p=P)
                sp.dma_start(b1raw[:, s * HFULL:(s + 1) * HFULL], full, allow_slow_non_contiguous=True).then_inc(S["small"], 16)
                rest = b1[s * HID + HFULL * P:(s + 1) * HID].rearrange("(p j) -> p j", j=1)
                sp.dma_start(b1raw[s * GATE0:s * GATE0 + HREM, 2 * HFULL:W1T], rest, allow_slow_non_contiguous=True).then_inc(S["small"], 16)
            sp.dma_start(wo[:, :, :], io["wo"][layer].rearrange("(k p) n -> p k n", p=P)).then_inc(S["w2_in"], 16)
            sp.wait_ge(S["w2pad"], 1)
            sp.dma_start(w2[:, 0:HFULL, :], io["w2"][layer, 0:HFULL * P].rearrange("(k p) n -> p k n", p=P)).then_inc(S["w2_in"], 16)
            sp.dma_start(w2[0:HREM, HFULL, :], io["w2"][layer, HFULL * P:HID]).then_inc(S["w2_in"], 16)
            sp.wait_ge(S["w1pad"], 2)
            st1 = stage[:, 0:KD * W1T * P].rearrange("p (k n) -> p k n", k=KD)
            w1 = io["w1"][layer].rearrange("(k p) n -> p k n", p=P)
            for s in range(2):
                sp.dma_start(st1[:, :, s * HFULL * P:(s + 1) * HFULL * P], w1[:, :, s * HID:s * HID + HFULL * P]).then_inc(S["w_in1"], 16)
                c = 2 * HFULL * P + s * GATE0
                sp.dma_start(st1[:, :, c:c + HREM], w1[:, :, s * HID + HFULL * P:(s + 1) * HID]).then_inc(S["w_in1"], 16)
            sp.wait_ge(S["w_in1"], 64)

        SMALL = 16 * (3 + 2 * 3 + 3 + 4)

        @block.gpsimd
        def _(pool):
            pool.wait_ge(S["tabs"], 2)

            def rotate(i, t):
                ge(pool, S["proj_sb"], 3 * (TT * i + t) + 2)
                ge(pool, S["rot_done"], TT * i + t)
                for j in range(2):
                    src = raw[:, t % 2, j * INNER:(j + 1) * INNER].rearrange("p (h s d) -> p h s d", h=HEADS, s=2)
                    dst = t2[:, j * INNER:(j + 1) * INNER].rearrange("p (h s d) -> p h s d", h=HEADS, s=2)
                    tab = sinT[:, t, j, :].rearrange("p (s d) -> p s d", s=2)
                    for s in range(2):
                        pool.tensor_tensor(dst[:, :, s, :], src[:, :, 1 - s, :],
                                           tab[:, s, :].unsqueeze(1).broadcast_to([P, HEADS, DH // 2]), ALU.mult).then_inc(S["t2_done"], 1)

            def step(i, attn, ffn):
                if attn:
                    for t in range(TT):
                        rotate(i, t)
                    for h in range(HEADS):
                        ge(pool, S["rinv_done"], HEADS * i + h + 1)
                        pr = Pr[:, h % 2, :].rearrange("p (t c) -> p t c", t=TT)
                        pool.tensor_tensor(pr[:, 0, P:2 * P], pr[:, 0, P:2 * P], rinv[:, h % 2, 0:1].broadcast_to([P, P]), ALU.mult)
                        pool.tensor_tensor(pr[:, 1:TT, :], pr[:, 1:TT, :], along(rinv[:, h % 2, 1:TT], 2 * P), ALU.mult).then_inc(S["p_done"], 1)
            pipeline(pool, step)

        @block.scalar
        def _(act):
            act.preload_act_table_set(NLE)
            act.wait_ge(S["w_in"], 16)
            st = stage[:, 0:KD * 3 * INNER].rearrange("p (k n) -> p k n", k=KD)
            act.activation(wq_hi[:, :, :], st, ACT.Copy).then_inc(S["wq_hi"], 1)
            act.wait_ge(S["w_in1"], 64)
            act.wait_ge(S["small"], SMALL)
            st1 = stage[:, 0:KD * W1T * P].rearrange("p (k n) -> p k n", k=KD)
            for k in range(KD):
                act.activation(w1_hi[:, k, :], st1[:, k, :], ACT.Copy, scale=gcol[:, k:k + 1]).then_inc(S["w1_hi"], 1)

            def copies(i, t):
                for c in range(3):
                    n = 3 * (TT * i + t) + c
                    ge(act, S["proj_ps"], n + 1)
                    if c == 0 and t >= 2:
                        ge(act, S["rot_done"], TT * i + t - 1)
                    dst = raw[:, t % 2, c * INNER:(c + 1) * INNER] if c < 2 else V[:, t, :]
                    act.activation(dst, ring[(t + c) % 2][:, :], ACT.Copy).then_inc(S["proj_sb"], 1)
                    if c == 1:
                        ge(act, S["proj_sb"], n + 1)
                        ge(act, S["ssq_done"], TT * i + t)
                        act.activation(sq[:, :], raw[:, t % 2, :], ACT.Square).then_inc(S["sq_done"], 1)

            def q_evac(i, t):
                ge(act, S["qT_ps"], TT * i + t + 1)
                for par in range(2):
                    rows = slice(par * DH, (par + 1) * DH)
                    last = act.activation(QT[rows, par, :, t * P:(t + 1) * P], psS[rows, 0:512].rearrange("p (a c) -> p a c", c=P), ACT.Copy)
                last.then_inc(S["qT_sb"], 1)

            def gelu(i, j):
                u = i - 1
                ge(act, S["w1_ps"], HT * u + j + 1)
                if j >= 2:
                    ge(act, S["u_done"], HT * u + j - 1)
                if j < HFULL:
                    act.activation(G[:, j % 2, :], psF[0][:, :], ACT.Gelu, bias=b1col[:, HFULL + j:HFULL + j + 1]).then_inc(S["gelu_done"], 1)
                else:
                    act.activation(G[0:HREM, j % 2, :], psF[0][GATE0:GATE0 + HREM, :], ACT.Gelu,
                                   bias=b1col[GATE0:GATE0 + HREM, 2 * HFULL:W1T]).then_inc(S["gelu_done"], 1)

            def p_evac(i, h):
                ge(act, S["pT_ps"], HEADS * i + h + 1)
                act.activation(PT[:, h % 2, 0:512], psP[:, 0:512], ACT.Copy).then_inc(S["pT_sb0"], 1)

            def softmax(i, h):
                ge(act, S["m_bias"], HEADS * i + h + 1)
                ge(act, S["pT_ps"], HEADS * i + h - 1)
                for t in range(TT):
                    c0 = P if t == 0 else 0
                    last = act.activation(Pr[:, h % 2, t * 2 * P + c0:(t + 1) * 2 * P], psS[:, t * 2 * P + c0:(t + 1) * 2 * P], ACT.Exp,
                                          bias=nb[:, h % 2, t:t + 1], scale=sc8[:, t, h:h + 1], accum_out=sums[:, h % 2, t:t + 1])
                last.then_inc(S["exp_done"], 1)

            def step(i, attn, ffn):
                if attn:
                    act.activation(hhi[:, :, :], h_view(xT, i), ACT.Copy).then_inc(S["h_hi"], 1)
                    copies(i, 0)
                if ffn:
                    ge(act, S["d_done"], i)
                    act.activation(sqF[:, :, :], dF[:, :, :], ACT.Square).then_inc(S["sqF_done"], 1)
                if attn:
                    copies(i, 1)
                if ffn:
                    ge(act, S["var_ps"], i)
                    act.activation(rstdF[:, :], psF[1][:, :], ACT.Ln, bias=epsc[:, 0:1]).then_inc(S["lnF_done"], 1)
                    ge(act, S["lnF_done"], i)
                    act.activation(rstdF[:, :], rstdF[:, :], ACT.Exp, scale=-0.5).then_inc(S["rstdF_done"], 1)
                if attn:
                    copies(i, 2)
                if ffn:
                    ge(act, S["hn_done"], i)
                    act.activation(fhi[:, :, :], dF[:, :, :], ACT.Copy).then_inc(S["f_hi"], 1)
                if attn:
                    copies(i, 3)
                    ge(act, S["clamped"], i + 1)
                    act.activation(lnq[:, :, :], ssq[:, :, :], ACT.Ln).then_inc(S["lnq_done"], 1)
                    ge(act, S["lnq_done"], i + 1)
                    act.activation(rn[:, :, :], lnq[:, :, :], ACT.Exp, scale=-0.5).then_inc(S["rn_done"], 1)
                if ffn:
                    gelu(i, 0)
                    gelu(i, 1)
                if attn:
                    for t in range(TT):
                        q_evac(i, t)
                if ffn:
                    for j in range(2, HT):
                        gelu(i, j)
                if attn:
                    act.preload_act_table_set(NLE)
                    for h in range(HEADS + 2):
                        if 1 <= h <= HEADS:
                            p_evac(i, h - 1)
                        if h < HEADS:
                            softmax(i, h)
                        if h >= 2 and h % 2:
                            pair = (h - 2) // 2
                            ge(act, S["o_ps"], HEADS // 2 * i + pair + 1)
                            act.activation(OT[:, pair, :], ring[pair % 2][:, :], ACT.Copy).then_inc(S["o_sb"], 1)
            pipeline(act, step)

        @block.vector
        def _(dve):
            dve.memset(b1raw[:, :], 0.0).then_inc(S["w1pad"], 1)
            dve.memset(w2[:, HFULL, :], 0.0).then_inc(S["w2pad"], 1)
            dve.memset(U[:, HFULL, :], 0.0)
            dve.wait_ge(S["small"], SMALL)
            for c, (tab, s) in enumerate(((cosT, scl), (sinT, scls))):
                dve.tensor_tensor(tab[:, :, :, :].rearrange("p t j d -> p t (j d)"), tab[:, :, :, :].rearrange("p t j d -> p t (j d)"),
                                  s[:, :, :].rearrange("p j d -> p (j d)").unsqueeze(1).broadcast_to([P, TT, 2 * DH]), ALU.mult).then_inc(S["tabs"], 1)
            dve.wait_ge(S["wq_hi"], 1)
            st = stage[:, 0:KD * 3 * INNER].rearrange("p (k n) -> p k n", k=KD)
            dve.tensor_tensor(wq_lo[:, :, :], st, wq_hi[:, :, :].bitcast(F32), ALU.subtract).then_inc(S["wq_lo"], 1)
            dve.wait_ge(S["wq_lo"], 1)
            st1 = stage[:, 0:KD * W1T * P].rearrange("p (k n) -> p k n", k=KD)
            dve.memset(st1[:, :, 2 * HFULL * P:], 0.0).then_inc(S["w1pad"], 1)
            dve.wait_ge(S["w1_hi"], KD)
            for k in range(KD):
                last = dve.scalar_tensor_tensor(out=w1_lo[:, k, :], in0=st1[:, k, :], scalar=gcol[:, k:k + 1],
                                                in1=w1_hi[:, k, :].bitcast(F32), op0=ALU.mult, op1=ALU.subtract)
            last.then_inc(S["w1_lo"], 1)
            dve.wait_ge(S["b1_ps"], 1)
            dve.tensor_tensor(b1col[:, :], psF[0][:, 0:W1T], b1raw[:, :], ALU.add).then_inc(S["b1_sb"], 1)
            dve.wait_ge(S["w1_lo"], 1)
            dve.memset(QT[DH:P, 0, :, :], 0.0)
            dve.memset(QT[0:DH, 1, :, :], 0.0).then_inc(S["zeroed"], 1)
            dve.wait_ge(S["tabs"], 2)
            dve.wait_ge(S["b1_sb"], 1)

            def rotate(i, t):
                n = TT * i + t
                ge(dve, S["sq_done"], n + 1)
                dve.tensor_reduce(ssq[:, t, :], sq[:, :].rearrange("p (h d) -> p h d", d=DH), AX.X, ALU.add).then_inc(S["ssq_done"], 1)
                for j in range(2):
                    last = dve.tensor_tensor(heads_of(rot[:, t, j * INNER:(j + 1) * INNER], HEADS),
                                             heads_of(raw[:, t % 2, j * INNER:(j + 1) * INNER], HEADS),
                                             cosT[:, t, j, :].unsqueeze(1).broadcast_to([P, HEADS, DH]), ALU.mult)
                last.then_inc(S["t1_done"], 1)
                ge(dve, S["t1_done"], n + 1)
                ge(dve, S["t2_done"], 4 * (n + 1))
                dve.tensor_tensor(rot[:, t, :], rot[:, t, :], t2[:, :], ALU.add).then_inc(S["rot_done"], 1)

            def gated(i, j):
                u = i - 1
                ge(dve, S["gelu_done"], HT * u + j + 1)
                if j < HFULL:
                    dve.scalar_tensor_tensor(out=U[:, j, :], in0=psF[1][:, :], scalar=b1col[:, j:j + 1], in1=G[:, j % 2, :],
                                             op0=ALU.add, op1=ALU.mult).then_inc(S["u_done"], 1)
                else:
                    dve.scalar_tensor_tensor(out=U[0:HREM, j, :], in0=psF[0][0:HREM, :], scalar=b1col[0:HREM, 2 * HFULL:W1T],
                                             in1=G[0:HREM, j % 2, :], op0=ALU.add, op1=ALU.mult).then_inc(S["u_done"], 1)

            def step(i, attn, ffn):
                if attn:
                    ge(dve, S["h_hi"], i + 1)
                    dve.tensor_tensor(hlo[:, :, :], h_view(xT, i), hhi[:, :, :].bitcast(F32), ALU.subtract).then_inc(S["h_lo"], 1)
                    rotate(i, 0)
                if ffn:
                    ge(dve, S["mean_ps"], i)
                    for k in range(KD):
                        last = dve.tensor_tensor(dF[:, k, :], dF[:, k, :], psF[0][:, :], ALU.subtract)
                    last.then_inc(S["d_done"], 1)
                if attn:
                    rotate(i, 1)
                if ffn:
                    ge(dve, S["rstdF_done"], i)
                    for k in range(KD):
                        last = dve.tensor_tensor(dF[:, k, :], dF[:, k, :], rstdF[:, :], ALU.mult)
                    last.then_inc(S["hn_done"], 1)
                if attn:
                    rotate(i, 2)
                if ffn:
                    ge(dve, S["f_hi"], i)
                    dve.tensor_tensor(flo[:, :, :], dF[:, :, :], fhi[:, :, :].bitcast(F32), ALU.subtract).then_inc(S["f_lo"], 1)
                if attn:
                    rotate(i, 3)
                    ge(dve, S["ssq_done"], TT * (i + 1))
                    dve.tensor_scalar(ssq[:, :, :], ssq[:, :, :], 1e-24, None, ALU.max).then_inc(S["clamped"], 1)
                    ge(dve, S["rn_done"], i + 1)
                    dve.tensor_scalar(sc8[:, :, :], rn[:, :, 0:HEADS], QK_SCALE, None, ALU.mult)
                    dve.tensor_scalar(nsc8[:, :, :], rn[:, :, 0:HEADS], -QK_SCALE, None, ALU.mult).then_inc(S["sc_done"], 1)
                    ge(dve, S["rot_done"], TT * (i + 1))
                    for t in range(TT):
                        kr = heads_of(rot[:, t, INNER:QKW], HEADS)
                        dve.tensor_tensor(kr, kr, along(rn[:, t, HEADS:2 * HEADS], DH), ALU.mult).then_inc(S["k_scaled"], 1)
                if ffn:
                    for j in range(4):
                        gated(i, j)
                if attn:
                    for t in range(TT):
                        ge(dve, S["kT_ps"], TT * i + t + 1)
                        dve.tensor_copy(KT[:, :, t * P:(t + 1) * P], psS[:, 512:1024].rearrange("p (a c) -> p a c", c=P)).then_inc(S["kT_sb"], 1)
                if ffn:
                    for j in range(4, HT):
                        gated(i, j)
                    ge(dve, S["w2_ps"], i)
                    for k in range(KD):
                        xk = xT[:, bass.ds(i - 1, 1), k * X1:k * X1 + N]
                        last = dve.scalar_tensor_tensor(out=xk, in0=psF[k][:, :].unsqueeze(1), scalar=b2col[:, k:k + 1], in1=xk,
                                                        op0=ALU.add, op1=ALU.add)
                    last.then_inc(S["x_ffn"], 1)
                if attn:
                    ge(dve, S["sc_done"], i + 1)
                    for h in range(HEADS + 1):
                        if h < HEADS:
                            n = HEADS * i + h + 1
                            ge(dve, S["s_ps"], n)
                            dve.reduce_max(mx[:, h % 2, 0:1], psS[:, P:2 * P], AX.X)
                            dve.reduce_max(mx[:, h % 2, 1:TT], psS[:, 2 * P:].rearrange("p (t c) -> p t c", c=2 * P), AX.X).then_inc(S["m_red"], 1)
                            ge(dve, S["m_red"], n)
                            dve.tensor_tensor(nb[:, h % 2, :], mx[:, h % 2, :], nsc8[:, :, h], ALU.mult).then_inc(S["m_bias"], 1)
                        if h >= 1:
                            ge(dve, S["pT_ps"], HEADS * i + h)
                            dve.tensor_copy(PT[:, (h - 1) % 2, 512:896], psP[:, 512:896]).then_inc(S["pT_sb1"], 1)
                        if h < HEADS:
                            ge(dve, S["exp_done"], HEADS * i + h + 1)
                            dve.reciprocal(rinv[:, h % 2, :], sums[:, h % 2, :]).then_inc(S["rinv_done"], 1)
                    ge(dve, S["wo_ps"], i + 1)
                    for k in range(KD):
                        xk = xT[:, bass.ds(i, 1), k * X1:k * X1 + N]
                        dve.tensor_tensor(xk, xk, ring[k][:, :].unsqueeze(1), ALU.add).then_inc(S["x_attn"], 1)
                    ge(dve, S["x_attn"], KD * (i + 1))
                    dve.tensor_scalar(dF[:, :, :], h_view(xT, i), 1.0, None, ALU.mult).then_inc(S["h_ready"], 1)
            pipeline(dve, step)

        @block.tensor
        def _(pe):
            pe.wait_ge(S["w_in1"], 64)
            pe.wait_ge(S["small"], SMALL)
            st1 = stage[:, 0:KD * W1T * P].rearrange("p (k n) -> p k n", k=KD)
            for j in range(W1T):
                for k in range(KD):
                    last = pe.matmul(psF[0][:, j:j + 1], st1[:, k, j * P:(j + 1) * P], bcol[:, k:k + 1], start=(k == 0), stop=(k == KD - 1))
            last.then_inc(S["b1_ps"], 1)
            pe.wait_ge(S["wq_lo"], 1)
            pe.wait_ge(S["b1_sb"], 1)
            pe.wait_ge(S["w2_in"], 48)
            pe.wait_ge(S["zeroed"], 1)

            def project(i, t):
                for c in range(3):
                    n = 3 * (TT * i + t) + c
                    if t == 0 and c == 0:
                        ge(pe, S["h_lo"], i + 1)
                        ge(pe, S["x_attn"], KD * i)
                    elif t or c > 1:
                        ge(pe, S["proj_sb"], n - 1)
                    m = 0
                    for k in range(KD):
                        for a, w in ((hhi, wq_hi), (hhi, wq_lo), (hlo, wq_hi)):
                            last = pe.matmul(ring[(t + c) % 2][:, :], a[:, k, t * P:(t + 1) * P], w[:, k, c * INNER:(c + 1) * INNER],
                                             start=(m == 0), stop=(m == 3 * KD - 1))
                            m += 1
                    last.then_inc(S["proj_ps"], 1)

            def mean(i):
                ge(pe, S["h_ready"], i)
                ge(pe, S["x_ffn"], i - 1)
                for k in range(KD):
                    last = pe.matmul(psF[0][:, :], ones[:, :], dF[:, k, :], start=(k == 0), stop=(k == KD - 1))
                last.then_inc(S["mean_ps"], 1)

            def variance(i):
                ge(pe, S["sqF_done"], i)
                for k in range(KD):
                    last = pe.matmul(psF[1][:, :], ones[:, :], sqF[:, k, :], start=(k == 0), stop=(k == KD - 1))
                last.then_inc(S["var_ps"], 1)

            def hidden(i, j):
                u = i - 1
                ge(pe, S["f_lo"], i)
                ge(pe, S["gelu_done"], HT * u + j)
                ge(pe, S["u_done"], HT * u + j)
                tiles = ((HFULL + j, 0), (j, 1)) if j < HFULL else ((2 * HFULL, 0),)
                for tile, bank in tiles:
                    m = 0
                    for k in range(KD):
                        for w, a in ((w1_hi, fhi), (w1_lo, fhi), (w1_hi, flo)):
                            last = pe.matmul(psF[bank][:, :], w[:, k, tile * P:(tile + 1) * P], a[:, k, :], start=(m == 0), stop=(m == 3 * KD - 1))
                            m += 1
                last.then_inc(S["w1_ps"], 1)

            def down(i):
                ge(pe, S["u_done"], HT * i)
                for c in range(KD):
                    for k in range(HT):
                        last = pe.matmul(psF[c][:, :], w2[:, k, c * P:(c + 1) * P], U[:, k, :], start=(k == 0), stop=(k == HT - 1))
                last.then_inc(S["w2_ps"], 1)

            def transposes(i, t, j):
                n = TT * i + t
                if j == 0:
                    ge(pe, S["rot_done"], n + 1)
                    ge(pe, S["qT_sb"], n)
                else:
                    ge(pe, S["k_scaled"], n + 1)
                    ge(pe, S["kT_sb"], n)
                for a in range(INNER // P):
                    last = pe.transpose(psS[:, j * 512 + a * P:j * 512 + (a + 1) * P], rot[:, t, j * INNER + a * P:j * INNER + (a + 1) * P], ident[:, :])
                last.then_inc(S["kT_ps" if j else "qT_ps"], 1)

            def scores(i, h):
                if h == 0:
                    ge(pe, S["qT_sb"], TT * (i + 1))
                    ge(pe, S["kT_sb"], TT * (i + 1))
                ge(pe, S["exp_done"], HEADS * i + h)
                for t in range(TT):
                    c0 = P if t == 0 else 0
                    out = psS[:, t * 2 * P + c0:(t + 1) * 2 * P]
                    pe.matmul(out, identb[:, :], maskT[:, c0:2 * P], start=True, stop=False)
                    last = pe.matmul(out, QT[:, h % 2, h // 2, t * P:(t + 1) * P], KT[:, h // 2, max(t - 1, 0) * P:(t + 1) * P], start=False, stop=True)
                last.then_inc(S["s_ps"], 1)

            def p_transposes(i, h):
                ge(pe, S["p_done"], HEADS * i + h + 1)
                ge(pe, S["pT_sb0"], HEADS * i + h)
                ge(pe, S["pT_sb1"], HEADS * i + h)
                for t in range(TT):
                    last = pe.transpose(psP[:, t * 2 * P:t * 2 * P + P], Pr[:, h % 2, t * 2 * P + P:(t + 1) * 2 * P], ident[:, :])
                    if t:
                        last = pe.transpose(psP[:, (t - 1) * 2 * P + P:t * 2 * P], Pr[:, h % 2, t * 2 * P:t * 2 * P + P], ident[:, :])
                last.then_inc(S["pT_ps"], 1)

            def values(i, h):
                pair, rows = h // 2, slice(h % 2 * DH, (h % 2 + 1) * DH)
                ge(pe, S["pT_sb0"], HEADS * i + h + 1)
                ge(pe, S["pT_sb1"], HEADS * i + h + 1)
                if h == 0:
                    ge(pe, S["proj_sb"], 3 * TT * (i + 1))
                if h % 2 == 0:
                    ge(pe, S["o_sb"], HEADS // 2 * i + pair - 1)
                for t in range(TT):
                    w = 2 * P if t < TT - 1 else P
                    last = pe.matmul(ring[pair % 2][rows, t * P:t * P + w], V[:, t, h * DH:(h + 1) * DH], PT[:, h % 2, t * 2 * P:t * 2 * P + w],
                                     start=(t == 0), stop=(t == TT - 1), skip_group_check=True)
                if h % 2:
                    last.then_inc(S["o_ps"], 1)

            def output(i):
                ge(pe, S["o_sb"], HEADS // 2 * (i + 1))
                for c in range(KD):
                    for a in range(INNER // P):
                        last = pe.matmul(ring[c][:, :], wo[:, a, c * P:(c + 1) * P], OT[:, a, :], start=(a == 0), stop=(a == INNER // P - 1))
                last.then_inc(S["wo_ps"], 1)

            def step(i, attn, ffn):
                if attn:
                    project(i, 0)
                if ffn:
                    mean(i)
                if attn:
                    project(i, 1)
                if ffn:
                    variance(i)
                if attn:
                    project(i, 2)
                    project(i, 3)
                if ffn:
                    hidden(i, 0)
                    hidden(i, 1)
                if attn:
                    for t in range(TT):
                        transposes(i, t, 0)
                if ffn:
                    hidden(i, 2)
                    hidden(i, 3)
                if attn:
                    for t in range(TT):
                        transposes(i, t, 1)
                if ffn:
                    hidden(i, 4)
                    hidden(i, 5)
                    down(i)
                if attn:
                    for h in range(HEADS + 2):
                        if h < HEADS:
                            scores(i, h)
                        if 1 <= h <= HEADS:
                            p_transposes(i, h - 1)
                        if h >= 2:
                            values(i, h - 2)
                    output(i)
            pe.wait_ge(S["w1_lo"], 1)
            pipeline(pe, step)


def combine_block(nc, io, xT, ident):
    ctx = ExitStack()
    with ctx:
        def sb(name, shape, dt=F32):
            return ctx.enter_context(nc.sbuf_tensor("c_" + name, shape, dt))

        x_in = sb("x", [P, 2, TT, D])
        s_in = sb("s", [P, 2, TT, D])
        E = sb("e", [P, 2, TT, D])
        O = sb("o", [P, 2, TT, D])
        yT = sb("yT", [P, 2, KD, N])
        ps = [ctx.enter_context(nc.psum_tensor(f"c_ps{j}", [P, TT, D], F32)) for j in range(2)]
        names = "yT x_in0 x_in1 tr silu prod sum out0 out1".split()
        S = {n: ctx.enter_context(nc.semaphore("c_" + n)) for n in names}
        start_at_zero(nc, S.values())
        block = ctx.enter_context(nc.Block())
        x_v = io["x"].rearrange("b (t p) d -> b p t d", p=P)
        s_v = io["s"].rearrange("b (t p) d -> b p t d", p=P)
        o_v = io["out"].rearrange("b (t p) d -> b p t d", p=P)

        def pairs(e, body):
            for par in range(2):
                body(0, par)
            with e.Fori(1, B // 2) as i:
                for par in range(2):
                    body(i, par)

        @block.sync
        def _(sp):
            def load(i, par):
                b = 2 * i + par
                ge(sp, S["sum"], b - 1)
                for dst, src in ((x_in, x_v), (s_in, s_v)):
                    sp.dma_start(at(dst, par), src[bass.ds(b, 1)].rearrange("b p t d -> p b t d")).then_inc(S[f"x_in{par}"], 16)
            pairs(sp, load)

        @block.gpsimd
        def _(pool):
            def body(i, par):
                b = 2 * i + par
                ge(pool, S["silu"], b + 1)
                ge(pool, S[f"x_in{par}"], 32 * (i + 1))
                pool.tensor_tensor(E[:, par], E[:, par], s_in[:, par], ALU.mult).then_inc(S["prod"], 1)
            pairs(pool, body)

        @block.scalar
        def _(act):
            def store(i, par):
                b = 2 * i + par
                ge(act, S["sum"], b + 1)
                act.dma_start(o_v[bass.ds(b, 1)].rearrange("b p t d -> p b t d"), at(O, par)).then_inc(S[f"out{par}"], 16)

            def silu(i, par):
                b = 2 * i + par
                ge(act, S["tr"], b + 1)
                ge(act, S["sum"], b - 1)
                act.activation(E[:, par], ps[par][:, :, :], ACT.Silu).then_inc(S["silu"], 1)

            for par in range(2):
                silu(0, par)
            with act.Fori(1, B // 2) as i:
                for par in range(2):
                    store(i - 1, par)
                    silu(i, par)
            for par in range(2):
                store(B // 2 - 1, par)
            act.wait_ge(S["out0"], 16 * (B // 2))
            act.wait_ge(S["out1"], 16 * (B // 2))

        @block.vector
        def _(dve):
            def copy(i, par):
                b = 2 * i + par
                ge(dve, S["tr"], b - 1)
                dve.tensor_scalar(yT[:, par], x_view(xT, b), 1.0, None, ALU.mult).then_inc(S["yT"], 1)

            def add_x(i, par):
                b = 2 * i + par
                ge(dve, S["prod"], b + 1)
                ge(dve, S[f"out{par}"], 16 * i)
                dve.tensor_tensor(O[:, par], E[:, par], x_in[:, par], ALU.add).then_inc(S["sum"], 1)

            copy(0, 0)
            copy(0, 1)
            add_x(0, 0)
            add_x(0, 1)
            with dve.Fori(1, B // 2) as i:
                copy(i, 0)
                copy(i, 1)
                add_x(i, 0)
                add_x(i, 1)

        @block.tensor
        def _(pe):
            def body(i, par):
                b = 2 * i + par
                ge(pe, S["yT"], b + 1)
                ge(pe, S["silu"], b - 1)
                for t in range(TT):
                    for k in range(KD):
                        last = pe.transpose(ps[par][:, t, k * P:(k + 1) * P], yT[:, par, k, t * P:(t + 1) * P], ident[:, :])
                last.then_inc(S["tr"], 1)
            pairs(pe, body)


def build(nc, io):
    with ExitStack() as ctx:
        xT = ctx.enter_context(nc.sbuf_tensor("xT", [P, B, XW], F32))
        ident = ctx.enter_context(nc.sbuf_tensor("ident", [P, P], F32))
        identb = ctx.enter_context(nc.sbuf_tensor("identb", [P, P], BF16))
        ones = ctx.enter_context(nc.sbuf_tensor("ones", [P, P], F32))
        epsc = ctx.enter_context(nc.sbuf_tensor("eps", [P, 1], F32))
        id_in = ctx.enter_context(nc.semaphore("id_in"))
        id_bf = ctx.enter_context(nc.semaphore("id_bf"))
        with nc.Block() as block:
            @block.sync
            def _(sp):
                sp.dma_start(ident[:, :], io["ident"]).then_inc(id_in, 16)
                sp.wait_ge(id_in, 16)

            @block.vector
            def _(dve):
                dve.memset(ones[:, :], 1.0 / D)
                dve.memset(epsc[:, :], EPS)
                dve.memset(xT[:, :, X1 - 1], 0.0)
                dve.wait_ge(id_in, 16)
                dve.tensor_copy(identb[:, :], ident[:, :]).then_inc(id_bf, 1)
                dve.wait_ge(id_bf, 1)
        attention_block(nc, io, xT, ident, identb, epsc)
        for layer in range(LAYERS):
            layer_block(nc, io, layer, xT, ident, identb, ones, epsc)
        combine_block(nc, io, xT, ident)


def shape_constants():
    f = np.float32
    i = np.arange(D // 2, dtype=f)
    theta = np.power(f(10000.0), f(-2.0) * (i - f(1.0)) / f(D)).astype(f)
    pos = np.arange(N, dtype=f)
    ang = pos[:, None] * theta[None, :]
    c, s = np.cos(ang).astype(f), np.sin(ang).astype(f)
    acos = np.repeat(c, 2, axis=1)
    asin = np.stack((s, -s), axis=-1).reshape(N, D)
    half = np.arange(0, DH, 2, dtype=f)
    inv = (f(1.0) / np.power(f(10000.0), half / f(DH))).astype(f)
    fr = pos[:, None] * inv[None, :]
    fr = np.concatenate([fr, fr], axis=-1)
    base = (half + f(0.4 * DH)) / f(1.4 * DH)
    power = (pos - f(N // 2)) / f(P // 2)
    xs = np.power(base[None, :], power[:, None]).astype(f)
    xs = np.concatenate([xs, xs], axis=-1)
    c, s = np.cos(fr).astype(f), np.sin(fr).astype(f)
    sign = np.concatenate([-np.ones(DH // 2, f), np.ones(DH // 2, f)])
    fcos = np.stack([c * xs, c / xs], axis=1)
    fsin = np.stack([s * xs * sign, s / xs * sign], axis=1)

    def rows(a):
        return np.ascontiguousarray(a.reshape(TT, P, *a.shape[1:]).swapaxes(0, 1).astype(f))
    q, k = np.arange(P)[:, None], np.arange(P)[None, :]
    own = np.where(k <= q, f(0), f(-3e38))
    prev = np.where(k >= q, f(0), f(-3e38))
    amask = np.concatenate([np.zeros((P, N - P), f), own], axis=1)
    fmask = np.concatenate([prev, own], axis=1)
    return dict(acos=rows(acos), asin=rows(asin), fcos=rows(fcos), fsin=rows(fsin), amask=amask, fmask=fmask, ident=np.eye(P, dtype=f))


NAMES = dict(x="L0_attn_x", wq="L0_attn_w_q", wk="L0_attn_w_k", wv="L0_attn_w_v", wqkv="L0_ffn_wqkv", q_scale="L0_ffn_q_scale",
             k_scale="L0_ffn_k_scale", wo="L0_ffn_wo", ln_g="L0_ffn_ln_g", ln_b="L0_ffn_ln_b", w1="L0_ffn_w1", b1="L0_ffn_b1",
             w2="L0_ffn_w2", b2="L0_ffn_b2")


def kernel(**inputs):
    import ml_dtypes
    import concourse.bacc as _bacc
    from concourse.bass_utils import run_bass_kernel_spmd as _run

    nc = _bacc.Bacc("TRN2", target_bir_lowering=False, num_devices=1)
    arrays, io = {}, {}
    for short, name in NAMES.items():
        arrays[f"in_{short}"] = np.ascontiguousarray(inputs[name])
    for short, a in shape_constants().items():
        arrays[f"in_{short}"] = a.astype(ml_dtypes.bfloat16) if short.endswith("mask") else a
    for key, a in arrays.items():
        io[key[3:]] = nc.dram_tensor(key, a.shape, mybir.dt.from_np(a.dtype), kind="ExternalInput").ap()
    io["s"] = nc.dram_tensor("scratch_s", (B, N, D), F32, kind="Internal").ap()
    io["out"] = nc.dram_tensor("out_dram", (B, N, D), F32, kind="ExternalOutput").ap()
    build(nc, io)
    r = _run(nc, [arrays], core_ids=[0])
    return r.results[0]["out_dram"]
```

```python
from contextlib import ExitStack

import numpy as np

import concourse.bass as bass
from concourse import mybir

ALU = mybir.AluOpType
ACT = mybir.ActivationFunctionType
AX = mybir.AxisListType
F32 = mybir.dt.float32
F32R = mybir.dt.float32r
BF16 = mybir.dt.bfloat16

P = 128
B, N, D = 8, 512, 256
TT = N // P
KD = D // P
HEADS, DH = 8, 64
INNER = HEADS * DH
HID = int(D * 4 * 2 / 3)
HFULL = HID // P
HREM = HID - HFULL * P
HT = HFULL + 1
W1T = 2 * HFULL + 1
GATE0 = 64
LAYERS = 2
QK_SCALE = 8.0
EPS = 1e-5
XW = 2 * (N + 4)
X1 = N + 4
NLE = "natural_log_exp_and_others"


def ge(engine, sem, value):
    if not isinstance(value, int) or value > 0:
        engine.wait_ge(sem, value)


def at(ap, i):
    return ap[:, bass.ds(i, 1)]


def x_view(xT, b):
    return xT[:, bass.ds(b, 1), 0:2 * X1].rearrange("p b (k c) -> p (b k) c", k=KD)[:, :, 0:N]


def h_view(xT, b):
    return xT[:, bass.ds(b, 1), 0:2 * (X1 - 1)].rearrange("p b (k c) -> p (b k) c", k=KD)[:, :, 0:N]


def spread(ap, n):
    return ap.unsqueeze(2).broadcast_to([ap.shape[0], ap.shape[1], n, ap.shape[2]])


def along(ap, n):
    return ap.unsqueeze(2).broadcast_to([ap.shape[0], ap.shape[1], n])


def start_at_zero(nc, semaphores):
    with nc.Block() as block:
        @block.sync
        def _(sp):
            for s in semaphores:
                sp.sem_clear(s)


def attention_block(nc, io, xT, ident, identb, epsc):
    ctx = ExitStack()
    with ctx:
        def sb(name, shape, dt=F32):
            return ctx.enter_context(nc.sbuf_tensor(name, shape, dt))

        def pb(name):
            return ctx.enter_context(nc.psum_tensor(name, [P, 512], F32))

        def sem(name):
            return ctx.enter_context(nc.semaphore("a_" + name))

        QKW = 2 * D
        wst = sb("aw_stage", [P, KD, 3 * D])
        whi = sb("aw_hi", [P, KD, 3 * D], F32R)
        wlo = sb("aw_lo", [P, KD, 3 * D], F32R)
        wraw = sb("aw_raw", [P, 3 * KD, D])
        cosT = sb("a_cos", [P, TT, D])
        sinT = sb("a_sin", [P, TT, D])
        maskT = sb("a_mask", [P, N], BF16)
        x_in = sb("a_x", [P, TT, D])
        stats = sb("a_stats", [P, TT, 6])
        mv = sb("a_mv", [P, TT, 2])
        spare = sb("a_spare", [P, 1])
        lnv = sb("a_lnv", [P, TT])
        rstd = sb("a_rstd", [P, TT])
        xn = sb("a_xn", [P, TT, D])
        hhi = sb("a_hhi", [P, KD, N], F32R)
        hlo = sb("a_hlo", [P, KD, N], F32R)
        raw = sb("a_raw", [P, 2, QKW])
        t2 = sb("a_t2", [P, 2, QKW])
        rot = sb("a_rot", [P, TT, QKW])
        V = sb("a_v", [P, TT, D])
        QK = sb("a_qk", [P, 2 * KD, N])
        Pr = sb("a_p", [P, TT, N])
        PT = sb("a_pt", [P, TT, N])
        mx = sb("a_mx", [P, TT])
        nb = sb("a_nb", [P, TT])
        sums = sb("a_sums", [P, TT])
        rinv = sb("a_rinv", [P, TT])
        O = sb("a_o", [P, TT, D])

        ring = [pb("a_ring0"), pb("a_ring1")]
        psT = pb("a_psT")
        psS = [pb("a_psS0"), pb("a_psS1")]
        psP = [pb("a_psP0"), pb("a_psP1")]
        psO = pb("a_psO")

        names = ("w_in c_in w_tr w_ev w_hi w_lo x_in0 bn agg lnv rstd xn xT_ps xT_hi xT_sb xT_lo "
                 "proj_ps proj_sb t2_done t1_done rot_done qkT_ps qkT_sb s_ps m_red m_bias exp_done "
                 "rinv_done pT_ps pT_sb o_ps o_sb out_dma").split()
        S = {n: sem(n) for n in names}
        start_at_zero(nc, S.values())
        block = ctx.enter_context(nc.Block())
        x_v = io["x"].rearrange("b (t p) d -> b p t d", p=P)
        s_v = io["s"].rearrange("b (t p) d -> b p t d", p=P)
        scale = 1.0 / np.sqrt(D)
        TILES = 2 * TT

        def pipeline(e, step):
            step(0, True, False)
            with e.Fori(1, B) as i:
                step(i, True, True)
            step(B, False, True)

        @block.sync
        def _(sp):
            sp.dma_start(x_in[:, :, :], x_v[0]).then_inc(S["x_in0"], 16)
            for j, w in enumerate(("wq", "wk", "wv")):
                sp.dma_start(wraw[:, KD * j:KD * (j + 1), :], io[w].rearrange("(k p) d -> p k d", p=P)).then_inc(S["w_in"], 16)
            sp.dma_start(cosT[:, :, :], io["acos"]).then_inc(S["c_in"], 16)
            sp.dma_start(sinT[:, :, :], io["asin"]).then_inc(S["c_in"], 16)
            sp.dma_start(maskT[:, :], io["amask"]).then_inc(S["c_in"], 16)

            def step(i, front, back):
                if front and not (isinstance(i, int) and i == B - 1):
                    ge(sp, S["xn"], i + 1)
                    sp.dma_start(at(x_in[:, :, :].unsqueeze(1), 0), x_v[bass.ds(i + 1, 1)].rearrange("b p t d -> p b t d")).then_inc(S["x_in0"], 16)
                if back:
                    ge(sp, S["o_sb"], TT * i)
                    sp.dma_start(s_v[bass.ds(i - 1, 1)].rearrange("b p t d -> p b t d"), O[:, :, :].unsqueeze(1)).then_inc(S["out_dma"], 16)
            step(0, True, False)
            with sp.Fori(1, B - 1) as i:
                step(i, True, True)
            step(B - 1, False, True)
            step(B, False, True)
            sp.wait_ge(S["out_dma"], 16 * (B + 1))

        @block.gpsimd
        def _(pool):
            pool.wait_ge(S["c_in"], 48)

            def step(i, front, back):
                if front:
                    for t in range(TT):
                        ge(pool, S["proj_sb"], TILES * i + t + 1)
                        ge(pool, S["rot_done"], TT * i + t - 1)
                        src = raw[:, t % 2, :].rearrange("p (q c s) -> p q c s", q=2, s=2)
                        dst = t2[:, t % 2, :].rearrange("p (q c s) -> p q c s", q=2, s=2)
                        tab = sinT[:, t, :].rearrange("p (c s) -> p c s", s=2).unsqueeze(1).broadcast_to([P, 2, D // 2, 2])
                        pool.tensor_tensor(dst[:, :, :, 0], src[:, :, :, 1], tab[:, :, :, 0], ALU.mult).then_inc(S["t2_done"], 1)
                        pool.tensor_tensor(dst[:, :, :, 1], src[:, :, :, 0], tab[:, :, :, 1], ALU.mult).then_inc(S["t2_done"], 1)
            pipeline(pool, step)

        @block.scalar
        def _(act):
            act.preload_act_table_set(NLE)
            for j in range(3 * KD // 2):
                act.wait_ge(S["w_tr"], j + 1)
                act.activation(wst[:, 0:KD, j * D:(j + 1) * D], ring[j % 2][:, :].rearrange("p (k o) -> p k o", k=KD), ACT.Copy).then_inc(S["w_ev"], 1)
            act.wait_ge(S["w_ev"], 3)
            act.activation(whi[:, :, :], wst[:, :, :], ACT.Copy).then_inc(S["w_hi"], 1)

            def proj(i, t):
                n = TILES * i + t
                ge(act, S["proj_ps"], n + 1)
                if t < TT:
                    ge(act, S["rot_done"], TT * i + t - 1)
                    act.activation(raw[:, t % 2, :], ring[t % 2][:, :], ACT.Copy).then_inc(S["proj_sb"], 1)
                else:
                    act.activation(V[:, t - TT, :], ring[t % 2][:, 0:D], ACT.Copy).then_inc(S["proj_sb"], 1)

            def norm(i):
                ge(act, S["agg"], i + 1)
                act.activation(lnv[:, :], mv[:, :, 1], ACT.Ln, bias=epsc[:, 0:1]).then_inc(S["lnv"], 1)
                ge(act, S["lnv"], i + 1)
                act.activation(rstd[:, :], lnv[:, :], ACT.Exp, scale=-0.5).then_inc(S["rstd"], 1)

            def high(i):
                ge(act, S["xT_ps"], i + 1)
                for k in range(KD):
                    act.activation(hhi[:, k, :], ring[k][:, :], ACT.Copy).then_inc(S["xT_hi"], 1)

            def softmax(i, t):
                w = (t + 1) * P
                ge(act, S["m_bias"], TT * (i - 1) + t + 1)
                act.activation(Pr[:, t, 0:w], psS[t % 2][:, 0:w], ACT.Exp, bias=nb[:, t:t + 1], scale=scale,
                               accum_out=sums[:, t:t + 1]).then_inc(S["exp_done"], 1)

            def out(i, t):
                ge(act, S["o_ps"], TT * (i - 1) + t + 1)
                ge(act, S["rinv_done"], TT * (i - 1) + t + 1)
                if t == 0:
                    ge(act, S["out_dma"], 16 * i)
                act.activation(O[:, t, :], psO[:, 0:D], ACT.Copy, scale=rinv[:, t:t + 1]).then_inc(S["o_sb"], 1)

            def step(i, front, back):
                if front:
                    norm(i)
                if back:
                    softmax(i, 0)
                    softmax(i, 1)
                if front:
                    high(i)
                    proj(i, 0)
                if back:
                    softmax(i, 2)
                    out(i, 0)
                if front:
                    proj(i, 1)
                if back:
                    softmax(i, 3)
                    out(i, 1)
                if front:
                    proj(i, 2)
                if back:
                    out(i, 2)
                if front:
                    proj(i, 3)
                if back:
                    out(i, 3)
                if front:
                    for t in range(TT):
                        ge(act, S["qkT_ps"], TT * i + t + 1)
                        act.activation(QK[:, :, t * P:(t + 1) * P], psT[:, :].rearrange("p (a c) -> p a c", c=P), ACT.Copy).then_inc(S["qkT_sb"], 1)
                    for t in range(TT, 2 * TT):
                        proj(i, t)
            pipeline(act, step)

        @block.vector
        def _(dve):
            dve.wait_ge(S["w_hi"], 1)
            dve.tensor_tensor(wlo[:, :, :], wst[:, :, :], whi[:, :, :].bitcast(F32), ALU.subtract).then_inc(S["w_lo"], 1)
            dve.memset(spare[:, :], 0.0).then_inc(S["out_dma"], 16)
            dve.wait_ge(S["c_in"], 48)

            def norm(i):
                ge(dve, S["x_in0"], 16 * (i + 1))
                for t in range(TT):
                    dve.bn_stats(stats[:, t, :], x_in[:, t, :]).then_inc(S["bn"], 1)
                ge(dve, S["bn"], TT * (i + 1))
                dve.memset(spare[:, :], 0.0)
                for t in range(TT):
                    last = dve.bn_aggr(mv[:, t, :], stats[:, t, :])
                last.then_inc(S["agg"], 1)
                ge(dve, S["rstd"], i + 1)
                for t in range(TT):
                    last = dve.tensor_scalar(xn[:, t, :], x_in[:, t, :], mv[:, t, 0:1], rstd[:, t:t + 1], ALU.subtract, ALU.mult)
                last.then_inc(S["xn"], 1)

            def low(i):
                ge(dve, S["xT_ps"], i + 1)
                ge(dve, S["xT_hi"], KD * (i + 1))
                for k in range(KD):
                    dve.tensor_tensor(hlo[:, k, :], ring[k][:, :], hhi[:, k, :].bitcast(F32), ALU.subtract).then_inc(S["xT_lo"], 1)
                for k in range(KD):
                    last = dve.tensor_copy(xT[:, bass.ds(i, 1), k * X1:k * X1 + N], ring[k][:, :].unsqueeze(1))
                last.then_inc(S["xT_sb"], 1)

            def rotate(i, t):
                ge(dve, S["proj_sb"], TILES * i + t + 1)
                r = rot[:, t, :].rearrange("p (q d) -> p q d", q=2)
                tab = cosT[:, t, :].unsqueeze(1).broadcast_to([P, 2, D])
                dve.tensor_tensor(r, raw[:, t % 2, :].rearrange("p (q d) -> p q d", q=2), tab, ALU.mult).then_inc(S["t1_done"], 1)
                ge(dve, S["t1_done"], TT * i + t + 1)
                ge(dve, S["t2_done"], 2 * (TT * i + t + 1))
                dve.tensor_tensor(rot[:, t, :], rot[:, t, :], t2[:, t % 2, :], ALU.add).then_inc(S["rot_done"], 1)

            def maxima(i, t):
                n = TT * (i - 1) + t + 1
                ge(dve, S["s_ps"], n)
                dve.reduce_max(mx[:, t:t + 1], psS[t % 2][:, 0:(t + 1) * P], AX.X).then_inc(S["m_red"], 1)
                ge(dve, S["m_red"], n)
                dve.tensor_scalar(nb[:, t:t + 1], mx[:, t:t + 1], -scale, None, ALU.mult).then_inc(S["m_bias"], 1)

            def inverse(i, t):
                ge(dve, S["exp_done"], TT * (i - 1) + t + 1)
                dve.reciprocal(rinv[:, t:t + 1], sums[:, t:t + 1]).then_inc(S["rinv_done"], 1)

            def p_copy(i, t):
                w = (t + 1) * P
                ge(dve, S["pT_ps"], TT * (i - 1) + t + 1)
                dve.tensor_copy(PT[:, t, 0:w], psP[t % 2][:, 0:w]).then_inc(S["pT_sb"], 1)

            def step(i, front, back):
                if front:
                    norm(i)
                if back:
                    maxima(i, 0)
                    maxima(i, 1)
                    inverse(i, 0)
                if front:
                    low(i)
                if back:
                    p_copy(i, 0)
                    inverse(i, 1)
                    maxima(i, 2)
                    p_copy(i, 1)
                if front:
                    rotate(i, 0)
                if back:
                    inverse(i, 2)
                    maxima(i, 3)
                    p_copy(i, 2)
                if front:
                    rotate(i, 1)
                if back:
                    inverse(i, 3)
                    p_copy(i, 3)
                if front:
                    rotate(i, 2)
                    rotate(i, 3)
            pipeline(dve, step)

        @block.tensor
        def _(pe):
            pe.wait_ge(S["w_in"], 48)
            for j in range(3):
                if j >= 2:
                    pe.wait_ge(S["w_ev"], j - 1)
                for k in range(KD):
                    for o in range(KD):
                        last = pe.transpose(ring[j % 2][:, k * D + o * P:k * D + (o + 1) * P],
                                            wraw[:, KD * j + o, k * P:(k + 1) * P], ident[:, :])
                last.then_inc(S["w_tr"], 1)
            pe.wait_ge(S["w_ev"], 3)
            pe.wait_ge(S["w_lo"], 1)

            def x_transposes(i):
                ge(pe, S["xn"], i + 1)
                ge(pe, S["proj_sb"], TILES * i)
                for k in range(KD):
                    for t in range(TT):
                        last = pe.transpose(ring[k][:, t * P:(t + 1) * P], xn[:, t, k * P:(k + 1) * P], ident[:, :])
                last.then_inc(S["xT_ps"], 1)

            def project(i, t):
                c0, w = (0, QKW) if t < TT else (QKW, D)
                tok = slice((t % TT) * P, (t % TT + 1) * P)
                if t < 2:
                    ge(pe, S["xT_lo"], KD * (i + 1))
                    ge(pe, S["xT_sb"], i + 1)
                else:
                    ge(pe, S["proj_sb"], TILES * i + t - 1)
                m = 0
                for k in range(KD):
                    for a, w_ in ((hhi, whi), (hhi, wlo), (hlo, whi)):
                        last = pe.matmul(ring[t % 2][:, 0:w], a[:, k, tok], w_[:, k, c0:c0 + w], start=(m == 0), stop=(m == 3 * KD - 1))
                        m += 1
                last.then_inc(S["proj_ps"], 1)

            def qk_transposes(i, t):
                ge(pe, S["rot_done"], TT * i + t + 1)
                ge(pe, S["qkT_sb"], TT * i + t)
                for a in range(2 * KD):
                    last = pe.transpose(psT[:, a * P:(a + 1) * P], rot[:, t, a * P:(a + 1) * P], ident[:, :])
                last.then_inc(S["qkT_ps"], 1)

            def scores(i, t):
                w = (t + 1) * P
                ge(pe, S["qkT_sb"], TT * i)
                if t >= 2:
                    ge(pe, S["exp_done"], TT * (i - 1) + t - 1)
                pe.matmul(psS[t % 2][:, 0:w], identb[:, :], maskT[:, N - w:N], start=True, stop=False)
                for k in range(KD):
                    last = pe.matmul(psS[t % 2][:, 0:w], QK[:, k, t * P:(t + 1) * P], QK[:, KD + k, 0:w], start=False, stop=(k == KD - 1))
                last.then_inc(S["s_ps"], 1)

            def p_transposes(i, t):
                ge(pe, S["exp_done"], TT * (i - 1) + t + 1)
                if t >= 2:
                    ge(pe, S["pT_sb"], TT * (i - 1) + t - 1)
                for k in range(t + 1):
                    last = pe.transpose(psP[t % 2][:, k * P:(k + 1) * P], Pr[:, t, k * P:(k + 1) * P], ident[:, :])
                last.then_inc(S["pT_ps"], 1)

            def values(i, t):
                ge(pe, S["pT_sb"], TT * (i - 1) + t + 1)
                ge(pe, S["proj_sb"], TILES * i)
                if t:
                    ge(pe, S["o_sb"], TT * (i - 1) + t)
                for k in range(t + 1):
                    last = pe.matmul(psO[:, 0:D], PT[:, t, k * P:(k + 1) * P], V[:, k, :], start=(k == 0), stop=(k == t))
                last.then_inc(S["o_ps"], 1)

            def step(i, front, back):
                if back:
                    scores(i, 0)
                    scores(i, 1)
                if front:
                    x_transposes(i)
                if back:
                    p_transposes(i, 0)
                if front:
                    project(i, 0)
                if back:
                    scores(i, 2)
                    p_transposes(i, 1)
                    values(i, 0)
                if front:
                    project(i, 1)
                if back:
                    scores(i, 3)
                    p_transposes(i, 2)
                    values(i, 1)
                if front:
                    project(i, 2)
                if back:
                    p_transposes(i, 3)
                    values(i, 2)
                if front:
                    project(i, 3)
                if back:
                    values(i, 3)
                if front:
                    for t in range(TT):
                        qk_transposes(i, t)
                    for t in range(TT, 2 * TT):
                        project(i, t)
            pipeline(pe, step)


def layer_block(nc, io, layer, xT, ident, identb, ones, epsc):
    ctx = ExitStack()
    with ctx:
        def sb(name, shape, dt=F32):
            return ctx.enter_context(nc.sbuf_tensor(f"l{layer}_{name}", shape, dt))

        def pb(name, n=1):
            return ctx.enter_context(nc.psum_tensor(f"l{layer}_{name}", [P, 512 * n], F32))

        def sem(name):
            return ctx.enter_context(nc.semaphore(f"l{layer}_{name}"))

        QKW = 2 * INNER
        wq_hi = sb("wq_hi", [P, KD, 3 * INNER], F32R)
        wq_lo = sb("wq_lo", [P, KD, 3 * INNER], F32R)
        w1_hi = sb("w1_hi", [P, KD, W1T * P], F32R)
        w1_lo = sb("w1_lo", [P, KD, W1T * P], F32R)
        wo = sb("wo", [P, INNER // P, D])
        w2 = sb("w2", [P, HT, D])
        gcol = sb("g", [P, KD])
        bcol = sb("b", [P, KD])
        b1raw = sb("b1raw", [P, W1T])
        b1col = sb("b1", [P, W1T])
        b2col = sb("b2", [P, KD])
        scl = sb("scl", [P, 2, DH])
        scls = sb("scls", [P, 2, DH])
        cosT = sb("cos", [P, TT, 2, DH])
        sinT = sb("sin", [P, TT, 2, DH])
        maskT = sb("mask", [P, 2 * P], BF16)
        raw = sb("raw", [P, 2, QKW])
        Pr = raw
        sq = sb("sq", [P, QKW])
        t2 = sb("t2", [P, QKW])
        rot = sb("rot", [P, TT, QKW])
        PT = rot
        ssq = sb("ssq", [P, TT, 2 * HEADS])
        lnq = sb("lnq", [P, TT, 2 * HEADS])
        rn = sb("rn", [P, TT, 2 * HEADS])
        sc8 = sb("sc8", [P, TT, HEADS])
        nsc8 = sb("nsc8", [P, TT, HEADS])
        hhi = sb("hhi", [P, KD, N], F32R)
        hlo = sb("hlo", [P, KD, N], F32R)
        dF = sb("dF", [P, KD, N])[:, :, :]
        sqF = sb("sqF", [P, KD, N])
        fhi = sb("fhi", [P, KD, N], F32R)
        flo = sb("flo", [P, KD, N], F32R)
        rstdF = sb("rstdF", [P, N])
        G = sb("G", [P, 2, N])
        U = sb("U", [P, HT, N])
        OT = U
        QT = sb("QT", [P, 2, INNER // P, N])
        stage = QT[:, :, :, :].rearrange("p a b c -> p (a b c)")
        KT = sb("KT", [P, INNER // P, N])
        V = sb("V", [P, TT, INNER])
        mx = sb("mx", [P, 2, TT])
        nb = sb("nb", [P, 2, TT])
        sums = sb("sums", [P, 2, TT])
        rinv = sb("rinv", [P, 2, TT])

        ring = [pb("ring0"), pb("ring1")]
        psS = pb("psS", 2)
        psP = pb("psP", 2)
        psF = pb("psF", 2)
        scores_of = (psS, psF)
        hidden_of = ((psF[:, 0:N], psF[:, N:2 * N]), (ring[0][:, :], ring[1][:, :]))

        names = ("w_in w_in1 h_ready small tabs w1pad w2pad w2_in wq_hi wq_lo w1_hi w1_lo b1_ps b1_sb zeroed "
                 "h_hi h_lo proj_ps proj_sb sq_done ssq_done t1_done t2_done rot_done clamped lnq_done rn_done "
                 "k_scaled sc_done qT_ps qT_sb kT_ps kT_sb s_ps m_red m_bias exp_done rinv_done p_done pT_ps "
                 "pT_sb0 pT_sb1 o_ps o_sb wo_ps x_attn mean_ps d_done sqF_done var_ps lnF_done rstdF_done hn_done "
                 "f_hi f_lo w1_ps gelu_done u_done w2_ps x_ffn").split()
        S = {n: sem(n) for n in names}
        start_at_zero(nc, S.values())
        block = ctx.enter_context(nc.Block())

        def heads_of(ap, n):
            return ap.rearrange("p (h d) -> p h d", h=n)

        def pipeline(e, step):
            step(0, True, False)
            with e.Fori(1, B) as i:
                step(i, True, True)
            step(B, False, True)

        @block.sync
        def _(sp):
            st = stage[:, 0:KD * 3 * INNER].rearrange("p (k n) -> p k n", k=KD)
            sp.dma_start(st, io["wqkv"][layer].rearrange("(k p) n -> p k n", p=P)).then_inc(S["w_in"], 16)
            sp.dma_start(cosT[:, :, :, :], io["fcos"]).then_inc(S["small"], 16)
            sp.dma_start(sinT[:, :, :, :], io["fsin"]).then_inc(S["small"], 16)
            sp.dma_start(maskT[:, :], io["fmask"]).then_inc(S["small"], 16)
            for j, n in enumerate(("q_scale", "k_scale")):
                row = io[n][layer:layer + 1, :]
                sp.dma_start(scl[:, j, :], row.broadcast_to([P, DH])).then_inc(S["small"], 16)
                for s in range(2):
                    sp.dma_start(scls[:, j, s * DH // 2:(s + 1) * DH // 2],
                                 row[:, (1 - s) * DH // 2:(2 - s) * DH // 2].broadcast_to([P, DH // 2])).then_inc(S["small"], 16)
            for dst, n in ((gcol, "ln_g"), (bcol, "ln_b"), (b2col, "b2")):
                sp.dma_start(dst[:, :], io[n][layer].rearrange("(k p) -> p k", p=P), allow_slow_non_contiguous=True).then_inc(S["small"], 16)
            b1 = io["b1"][layer]
            sp.wait_ge(S["w1pad"], 1)
            for s in range(2):
                full = b1[s * HID:s * HID + HFULL * P].rearrange("(j p) -> p j", p=P)
                sp.dma_start(b1raw[:, s * HFULL:(s + 1) * HFULL], full, allow_slow_non_contiguous=True).then_inc(S["small"], 16)
                rest = b1[s * HID + HFULL * P:(s + 1) * HID].rearrange("(p j) -> p j", j=1)
                sp.dma_start(b1raw[s * GATE0:s * GATE0 + HREM, 2 * HFULL:W1T], rest, allow_slow_non_contiguous=True).then_inc(S["small"], 16)
            sp.dma_start(wo[:, :, :], io["wo"][layer].rearrange("(k p) n -> p k n", p=P)).then_inc(S["w2_in"], 16)
            sp.wait_ge(S["w2pad"], 1)
            sp.dma_start(w2[:, 0:HFULL, :], io["w2"][layer, 0:HFULL * P].rearrange("(k p) n -> p k n", p=P)).then_inc(S["w2_in"], 16)
            sp.dma_start(w2[0:HREM, HFULL, :], io["w2"][layer, HFULL * P:HID]).then_inc(S["w2_in"], 16)
            sp.wait_ge(S["w1pad"], 2)
            st1 = stage[:, 0:KD * W1T * P].rearrange("p (k n) -> p k n", k=KD)
            w1 = io["w1"][layer].rearrange("(k p) n -> p k n", p=P)
            for s in range(2):
                sp.dma_start(st1[:, :, s * HFULL * P:(s + 1) * HFULL * P], w1[:, :, s * HID:s * HID + HFULL * P]).then_inc(S["w_in1"], 16)
                c = 2 * HFULL * P + s * GATE0
                sp.dma_start(st1[:, :, c:c + HREM], w1[:, :, s * HID + HFULL * P:(s + 1) * HID]).then_inc(S["w_in1"], 16)
            sp.wait_ge(S["w_in1"], 64)

        SMALL = 16 * (3 + 2 * 3 + 3 + 4)

        @block.gpsimd
        def _(pool):
            pool.wait_ge(S["tabs"], 2)

            def rotate(i, t):
                ge(pool, S["proj_sb"], 3 * (TT * i + t) + 2)
                ge(pool, S["rot_done"], TT * i + t)
                for j in range(2):
                    src = raw[:, t % 2, j * INNER:(j + 1) * INNER].rearrange("p (h s d) -> p h s d", h=HEADS, s=2)
                    dst = t2[:, j * INNER:(j + 1) * INNER].rearrange("p (h s d) -> p h s d", h=HEADS, s=2)
                    tab = sinT[:, t, j, :].rearrange("p (s d) -> p s d", s=2)
                    for s in range(2):
                        pool.tensor_tensor(dst[:, :, s, :], src[:, :, 1 - s, :],
                                           tab[:, s, :].unsqueeze(1).broadcast_to([P, HEADS, DH // 2]), ALU.mult).then_inc(S["t2_done"], 1)

            def scale_k(i, t):
                n = TT * i + t + 1
                ge(pool, S["rot_done"], n)
                ge(pool, S["rn_done"], n)
                kr = heads_of(rot[:, t, INNER:QKW], HEADS)
                pool.tensor_tensor(kr, kr, along(rn[:, t, HEADS:2 * HEADS], DH), ALU.mult).then_inc(S["k_scaled"], 1)

            def step(i, attn, ffn):
                if attn:
                    rotate(i, 0)
                    rotate(i, 1)
                    scale_k(i, 0)
                    rotate(i, 2)
                    scale_k(i, 1)
                if ffn:
                    ge(pool, S["rstdF_done"], i)
                    pool.tensor_tensor(dF, dF, rstdF[:, :].unsqueeze(1).broadcast_to([P, KD, N]), ALU.mult).then_inc(S["hn_done"], 1)
                if attn:
                    rotate(i, 3)
                    scale_k(i, 2)
                if ffn:
                    ge(pool, S["f_hi"], i)
                    pool.tensor_tensor(flo[:, :, :], dF, fhi[:, :, :].bitcast(F32), ALU.subtract).then_inc(S["f_lo"], 1)
                if attn:
                    scale_k(i, 3)
                    for h in range(HEADS):
                        ge(pool, S["rinv_done"], HEADS * i + h + 1)
                        pr = Pr[:, h % 2, :].rearrange("p (t c) -> p t c", t=TT)
                        pool.tensor_tensor(pr[:, 0, P:2 * P], pr[:, 0, P:2 * P], rinv[:, h % 2, 0:1].broadcast_to([P, P]), ALU.mult)
                        pool.tensor_tensor(pr[:, 1:TT, :], pr[:, 1:TT, :], along(rinv[:, h % 2, 1:TT], 2 * P), ALU.mult).then_inc(S["p_done"], 1)
            pipeline(pool, step)

        @block.scalar
        def _(act):
            act.preload_act_table_set(NLE)
            act.wait_ge(S["w_in"], 16)
            st = stage[:, 0:KD * 3 * INNER].rearrange("p (k n) -> p k n", k=KD)
            act.activation(wq_hi[:, :, :], st, ACT.Copy).then_inc(S["wq_hi"], 1)
            act.wait_ge(S["w_in1"], 64)
            act.wait_ge(S["small"], SMALL)
            st1 = stage[:, 0:KD * W1T * P].rearrange("p (k n) -> p k n", k=KD)
            for k in range(KD):
                act.activation(w1_hi[:, k, :], st1[:, k, :], ACT.Copy, scale=gcol[:, k:k + 1]).then_inc(S["w1_hi"], 1)

            def copies(i, t):
                for c in range(3):
                    n = 3 * (TT * i + t) + c
                    ge(act, S["proj_ps"], n + 1)
                    if c == 0 and t >= 2:
                        ge(act, S["rot_done"], TT * i + t - 1)
                    dst = raw[:, t % 2, c * INNER:(c + 1) * INNER] if c < 2 else V[:, t, :]
                    act.activation(dst, ring[(t + c) % 2][:, :], ACT.Copy).then_inc(S["proj_sb"], 1)
                    if c == 1:
                        ge(act, S["proj_sb"], n + 1)
                        ge(act, S["ssq_done"], TT * i + t)
                        act.activation(sq[:, :], raw[:, t % 2, :], ACT.Square).then_inc(S["sq_done"], 1)
                ge(act, S["clamped"], TT * i + t + 1)
                act.activation(lnq[:, t, :], ssq[:, t, :], ACT.Ln).then_inc(S["lnq_done"], 1)
                ge(act, S["lnq_done"], TT * i + t + 1)
                act.activation(rn[:, t, :], lnq[:, t, :], ACT.Exp, scale=-0.5).then_inc(S["rn_done"], 1)

            def high(b, n):
                ge(act, S["proj_ps"], 3 * TT * (n - 1))
                act.activation(hhi[:, :, :], h_view(xT, b), ACT.Copy).then_inc(S["h_hi"], 1)

            def q_evac(i, t):
                ge(act, S["qT_ps"], TT * i + t + 1)
                for par in range(2):
                    rows = slice(par * DH, (par + 1) * DH)
                    last = act.activation(QT[rows, par, :, t * P:(t + 1) * P], psS[rows, 0:512].rearrange("p (a c) -> p a c", c=P), ACT.Copy)
                last.then_inc(S["qT_sb"], 1)

            def gelu(i, j):
                u = i - 1
                ge(act, S["w1_ps"], HT * u + j + 1)
                if j >= 2:
                    ge(act, S["u_done"], HT * u + j - 1)
                gate = hidden_of[j % 2][0]
                if j < HFULL:
                    act.activation(G[:, j % 2, :], gate, ACT.Gelu, bias=b1col[:, HFULL + j:HFULL + j + 1]).then_inc(S["gelu_done"], 1)
                else:
                    act.activation(G[0:HREM, j % 2, :], gate[GATE0:GATE0 + HREM, :], ACT.Gelu,
                                   bias=b1col[GATE0:GATE0 + HREM, 2 * HFULL:W1T]).then_inc(S["gelu_done"], 1)

            def p_evac(i, h):
                ge(act, S["pT_ps"], HEADS * i + h + 1)
                act.activation(PT[:, h % 2, 0:512], psP[:, 0:512], ACT.Copy).then_inc(S["pT_sb0"], 1)

            def softmax(i, h):
                ge(act, S["m_bias"], HEADS * i + h + 1)
                ge(act, S["pT_ps"], HEADS * i + h - 1)
                ps = scores_of[h % 2]
                for t in range(TT):
                    c0 = P if t == 0 else 0
                    last = act.activation(Pr[:, h % 2, t * 2 * P + c0:(t + 1) * 2 * P], ps[:, t * 2 * P + c0:(t + 1) * 2 * P], ACT.Exp,
                                          bias=nb[:, h % 2, t:t + 1], scale=sc8[:, t, h:h + 1], accum_out=sums[:, h % 2, t:t + 1])
                last.then_inc(S["exp_done"], 1)

            def step(i, attn, ffn):
                if attn:
                    copies(i, 0)
                    copies(i, 1)
                if ffn:
                    ge(act, S["d_done"], i)
                    act.activation(sqF[:, :, :], dF, ACT.Square).then_inc(S["sqF_done"], 1)
                if attn:
                    q_evac(i, 0)
                    copies(i, 2)
                if ffn:
                    ge(act, S["var_ps"], i)
                    act.activation(rstdF[:, :], psF[:, N:2 * N], ACT.Ln, bias=epsc[:, 0:1]).then_inc(S["lnF_done"], 1)
                    ge(act, S["lnF_done"], i)
                    act.activation(rstdF[:, :], rstdF[:, :], ACT.Exp, scale=-0.5).then_inc(S["rstdF_done"], 1)
                if attn:
                    q_evac(i, 1)
                    copies(i, 3)
                if ffn:
                    ge(act, S["hn_done"], i)
                    act.activation(fhi[:, :, :], dF, ACT.Copy).then_inc(S["f_hi"], 1)
                if attn:
                    q_evac(i, 2)
                if ffn:
                    gelu(i, 0)
                if attn:
                    q_evac(i, 3)
                if ffn:
                    for j in range(1, HT):
                        gelu(i, j)
                if attn:
                    act.preload_act_table_set(NLE)
                    high((i + 1) % B, i + 2)
                    for h in range(HEADS + 3):
                        if 2 <= h < HEADS + 2:
                            p_evac(i, h - 2)
                        if h < HEADS:
                            softmax(i, h)
                        if h >= 3 and h % 2 == 0:
                            pair = (h - 3) // 2
                            ge(act, S["o_ps"], HEADS // 2 * i + pair + 1)
                            act.activation(OT[:, pair, :], ring[pair % 2][:, :], ACT.Copy).then_inc(S["o_sb"], 1)
            high(0, 1)
            pipeline(act, step)

        @block.vector
        def _(dve):
            dve.memset(b1raw[:, :], 0.0).then_inc(S["w1pad"], 1)
            dve.memset(w2[:, HFULL, :], 0.0).then_inc(S["w2pad"], 1)
            dve.memset(U[:, HFULL, :], 0.0)
            dve.wait_ge(S["small"], SMALL)
            for c, (tab, s) in enumerate(((cosT, scl), (sinT, scls))):
                dve.tensor_tensor(tab[:, :, :, :].rearrange("p t j d -> p t (j d)"), tab[:, :, :, :].rearrange("p t j d -> p t (j d)"),
                                  s[:, :, :].rearrange("p j d -> p (j d)").unsqueeze(1).broadcast_to([P, TT, 2 * DH]), ALU.mult).then_inc(S["tabs"], 1)
            dve.wait_ge(S["wq_hi"], 1)
            st = stage[:, 0:KD * 3 * INNER].rearrange("p (k n) -> p k n", k=KD)
            dve.tensor_tensor(wq_lo[:, :, :], st, wq_hi[:, :, :].bitcast(F32), ALU.subtract).then_inc(S["wq_lo"], 1)
            dve.wait_ge(S["wq_lo"], 1)
            st1 = stage[:, 0:KD * W1T * P].rearrange("p (k n) -> p k n", k=KD)
            dve.memset(st1[:, :, 2 * HFULL * P:], 0.0).then_inc(S["w1pad"], 1)
            dve.wait_ge(S["w1_hi"], KD)
            for k in range(KD):
                last = dve.scalar_tensor_tensor(out=w1_lo[:, k, :], in0=st1[:, k, :], scalar=gcol[:, k:k + 1],
                                                in1=w1_hi[:, k, :].bitcast(F32), op0=ALU.mult, op1=ALU.subtract)
            last.then_inc(S["w1_lo"], 1)
            dve.wait_ge(S["b1_ps"], 1)
            dve.tensor_tensor(b1col[:, :], psF[:, 0:W1T], b1raw[:, :], ALU.add).then_inc(S["b1_sb"], 1)
            dve.wait_ge(S["w1_lo"], 1)
            dve.memset(QT[DH:P, 0, :, :], 0.0)
            dve.memset(QT[0:DH, 1, :, :], 0.0).then_inc(S["zeroed"], 1)
            dve.wait_ge(S["tabs"], 2)
            dve.wait_ge(S["b1_sb"], 1)

            def rotate(i, t):
                n = TT * i + t
                ge(dve, S["sq_done"], n + 1)
                dve.tensor_reduce(ssq[:, t, :], sq[:, :].rearrange("p (h d) -> p h d", d=DH), AX.X, ALU.add).then_inc(S["ssq_done"], 1)
                ge(dve, S["ssq_done"], n + 1)
                dve.tensor_scalar(ssq[:, t, :], ssq[:, t, :], 1e-24, None, ALU.max).then_inc(S["clamped"], 1)
                for j in range(2):
                    last = dve.tensor_tensor(heads_of(rot[:, t, j * INNER:(j + 1) * INNER], HEADS),
                                             heads_of(raw[:, t % 2, j * INNER:(j + 1) * INNER], HEADS),
                                             cosT[:, t, j, :].unsqueeze(1).broadcast_to([P, HEADS, DH]), ALU.mult)
                last.then_inc(S["t1_done"], 1)
                ge(dve, S["t1_done"], n + 1)
                ge(dve, S["t2_done"], 4 * (n + 1))
                dve.tensor_tensor(rot[:, t, :], rot[:, t, :], t2[:, :], ALU.add).then_inc(S["rot_done"], 1)

            def gated(i, j):
                u = i - 1
                ge(dve, S["gelu_done"], HT * u + j + 1)
                gate, value = hidden_of[j % 2]
                if j < HFULL:
                    dve.scalar_tensor_tensor(out=U[:, j, :], in0=value, scalar=b1col[:, j:j + 1], in1=G[:, j % 2, :],
                                             op0=ALU.add, op1=ALU.mult).then_inc(S["u_done"], 1)
                else:
                    dve.scalar_tensor_tensor(out=U[0:HREM, j, :], in0=gate[0:HREM, :], scalar=b1col[0:HREM, 2 * HFULL:W1T],
                                             in1=G[0:HREM, j % 2, :], op0=ALU.add, op1=ALU.mult).then_inc(S["u_done"], 1)

            def low(b, n):
                ge(dve, S["h_hi"], n)
                dve.tensor_tensor(hlo[:, :, :], h_view(xT, b), hhi[:, :, :].bitcast(F32), ALU.subtract).then_inc(S["h_lo"], 1)

            def k_evac(i, t):
                ge(dve, S["kT_ps"], TT * i + t + 1)
                dve.tensor_copy(KT[:, :, t * P:(t + 1) * P], psS[:, 512:1024].rearrange("p (a c) -> p a c", c=P)).then_inc(S["kT_sb"], 1)

            def step(i, attn, ffn):
                if attn:
                    rotate(i, 0)
                if ffn:
                    ge(dve, S["mean_ps"], i)
                    for k in range(KD):
                        last = dve.tensor_tensor(dF[:, k], dF[:, k], psF[:, 0:N], ALU.subtract)
                    last.then_inc(S["d_done"], 1)
                if attn:
                    rotate(i, 1)
                    k_evac(i, 0)
                    rotate(i, 2)
                    k_evac(i, 1)
                    rotate(i, 3)
                    k_evac(i, 2)
                if ffn:
                    gated(i, 0)
                if attn:
                    k_evac(i, 3)
                    ge(dve, S["rn_done"], TT * (i + 1))
                    dve.tensor_scalar(sc8[:, :, :], rn[:, :, 0:HEADS], QK_SCALE, None, ALU.mult)
                    dve.tensor_scalar(nsc8[:, :, :], rn[:, :, 0:HEADS], -QK_SCALE, None, ALU.mult).then_inc(S["sc_done"], 1)
                if ffn:
                    for j in range(1, HT):
                        gated(i, j)
                if attn:
                    low((i + 1) % B, i + 2)
                if ffn:
                    ge(dve, S["w2_ps"], i)
                    for k in range(KD):
                        xk = xT[:, bass.ds(i - 1, 1), k * X1:k * X1 + N]
                        last = dve.scalar_tensor_tensor(out=xk, in0=psP[:, k * N:(k + 1) * N].unsqueeze(1), scalar=b2col[:, k:k + 1], in1=xk,
                                                        op0=ALU.add, op1=ALU.add)
                    last.then_inc(S["x_ffn"], 1)
                if attn:
                    ge(dve, S["sc_done"], i + 1)
                    for h in range(HEADS + 2):
                        ps = scores_of[h % 2]
                        if h < HEADS:
                            n = HEADS * i + h + 1
                            ge(dve, S["s_ps"], n)
                            dve.reduce_max(mx[:, h % 2, 0:1], ps[:, P:2 * P], AX.X)
                            dve.reduce_max(mx[:, h % 2, 1:TT], ps[:, 2 * P:].rearrange("p (t c) -> p t c", c=2 * P), AX.X).then_inc(S["m_red"], 1)
                            ge(dve, S["m_red"], n)
                            dve.tensor_tensor(nb[:, h % 2, :], mx[:, h % 2, :], nsc8[:, :, h], ALU.mult).then_inc(S["m_bias"], 1)
                        if h >= 2:
                            ge(dve, S["pT_ps"], HEADS * i + h - 1)
                            dve.tensor_copy(PT[:, h % 2, 512:896], psP[:, 512:896]).then_inc(S["pT_sb1"], 1)
                        if h < HEADS:
                            ge(dve, S["exp_done"], HEADS * i + h + 1)
                            dve.reciprocal(rinv[:, h % 2, :], sums[:, h % 2, :]).then_inc(S["rinv_done"], 1)
                    ge(dve, S["wo_ps"], i + 1)
                    for k in range(KD):
                        xk = xT[:, bass.ds(i, 1), k * X1:k * X1 + N]
                        dve.tensor_tensor(xk, xk, psP[:, k * N:(k + 1) * N].unsqueeze(1), ALU.add).then_inc(S["x_attn"], 1)
                    ge(dve, S["x_attn"], KD * (i + 1))
                    dve.tensor_scalar(dF, h_view(xT, i), 1.0, None, ALU.mult).then_inc(S["h_ready"], 1)
            low(0, 1)
            pipeline(dve, step)

        @block.tensor
        def _(pe):
            pe.wait_ge(S["w_in1"], 64)
            pe.wait_ge(S["small"], SMALL)
            st1 = stage[:, 0:KD * W1T * P].rearrange("p (k n) -> p k n", k=KD)
            for j in range(W1T):
                for k in range(KD):
                    last = pe.matmul(psF[:, j:j + 1], st1[:, k, j * P:(j + 1) * P], bcol[:, k:k + 1], start=(k == 0), stop=(k == KD - 1))
            last.then_inc(S["b1_ps"], 1)
            pe.wait_ge(S["wq_lo"], 1)
            pe.wait_ge(S["b1_sb"], 1)
            pe.wait_ge(S["w2_in"], 48)
            pe.wait_ge(S["zeroed"], 1)

            def project(i, t):
                for c in range(3):
                    n = 3 * (TT * i + t) + c
                    if t == 0 and c == 0:
                        ge(pe, S["h_lo"], i + 1)
                    elif t or c > 1:
                        ge(pe, S["proj_sb"], n - 1)
                    m = 0
                    for k in range(KD):
                        for a, w in ((hhi, wq_hi), (hhi, wq_lo), (hlo, wq_hi)):
                            last = pe.matmul(ring[(t + c) % 2][:, :], a[:, k, t * P:(t + 1) * P], w[:, k, c * INNER:(c + 1) * INNER],
                                             start=(m == 0), stop=(m == 3 * KD - 1))
                            m += 1
                    last.then_inc(S["proj_ps"], 1)

            def mean(i):
                ge(pe, S["h_ready"], i)
                for k in range(KD):
                    last = pe.matmul(psF[:, 0:N], ones[:, :], dF[:, k], start=(k == 0), stop=(k == KD - 1))
                last.then_inc(S["mean_ps"], 1)

            def variance(i):
                ge(pe, S["sqF_done"], i)
                for k in range(KD):
                    last = pe.matmul(psF[:, N:2 * N], ones[:, :], sqF[:, k, :], start=(k == 0), stop=(k == KD - 1))
                last.then_inc(S["var_ps"], 1)

            def hidden(i, j, attn):
                u = i - 1
                ge(pe, S["f_lo"], i)
                if j == 1 and attn:
                    ge(pe, S["proj_sb"], 3 * TT * (i + 1))
                if j >= 2:
                    ge(pe, S["u_done"], HT * u + j - 1)
                tiles = ((HFULL + j, 0), (j, 1)) if j < HFULL else ((2 * HFULL, 0),)
                for tile, bank in tiles:
                    m = 0
                    for k in range(KD):
                        for w, a in ((w1_hi, fhi), (w1_lo, fhi), (w1_hi, flo)):
                            last = pe.matmul(hidden_of[j % 2][bank], w[:, k, tile * P:(tile + 1) * P], a[:, k, :], start=(m == 0), stop=(m == 3 * KD - 1))
                            m += 1
                last.then_inc(S["w1_ps"], 1)

            def down(i):
                ge(pe, S["u_done"], HT * i)
                ge(pe, S["x_attn"], KD * i)
                for c in range(KD):
                    for k in range(HT):
                        last = pe.matmul(psP[:, c * N:(c + 1) * N], w2[:, k, c * P:(c + 1) * P], U[:, k, :], start=(k == 0), stop=(k == HT - 1))
                last.then_inc(S["w2_ps"], 1)

            def transposes(i, t):
                n = TT * i + t
                for j, (there, free, done) in enumerate((("rot_done", "qT_sb", "qT_ps"), ("k_scaled", "kT_sb", "kT_ps"))):
                    ge(pe, S[there], n + 1)
                    if t:
                        ge(pe, S[free], n)
                    for a in range(INNER // P):
                        last = pe.transpose(psS[:, j * 512 + a * P:j * 512 + (a + 1) * P],
                                            rot[:, t, j * INNER + a * P:j * INNER + (a + 1) * P], ident[:, :])
                    last.then_inc(S[done], 1)

            def scores(i, h):
                if h == 0:
                    ge(pe, S["qT_sb"], TT * (i + 1))
                    ge(pe, S["kT_sb"], TT * (i + 1))
                if h >= 2:
                    ge(pe, S["exp_done"], HEADS * i + h - 1)
                for t in range(TT):
                    c0 = P if t == 0 else 0
                    out = scores_of[h % 2][:, t * 2 * P + c0:(t + 1) * 2 * P]
                    pe.matmul(out, identb[:, :], maskT[:, c0:2 * P], start=True, stop=False)
                    last = pe.matmul(out, QT[:, h % 2, h // 2, t * P:(t + 1) * P], KT[:, h // 2, max(t - 1, 0) * P:(t + 1) * P], start=False, stop=True)
                last.then_inc(S["s_ps"], 1)

            def p_transposes(i, h, ffn):
                ge(pe, S["p_done"], HEADS * i + h + 1)
                if h:
                    ge(pe, S["pT_sb0"], HEADS * i + h)
                    ge(pe, S["pT_sb1"], HEADS * i + h)
                elif ffn:
                    ge(pe, S["x_ffn"], i)
                for t in range(TT):
                    last = pe.transpose(psP[:, t * 2 * P:t * 2 * P + P], Pr[:, h % 2, t * 2 * P + P:(t + 1) * 2 * P], ident[:, :])
                    if t:
                        last = pe.transpose(psP[:, (t - 1) * 2 * P + P:t * 2 * P], Pr[:, h % 2, t * 2 * P:t * 2 * P + P], ident[:, :])
                last.then_inc(S["pT_ps"], 1)

            def values(i, h):
                pair, rows = h // 2, slice(h % 2 * DH, (h % 2 + 1) * DH)
                ge(pe, S["pT_sb0"], HEADS * i + h + 1)
                ge(pe, S["pT_sb1"], HEADS * i + h + 1)
                if h == 0:
                    ge(pe, S["proj_sb"], 3 * TT * (i + 1))
                if h % 2 == 0 and pair >= 2:
                    ge(pe, S["o_sb"], HEADS // 2 * i + pair - 1)
                for t in range(TT):
                    w = 2 * P if t < TT - 1 else P
                    last = pe.matmul(ring[pair % 2][rows, t * P:t * P + w], V[:, t, h * DH:(h + 1) * DH], PT[:, h % 2, t * 2 * P:t * 2 * P + w],
                                     start=(t == 0), stop=(t == TT - 1), skip_group_check=True)
                if h % 2:
                    last.then_inc(S["o_ps"], 1)

            def output(i):
                ge(pe, S["o_sb"], HEADS // 2 * (i + 1))
                for c in range(KD):
                    for a in range(INNER // P):
                        last = pe.matmul(psP[:, c * N:(c + 1) * N], wo[:, a, c * P:(c + 1) * P], OT[:, a, :], start=(a == 0), stop=(a == INNER // P - 1))
                last.then_inc(S["wo_ps"], 1)

            def step(i, attn, ffn):
                if attn:
                    project(i, 0)
                if ffn:
                    mean(i)
                if attn:
                    project(i, 1)
                    transposes(i, 0)
                    project(i, 2)
                if ffn:
                    variance(i)
                if attn:
                    transposes(i, 1)
                    project(i, 3)
                    transposes(i, 2)
                if ffn:
                    hidden(i, 0, attn)
                if attn:
                    transposes(i, 3)
                if ffn:
                    for j in range(1, HT):
                        hidden(i, j, attn)
                    down(i)
                if attn:
                    for h in range(HEADS + 3):
                        if h < HEADS:
                            scores(i, h)
                        if 2 <= h < HEADS + 2:
                            p_transposes(i, h - 2, ffn)
                        if h >= 3:
                            values(i, h - 3)
                    output(i)
            pe.wait_ge(S["w1_lo"], 1)
            pipeline(pe, step)


def combine_block(nc, io, xT, ident):
    ctx = ExitStack()
    with ctx:
        def sb(name, shape, dt=F32):
            return ctx.enter_context(nc.sbuf_tensor("c_" + name, shape, dt))

        x_in = sb("x", [P, 2, TT, D])
        s_in = sb("s", [P, 2, TT, D])
        E = sb("e", [P, 2, TT, D])
        O = sb("o", [P, 2, TT, D])
        yT = sb("yT", [P, 2, KD, N])
        ps = [ctx.enter_context(nc.psum_tensor(f"c_ps{j}", [P, TT, D], F32)) for j in range(2)]
        names = "yT x_in0 x_in1 tr silu prod sum out0 out1".split()
        S = {n: ctx.enter_context(nc.semaphore("c_" + n)) for n in names}
        start_at_zero(nc, S.values())
        block = ctx.enter_context(nc.Block())
        x_v = io["x"].rearrange("b (t p) d -> b p t d", p=P)
        s_v = io["s"].rearrange("b (t p) d -> b p t d", p=P)
        o_v = io["out"].rearrange("b (t p) d -> b p t d", p=P)

        def pairs(e, body):
            for par in range(2):
                body(0, par)
            with e.Fori(1, B // 2) as i:
                for par in range(2):
                    body(i, par)

        @block.sync
        def _(sp):
            def load(i, par):
                b = 2 * i + par
                ge(sp, S["sum"], b - 1)
                for dst, src in ((x_in, x_v), (s_in, s_v)):
                    sp.dma_start(at(dst, par), src[bass.ds(b, 1)].rearrange("b p t d -> p b t d")).then_inc(S[f"x_in{par}"], 16)
            pairs(sp, load)

        @block.gpsimd
        def _(pool):
            def body(i, par):
                b = 2 * i + par
                ge(pool, S["silu"], b + 1)
                ge(pool, S[f"x_in{par}"], 32 * (i + 1))
                pool.tensor_tensor(E[:, par], E[:, par], s_in[:, par], ALU.mult).then_inc(S["prod"], 1)
            pairs(pool, body)

        @block.scalar
        def _(act):
            def store(i, par):
                b = 2 * i + par
                ge(act, S["sum"], b + 1)
                act.dma_start(o_v[bass.ds(b, 1)].rearrange("b p t d -> p b t d"), at(O, par)).then_inc(S[f"out{par}"], 16)

            def silu(i, par):
                b = 2 * i + par
                ge(act, S["tr"], b + 1)
                ge(act, S["sum"], b - 1)
                act.activation(E[:, par], ps[par][:, :, :], ACT.Silu).then_inc(S["silu"], 1)

            for par in range(2):
                silu(0, par)
            with act.Fori(1, B // 2) as i:
                for par in range(2):
                    store(i - 1, par)
                    silu(i, par)
            for par in range(2):
                store(B // 2 - 1, par)
            act.wait_ge(S["out0"], 16 * (B // 2))
            act.wait_ge(S["out1"], 16 * (B // 2))

        @block.vector
        def _(dve):
            def copy(i, par):
                b = 2 * i + par
                ge(dve, S["tr"], b - 1)
                dve.tensor_scalar(yT[:, par], x_view(xT, b), 1.0, None, ALU.mult).then_inc(S["yT"], 1)

            def add_x(i, par):
                b = 2 * i + par
                ge(dve, S["prod"], b + 1)
                ge(dve, S[f"out{par}"], 16 * i)
                dve.tensor_tensor(O[:, par], E[:, par], x_in[:, par], ALU.add).then_inc(S["sum"], 1)

            copy(0, 0)
            copy(0, 1)
            add_x(0, 0)
            add_x(0, 1)
            with dve.Fori(1, B // 2) as i:
                copy(i, 0)
                copy(i, 1)
                add_x(i, 0)
                add_x(i, 1)

        @block.tensor
        def _(pe):
            def body(i, par):
                b = 2 * i + par
                ge(pe, S["yT"], b + 1)
                ge(pe, S["silu"], b - 1)
                for t in range(TT):
                    for k in range(KD):
                        last = pe.transpose(ps[par][:, t, k * P:(k + 1) * P], yT[:, par, k, t * P:(t + 1) * P], ident[:, :])
                last.then_inc(S["tr"], 1)
            pairs(pe, body)


def build(nc, io):
    with ExitStack() as ctx:
        xT = ctx.enter_context(nc.sbuf_tensor("xT", [P, B, XW], F32))
        ident = ctx.enter_context(nc.sbuf_tensor("ident", [P, P], F32))
        identb = ctx.enter_context(nc.sbuf_tensor("identb", [P, P], BF16))
        ones = ctx.enter_context(nc.sbuf_tensor("ones", [P, P], F32))
        epsc = ctx.enter_context(nc.sbuf_tensor("eps", [P, 1], F32))
        id_in = ctx.enter_context(nc.semaphore("id_in"))
        id_bf = ctx.enter_context(nc.semaphore("id_bf"))
        with nc.Block() as block:
            @block.sync
            def _(sp):
                sp.dma_start(ident[:, :], io["ident"]).then_inc(id_in, 16)
                sp.wait_ge(id_in, 16)

            @block.vector
            def _(dve):
                dve.memset(ones[:, :], 1.0 / D)
                dve.memset(epsc[:, :], EPS)
                dve.memset(xT[:, :, X1 - 1], 0.0)
                dve.wait_ge(id_in, 16)
                dve.tensor_copy(identb[:, :], ident[:, :]).then_inc(id_bf, 1)
                dve.wait_ge(id_bf, 1)
        attention_block(nc, io, xT, ident, identb, epsc)
        for layer in range(LAYERS):
            layer_block(nc, io, layer, xT, ident, identb, ones, epsc)
        combine_block(nc, io, xT, ident)


def shape_constants():
    f = np.float32
    i = np.arange(D // 2, dtype=f)
    theta = np.power(f(10000.0), f(-2.0) * (i - f(1.0)) / f(D)).astype(f)
    pos = np.arange(N, dtype=f)
    ang = pos[:, None] * theta[None, :]
    c, s = np.cos(ang).astype(f), np.sin(ang).astype(f)
    acos = np.repeat(c, 2, axis=1)
    asin = np.stack((s, -s), axis=-1).reshape(N, D)
    half = np.arange(0, DH, 2, dtype=f)
    inv = (f(1.0) / np.power(f(10000.0), half / f(DH))).astype(f)
    fr = pos[:, None] * inv[None, :]
    fr = np.concatenate([fr, fr], axis=-1)
    base = (half + f(0.4 * DH)) / f(1.4 * DH)
    power = (pos - f(N // 2)) / f(P // 2)
    xs = np.power(base[None, :], power[:, None]).astype(f)
    xs = np.concatenate([xs, xs], axis=-1)
    c, s = np.cos(fr).astype(f), np.sin(fr).astype(f)
    sign = np.concatenate([-np.ones(DH // 2, f), np.ones(DH // 2, f)])
    fcos = np.stack([c * xs, c / xs], axis=1)
    fsin = np.stack([s * xs * sign, s / xs * sign], axis=1)

    def rows(a):
        return np.ascontiguousarray(a.reshape(TT, P, *a.shape[1:]).swapaxes(0, 1).astype(f))
    q, k = np.arange(P)[:, None], np.arange(P)[None, :]
    own = np.where(k <= q, f(0), f(-3e38))
    prev = np.where(k >= q, f(0), f(-3e38))
    amask = np.concatenate([np.zeros((P, N - P), f), own], axis=1)
    fmask = np.concatenate([prev, own], axis=1)
    return dict(acos=rows(acos), asin=rows(asin), fcos=rows(fcos), fsin=rows(fsin), amask=amask, fmask=fmask, ident=np.eye(P, dtype=f))


NAMES = dict(x="L0_attn_x", wq="L0_attn_w_q", wk="L0_attn_w_k", wv="L0_attn_w_v", wqkv="L0_ffn_wqkv", q_scale="L0_ffn_q_scale",
             k_scale="L0_ffn_k_scale", wo="L0_ffn_wo", ln_g="L0_ffn_ln_g", ln_b="L0_ffn_ln_b", w1="L0_ffn_w1", b1="L0_ffn_b1",
             w2="L0_ffn_w2", b2="L0_ffn_b2")


def kernel(**inputs):
    import ml_dtypes
    import concourse.bacc as _bacc
    from concourse.bass_utils import run_bass_kernel_spmd as _run

    nc = _bacc.Bacc("TRN2", target_bir_lowering=False, num_devices=1)
    arrays, io = {}, {}
    for short, name in NAMES.items():
        arrays[f"in_{short}"] = np.ascontiguousarray(inputs[name])
    for short, a in shape_constants().items():
        arrays[f"in_{short}"] = a.astype(ml_dtypes.bfloat16) if short.endswith("mask") else a
    for key, a in arrays.items():
        io[key[3:]] = nc.dram_tensor(key, a.shape, mybir.dt.from_np(a.dtype), kind="ExternalInput").ap()
    io["s"] = nc.dram_tensor("scratch_s", (B, N, D), F32, kind="Internal").ap()
    io["out"] = nc.dram_tensor("out_dram", (B, N, D), F32, kind="ExternalOutput").ap()
    build(nc, io)
    r = _run(nc, [arrays], core_ids=[0])
    return r.results[0]["out_dram"]
```

```python
from contextlib import ExitStack

import numpy as np

import concourse.bass as bass
from concourse import mybir

ALU = mybir.AluOpType
ACT = mybir.ActivationFunctionType
AX = mybir.AxisListType
F32 = mybir.dt.float32
F32R = mybir.dt.float32r
BF16 = mybir.dt.bfloat16

P = 128
B, N, D = 8, 512, 256
TT = N // P
KD = D // P
HEADS, DH = 8, 64
INNER = HEADS * DH
HID = int(D * 4 * 2 / 3)
HFULL = HID // P
HREM = HID - HFULL * P
HT = HFULL + 1
W1T = 2 * HFULL + 1
GATE0 = 64
LAYERS = 2
QK_SCALE = 8.0
EPS = 1e-5
XW = 2 * (N + 4)
X1 = N + 4
NLE = "natural_log_exp_and_others"


def ge(engine, sem, value):
    if not isinstance(value, int) or value > 0:
        engine.wait_ge(sem, value)


def at(ap, i):
    return ap[:, bass.ds(i, 1)]


def x_view(xT, b):
    return xT[:, bass.ds(b, 1), 0:2 * X1].rearrange("p b (k c) -> p (b k) c", k=KD)[:, :, 0:N]


def h_view(xT, b):
    return xT[:, bass.ds(b, 1), 0:2 * (X1 - 1)].rearrange("p b (k c) -> p (b k) c", k=KD)[:, :, 0:N]


def along(ap, n):
    return ap.unsqueeze(2).broadcast_to([ap.shape[0], ap.shape[1], n])


class Weights:

    def __init__(self, ctx, nc, io):
        def sb(name, shape, dt=F32):
            return ctx.enter_context(nc.sbuf_tensor("w_" + name, shape, dt))
        self.io = io
        self.wq_hi = sb("wq_hi", [P, KD, 3 * INNER], F32R)
        self.wq_lo = sb("wq_lo", [P, KD, 3 * INNER], F32R)
        self.w1_hi = sb("w1_hi", [P, KD, W1T * P], F32R)
        self.w1_lo = sb("w1_lo", [P, KD, W1T * P], F32R)
        self.wo = sb("wo", [P, INNER // P, D])
        self.w2 = sb("w2", [P, HT, D])
        self.gcol = sb("g", [P, LAYERS, KD])
        self.bcol = sb("b", [P, LAYERS, KD])
        self.b1raw = sb("b1raw", [P, LAYERS, W1T])
        self.b1col = sb("b1", [P, LAYERS, W1T])
        self.b2col = sb("b2", [P, LAYERS, KD])
        self.cosT = sb("cos", [P, LAYERS, TT, 2, DH])
        self.sinT = sb("sin", [P, LAYERS, TT, 2, DH])
        self.maskT = sb("mask", [P, 2 * P], BF16)
        names = ("wq_in0 wq_in1 w1_in small tabs w1pad w2pad wo_in w2_in b1pad wq_hi wq_lo w1_hi w1_lo b1_ps b1_sb").split()
        self.S = {n: ctx.enter_context(nc.semaphore("w_" + n)) for n in names}

    def load_wqkv(self, sp, layer, stage):
        for k in range(KD):
            sp.dma_start(stage[:, k, :], self.io["wqkv"][layer, k * P:(k + 1) * P]).then_inc(self.S[f"wq_in{k}"], 16)

    def load_w1(self, sp, layer, stage):
        w1 = self.io["w1"][layer].rearrange("(k p) n -> p k n", p=P)
        sp.wait_ge(self.S["w1pad"], layer + 1)
        for s in range(2):
            sp.dma_start(stage[:, :, s * HFULL * P:(s + 1) * HFULL * P], w1[:, :, s * HID:s * HID + HFULL * P]).then_inc(self.S["w1_in"], 16)
            c = 2 * HFULL * P + s * GATE0
            sp.dma_start(stage[:, :, c:c + HREM], w1[:, :, s * HID + HFULL * P:(s + 1) * HID]).then_inc(self.S["w1_in"], 16)

    def load_wo(self, sp, layer):
        sp.dma_start(self.wo[:, :, :], self.io["wo"][layer].rearrange("(k p) n -> p k n", p=P)).then_inc(self.S["wo_in"], 16)

    def load_w2(self, sp, layer):
        sp.dma_start(self.w2[:, 0:HFULL, :], self.io["w2"][layer, 0:HFULL * P].rearrange("(k p) n -> p k n", p=P)).then_inc(self.S["w2_in"], 16)
        sp.dma_start(self.w2[0:HREM, HFULL, :], self.io["w2"][layer, HFULL * P:HID]).then_inc(self.S["w2_in"], 16)

    def load_small(self, sp, scl, scls):
        io, small = self.io, self.S["small"]
        sp.dma_start(self.maskT[:, :], io["fmask"]).then_inc(small, 16)
        sp.wait_ge(self.S["b1pad"], 1)
        for l in range(LAYERS):
            sp.dma_start(self.cosT[:, l], io["fcos"]).then_inc(small, 16)
            sp.dma_start(self.sinT[:, l], io["fsin"]).then_inc(small, 16)
            for j, n in enumerate(("q_scale", "k_scale")):
                row = io[n][l:l + 1, :]
                sp.dma_start(scl[:, l, j, :], row.broadcast_to([P, DH])).then_inc(small, 16)
                for s in range(2):
                    sp.dma_start(scls[:, l, j, s * DH // 2:(s + 1) * DH // 2],
                                 row[:, (1 - s) * DH // 2:(2 - s) * DH // 2].broadcast_to([P, DH // 2])).then_inc(small, 16)
            for dst, n in ((self.gcol, "ln_g"), (self.bcol, "ln_b"), (self.b2col, "b2")):
                sp.dma_start(dst[:, l, :], io[n][l].rearrange("(k p) -> p k", p=P), allow_slow_non_contiguous=True).then_inc(small, 16)
            b1 = io["b1"][l]
            for s in range(2):
                full = b1[s * HID:s * HID + HFULL * P].rearrange("(j p) -> p j", p=P)
                sp.dma_start(self.b1raw[:, l, s * HFULL:(s + 1) * HFULL], full, allow_slow_non_contiguous=True).then_inc(small, 16)
                rest = b1[s * HID + HFULL * P:(s + 1) * HID].rearrange("(p j) -> p j", j=1)
                sp.dma_start(self.b1raw[s * GATE0:s * GATE0 + HREM, l, 2 * HFULL:W1T], rest, allow_slow_non_contiguous=True).then_inc(small, 16)

    SMALL = 16 * (1 + LAYERS * (2 + 2 * 3 + 3 + 4))

    def high_wqkv(self, act, layer, stage, k):
        act.wait_ge(self.S[f"wq_in{k}"], 16 * (layer + 1))
        act.activation(self.wq_hi[:, k, :], stage[:, k, :], ACT.Copy).then_inc(self.S["wq_hi"], 1)

    def high_w1(self, act, layer, stage, k):
        act.wait_ge(self.S["w1_in"], 64 * (layer + 1))
        act.wait_ge(self.S["small"], self.SMALL)
        act.activation(self.w1_hi[:, k, :], stage[:, k, :], ACT.Copy, scale=self.gcol[:, layer, k:k + 1]).then_inc(self.S["w1_hi"], 1)

    def low_wqkv(self, dve, layer, stage, k):
        dve.wait_ge(self.S["wq_hi"], KD * layer + k + 1)
        dve.tensor_tensor(self.wq_lo[:, k, :], stage[:, k, :], self.wq_hi[:, k, :].bitcast(F32), ALU.subtract).then_inc(self.S["wq_lo"], 1)

    def low_w1(self, dve, layer, stage, k):
        dve.wait_ge(self.S["w1_hi"], KD * layer + k + 1)
        dve.scalar_tensor_tensor(out=self.w1_lo[:, k, :], in0=stage[:, k, :], scalar=self.gcol[:, layer, k:k + 1],
                                 in1=self.w1_hi[:, k, :].bitcast(F32), op0=ALU.mult, op1=ALU.subtract).then_inc(self.S["w1_lo"], 1)

    def b1_products(self, pe, layer, stage, ps):
        pe.wait_ge(self.S["w1_in"], 64 * (layer + 1))
        pe.wait_ge(self.S["small"], self.SMALL)
        for j in range(W1T):
            for k in range(KD):
                last = pe.matmul(ps[:, j:j + 1], stage[:, k, j * P:(j + 1) * P], self.bcol[:, layer, k:k + 1], start=(k == 0), stop=(k == KD - 1))
        last.then_inc(self.S["b1_ps"], 1)

    def b1_columns(self, dve, layer, ps):
        dve.wait_ge(self.S["b1_ps"], layer + 1)
        dve.tensor_tensor(self.b1col[:, layer, :], ps[:, 0:W1T], self.b1raw[:, layer, :], ALU.add).then_inc(self.S["b1_sb"], 1)


def attention_block(nc, outer, io, W, xT, ident, identb, ones, epsc):
    ctx = ExitStack()
    with ctx:
        def sb(name, shape, dt=F32):
            return ctx.enter_context(nc.sbuf_tensor(name, shape, dt))

        def pb(name):
            return ctx.enter_context(nc.psum_tensor(name, [P, 512], F32))

        def sem(name):
            return outer.enter_context(nc.semaphore("a_" + name))

        QKW = 2 * D
        stage_q = sb("aw_stage", [P, KD, 3 * INNER])
        wraw = stage_q[:, 0, :].rearrange("p (k n) -> p k n", k=3 * KD)
        whi = sb("aw_hi", [P, KD, 3 * D], F32R)
        wlo = sb("aw_lo", [P, KD, 3 * D], F32R)
        tables = sb("a_tables", [P, 3 * TT * D])
        cosT, sinT, x_in = (tables[:, j * TT * D:(j + 1) * TT * D].rearrange("p (t d) -> p t d", t=TT) for j in range(3))
        stage1 = tables[:, 0:KD * W1T * P].rearrange("p (k n) -> p k n", k=KD)
        scl = sb("a_scl", [P, LAYERS, 2, DH])
        scls = sb("a_scls", [P, LAYERS, 2, DH])
        maskT = sb("a_mask", [P, N], BF16)
        stats = sb("a_stats", [P, TT, 6])
        mv = sb("a_mv", [P, TT, 2])
        spare = sb("a_spare", [P, 1])
        lnv = sb("a_lnv", [P, TT])
        rstd = sb("a_rstd", [P, TT])
        xn = sb("a_xn", [P, TT, D])
        hhi = sb("a_hhi", [P, KD, N], F32R)
        hlo = sb("a_hlo", [P, KD, N], F32R)
        raw = sb("a_raw", [P, 2, QKW])
        t2 = sb("a_t2", [P, 2, QKW])
        rot = sb("a_rot", [P, TT, QKW])
        V = sb("a_v", [P, TT, D])
        QK = sb("a_qk", [P, 2 * KD, N])
        Pr = sb("a_p", [P, TT, N])
        PT = sb("a_pt", [P, TT, N])
        mx = sb("a_mx", [P, TT])
        nb = sb("a_nb", [P, TT])
        sums = sb("a_sums", [P, TT])
        rinv = sb("a_rinv", [P, TT])
        O = sb("a_o", [P, TT, D])

        ring = [pb("a_ring0"), pb("a_ring1")]
        psT = pb("a_psT")
        psS = [pb("a_psS0"), pb("a_psS1")]
        psP = [pb("a_psP0"), pb("a_psP1")]
        psO = pb("a_psO")
        w_bank = (ring[0], ring[1], psT)
        qkT_bank = (psT, psP[0])

        names = ("id_in id_bf consts w_in c_in w_tr w_hi w_lo x_in0 bn agg lnv rstd xn xT_ps xT_hi xT_sb xT_lo "
                 "proj_ps proj_sb t2_done t1_done rot_done qkT_ps qkT_sb s_ps m_red m_bias exp_done "
                 "rinv_done pT_ps pT_sb o_ps o_sb out_dma").split()
        S = {n: sem(n) for n in names}
        block = ctx.enter_context(nc.Block())
        x_v = io["x"].rearrange("b (t p) d -> b p t d", p=P)
        s_v = io["s"].rearrange("b (t p) d -> b p t d", p=P)
        scale = 1.0 / np.sqrt(D)
        TILES = 2 * TT

        def pipeline(e, step):
            step(0, True, False)
            with e.Fori(1, B - 1) as i:
                step(i, True, True)
            step(B - 1, True, True)
            step(B, False, True)

        def has_next(i, front):
            return front and not (isinstance(i, int) and i == B - 1)

        WS = W.S

        @block.sync
        def _(sp):
            sp.dma_start(x_in[:, :, :], x_v[0]).then_inc(S["x_in0"], 16)
            for j, w in enumerate(("wq", "wk", "wv")):
                if j == 0:
                    sp.dma_start(ident[:, :], io["ident"]).then_inc(S["id_in"], 16)
                sp.dma_start(wraw[:, KD * j:KD * (j + 1), :], io[w].rearrange("(k p) d -> p k d", p=P)).then_inc(S["w_in"], 16)
            sp.dma_start(cosT[:, :, :], io["acos"]).then_inc(S["c_in"], 16)
            sp.dma_start(sinT[:, :, :], io["asin"]).then_inc(S["c_in"], 16)
            sp.dma_start(maskT[:, :], io["amask"]).then_inc(S["c_in"], 16)
            W.load_small(sp, scl, scls)
            W.load_wo(sp, 0)
            sp.wait_ge(WS["w2pad"], 1)
            W.load_w2(sp, 0)
            sp.wait_ge(S["w_tr"], 3)
            W.load_wqkv(sp, 0, stage_q)

            def step(i, front, back):
                if has_next(i, front):
                    ge(sp, S["xn"], i + 1)
                    sp.dma_start(at(x_in[:, :, :].unsqueeze(1), 0), x_v[bass.ds(i + 1, 1)].rearrange("b p t d -> p b t d")).then_inc(S["x_in0"], 16)
                if back:
                    ge(sp, S["o_sb"], TT * i)
                    sp.dma_start(s_v[bass.ds(i - 1, 1)].rearrange("b p t d -> p b t d"), O[:, :, :].unsqueeze(1)).then_inc(S["out_dma"], 16)
                if isinstance(i, int) and i == B - 1:
                    W.load_w1(sp, 0, stage1)
            pipeline(sp, step)
            sp.wait_ge(S["out_dma"], 16 * (B + 1))

        @block.gpsimd
        def _(pool):
            pool.wait_ge(S["c_in"], 48)
            pool.wait_ge(WS["small"], W.SMALL)
            for l in range(LAYERS):
                for tab, s in ((W.cosT, scl), (W.sinT, scls)):
                    rows = tab[:, l].rearrange("p t j d -> p t (j d)")
                    pool.tensor_tensor(rows, rows, s[:, l].rearrange("p j d -> p (j d)").unsqueeze(1).broadcast_to([P, TT, 2 * DH]), ALU.mult).then_inc(WS["tabs"], 1)

            def step(i, front, back):
                if front:
                    for t in range(TT):
                        ge(pool, S["proj_sb"], TILES * i + t + 1)
                        ge(pool, S["rot_done"], TT * i + t - 1)
                        src = raw[:, t % 2, :].rearrange("p (q c s) -> p q c s", q=2, s=2)
                        dst = t2[:, t % 2, :].rearrange("p (q c s) -> p q c s", q=2, s=2)
                        tab = sinT[:, t, :].rearrange("p (c s) -> p c s", s=2).unsqueeze(1).broadcast_to([P, 2, D // 2, 2])
                        pool.tensor_tensor(dst[:, :, :, 0], src[:, :, :, 1], tab[:, :, :, 0], ALU.mult).then_inc(S["t2_done"], 1)
                        pool.tensor_tensor(dst[:, :, :, 1], src[:, :, :, 0], tab[:, :, :, 1], ALU.mult).then_inc(S["t2_done"], 1)
            pipeline(pool, step)

        @block.scalar
        def _(act):
            act.preload_act_table_set(NLE)
            def proj(i, t):
                n = TILES * i + t
                ge(act, S["proj_ps"], n + 1)
                if t < TT:
                    ge(act, S["rot_done"], TT * i + t - 1)
                    act.activation(raw[:, t % 2, :], ring[t % 2][:, :], ACT.Copy).then_inc(S["proj_sb"], 1)
                else:
                    act.activation(V[:, t - TT, :], ring[t % 2][:, 0:D], ACT.Copy).then_inc(S["proj_sb"], 1)

            def norm(i):
                ge(act, S["agg"], i + 1)
                act.activation(lnv[:, :], mv[:, :, 1], ACT.Ln, bias=epsc[:, 0:1]).then_inc(S["lnv"], 1)
                ge(act, S["lnv"], i + 1)
                act.activation(rstd[:, :], lnv[:, :], ACT.Exp, scale=-0.5).then_inc(S["rstd"], 1)

            def high(i):
                ge(act, S["xT_ps"], i + 1)
                for k in (1, 0):
                    act.activation(hhi[:, k, :], ring[k][:, :], ACT.Copy).then_inc(S["xT_hi"], 1)
                ge(act, S["xT_lo"], KD * i + 1)
                act.activation(xT[:, bass.ds(i, 1), X1:X1 + N], ring[1][:, :].unsqueeze(1), ACT.Copy).then_inc(S["xT_sb"], 1)

            def softmax(i, t):
                w = (t + 1) * P
                ge(act, S["m_bias"], TT * (i - 1) + t + 1)
                act.activation(Pr[:, t, 0:w], psS[t % 2][:, 0:w], ACT.Exp, bias=nb[:, t:t + 1], scale=scale,
                               accum_out=sums[:, t:t + 1]).then_inc(S["exp_done"], 1)

            def out(i, t):
                ge(act, S["o_ps"], TT * (i - 1) + t + 1)
                ge(act, S["rinv_done"], TT * (i - 1) + t + 1)
                if t == 0:
                    ge(act, S["out_dma"], 16 * i)
                act.activation(O[:, t, :], psO[:, 0:D], ACT.Copy, scale=rinv[:, t:t + 1]).then_inc(S["o_sb"], 1)

            def qk_evac(i, t):
                ge(act, S["qkT_ps"], TT * i + t + 1)
                act.activation(QK[:, :, t * P:(t + 1) * P], qkT_bank[t % 2][:, :].rearrange("p (a c) -> p a c", c=P), ACT.Copy).then_inc(S["qkT_sb"], 1)

            def step(i, front, back):
                if front:
                    high(i)
                if back:
                    softmax(i, 0)
                    softmax(i, 1)
                if front:
                    proj(i, 0)
                if not front:
                    W.high_wqkv(act, 0, stage_q, 0)
                if back:
                    softmax(i, 2)
                    out(i, 0)
                if not front:
                    W.high_wqkv(act, 0, stage_q, 1)
                if front:
                    proj(i, 1)
                if back:
                    softmax(i, 3)
                    out(i, 1)
                if front:
                    proj(i, 2)
                if back:
                    out(i, 2)
                if front:
                    proj(i, 3)
                if back:
                    out(i, 3)
                if not front:
                    for k in range(KD):
                        W.high_w1(act, 0, stage1, k)
                if front:
                    qk_evac(i, 0)
                    qk_evac(i, 1)
                    proj(i, TT)
                    qk_evac(i, 2)
                    proj(i, TT + 1)
                    if has_next(i, front):
                        norm(i + 1)
                    qk_evac(i, 3)
                    proj(i, TT + 2)
                    proj(i, TT + 3)

            act.wait_ge(S["consts"], 1)
            norm(0)
            for j in range(3):
                act.wait_ge(S["w_tr"], j + 1)
                act.activation(whi[:, :, j * D:(j + 1) * D], w_bank[j][:, :].rearrange("p (k o) -> p k o", k=KD), ACT.Copy).then_inc(S["w_hi"], 1)
            pipeline(act, step)

        @block.vector
        def _(dve):
            dve.memset(epsc[:, :], EPS).then_inc(S["consts"], 1)
            dve.memset(ones[:, :], 1.0 / D)
            dve.memset(xT[:, :, X1 - 1], 0.0)
            dve.memset(W.b1raw[:, :, :], 0.0).then_inc(WS["b1pad"], 1)
            dve.memset(W.w2[:, HFULL, :], 0.0).then_inc(WS["w2pad"], 1)
            dve.memset(spare[:, :], 0.0).then_inc(S["out_dma"], 16)
            dve.wait_ge(S["c_in"], 48)

            def norm(i):
                ge(dve, S["x_in0"], 16 * (i + 1))
                for t in range(TT):
                    dve.bn_stats(stats[:, t, :], x_in[:, t, :]).then_inc(S["bn"], 1)
                ge(dve, S["bn"], TT * (i + 1))
                dve.memset(spare[:, :], 0.0)
                for t in range(TT):
                    last = dve.bn_aggr(mv[:, t, :], stats[:, t, :])
                last.then_inc(S["agg"], 1)
                ge(dve, S["rstd"], i + 1)
                for t in range(TT):
                    last = dve.tensor_scalar(xn[:, t, :], x_in[:, t, :], mv[:, t, 0:1], rstd[:, t:t + 1], ALU.subtract, ALU.mult)
                last.then_inc(S["xn"], 1)

            def low(i):
                ge(dve, S["xT_ps"], i + 1)
                for k in (1, 0):
                    ge(dve, S["xT_hi"], KD * i + KD - k)
                    dve.tensor_tensor(hlo[:, k, :], ring[k][:, :], hhi[:, k, :].bitcast(F32), ALU.subtract).then_inc(S["xT_lo"], 1)
                dve.tensor_copy(xT[:, bass.ds(i, 1), 0:N], ring[0][:, :].unsqueeze(1)).then_inc(S["xT_sb"], 1)

            def rotate(i, t):
                ge(dve, S["proj_sb"], TILES * i + t + 1)
                r = rot[:, t, :].rearrange("p (q d) -> p q d", q=2)
                tab = cosT[:, t, :].unsqueeze(1).broadcast_to([P, 2, D])
                dve.tensor_tensor(r, raw[:, t % 2, :].rearrange("p (q d) -> p q d", q=2), tab, ALU.mult).then_inc(S["t1_done"], 1)
                ge(dve, S["t1_done"], TT * i + t + 1)
                ge(dve, S["t2_done"], 2 * (TT * i + t + 1))
                dve.tensor_tensor(rot[:, t, :], rot[:, t, :], t2[:, t % 2, :], ALU.add).then_inc(S["rot_done"], 1)

            def maxima(i, t):
                n = TT * (i - 1) + t + 1
                ge(dve, S["s_ps"], n)
                dve.reduce_max(mx[:, t:t + 1], psS[t % 2][:, 0:(t + 1) * P], AX.X).then_inc(S["m_red"], 1)
                ge(dve, S["m_red"], n)
                dve.tensor_scalar(nb[:, t:t + 1], mx[:, t:t + 1], -scale, None, ALU.mult).then_inc(S["m_bias"], 1)

            def inverse(i, t):
                ge(dve, S["exp_done"], TT * (i - 1) + t + 1)
                dve.reciprocal(rinv[:, t:t + 1], sums[:, t:t + 1]).then_inc(S["rinv_done"], 1)

            def p_copy(i, t):
                w = (t + 1) * P
                ge(dve, S["pT_ps"], TT * (i - 1) + t + 1)
                dve.tensor_copy(PT[:, t, 0:w], psP[t % 2][:, 0:w]).then_inc(S["pT_sb"], 1)

            def step(i, front, back):
                if front:
                    low(i)
                else:
                    dve.wait_ge(S["rot_done"], TT * B)
                    dve.wait_ge(S["xn"], B)
                    dve.wait_ge(S["t2_done"], 2 * TT * B)
                    dve.memset(stage1[:, :, 2 * HFULL * P:], 0.0).then_inc(WS["w1pad"], 1)
                if back:
                    maxima(i, 0)
                    maxima(i, 1)
                    inverse(i, 0)
                    p_copy(i, 0)
                    inverse(i, 1)
                    maxima(i, 2)
                    p_copy(i, 1)
                if front:
                    rotate(i, 0)
                if back:
                    inverse(i, 2)
                    maxima(i, 3)
                    p_copy(i, 2)
                if front:
                    rotate(i, 1)
                if back:
                    inverse(i, 3)
                    p_copy(i, 3)
                if not front:
                    for k in range(KD):
                        W.low_wqkv(dve, 0, stage_q, k)
                    for k in range(KD):
                        W.low_w1(dve, 0, stage1, k)
                    W.b1_columns(dve, 0, psT)
                if front:
                    rotate(i, 2)
                    rotate(i, 3)
                    if has_next(i, front):
                        norm(i + 1)
            norm(0)
            dve.wait_ge(S["id_in"], 16)
            dve.tensor_copy(identb[:, :], ident[:, :]).then_inc(S["id_bf"], 1)
            for j in range(3):
                dve.wait_ge(S["w_hi"], j + 1)
                part = slice(j * D, (j + 1) * D)
                dve.tensor_tensor(wlo[:, :, part], w_bank[j][:, :].rearrange("p (k o) -> p k o", k=KD), whi[:, :, part].bitcast(F32), ALU.subtract).then_inc(S["w_lo"], 1)
            pipeline(dve, step)

        @block.tensor
        def _(pe):
            pe.wait_ge(S["id_in"], 16)
            pe.wait_ge(S["w_in"], 48)
            for j in range(3):
                for k in range(KD):
                    for o in range(KD):
                        last = pe.transpose(w_bank[j][:, k * D + o * P:k * D + (o + 1) * P],
                                            wraw[:, KD * j + o, k * P:(k + 1) * P], ident[:, :])
                last.then_inc(S["w_tr"], 1)
            pe.wait_ge(S["id_bf"], 1)
            pe.wait_ge(S["w_lo"], 3)

            def x_transposes(i):
                ge(pe, S["xn"], i + 1)
                ge(pe, S["proj_sb"], TILES * i)
                for k in range(KD):
                    for t in range(TT):
                        last = pe.transpose(ring[k][:, t * P:(t + 1) * P], xn[:, t, k * P:(k + 1) * P], ident[:, :])
                last.then_inc(S["xT_ps"], 1)

            def project(i, t):
                c0, w = (0, QKW) if t < TT else (QKW, D)
                tok = slice((t % TT) * P, (t % TT + 1) * P)
                if t < 2:
                    ge(pe, S["xT_lo"], KD * (i + 1))
                    ge(pe, S["xT_sb"], KD * (i + 1))
                else:
                    ge(pe, S["proj_sb"], TILES * i + t - 1)
                m = 0
                for k in range(KD):
                    for a, w_ in ((hhi, whi), (hhi, wlo), (hlo, whi)):
                        last = pe.matmul(ring[t % 2][:, 0:w], a[:, k, tok], w_[:, k, c0:c0 + w], start=(m == 0), stop=(m == 3 * KD - 1))
                        m += 1
                last.then_inc(S["proj_ps"], 1)

            def qk_transposes(i, t):
                ge(pe, S["rot_done"], TT * i + t + 1)
                if t >= 2:
                    ge(pe, S["qkT_sb"], TT * i + t - 1)
                for a in range(2 * KD):
                    last = pe.transpose(qkT_bank[t % 2][:, a * P:(a + 1) * P], rot[:, t, a * P:(a + 1) * P], ident[:, :])
                last.then_inc(S["qkT_ps"], 1)

            def scores(i, t):
                w = (t + 1) * P
                ge(pe, S["qkT_sb"], TT * i)
                if t >= 2:
                    ge(pe, S["exp_done"], TT * (i - 1) + t - 1)
                pe.matmul(psS[t % 2][:, 0:w], identb[:, :], maskT[:, N - w:N], start=True, stop=False)
                for k in range(KD):
                    last = pe.matmul(psS[t % 2][:, 0:w], QK[:, k, t * P:(t + 1) * P], QK[:, KD + k, 0:w], start=False, stop=(k == KD - 1))
                last.then_inc(S["s_ps"], 1)

            def p_transposes(i, t):
                ge(pe, S["exp_done"], TT * (i - 1) + t + 1)
                if t >= 2:
                    ge(pe, S["pT_sb"], TT * (i - 1) + t - 1)
                for k in range(t + 1):
                    last = pe.transpose(psP[t % 2][:, k * P:(k + 1) * P], Pr[:, t, k * P:(k + 1) * P], ident[:, :])
                last.then_inc(S["pT_ps"], 1)

            def values(i, t):
                ge(pe, S["pT_sb"], TT * (i - 1) + t + 1)
                ge(pe, S["proj_sb"], TILES * i)
                if t:
                    ge(pe, S["o_sb"], TT * (i - 1) + t)
                for k in range(t + 1):
                    last = pe.matmul(psO[:, 0:D], PT[:, t, k * P:(k + 1) * P], V[:, k, :], start=(k == 0), stop=(k == t))
                last.then_inc(S["o_ps"], 1)

            def step(i, front, back):
                if front:
                    x_transposes(i)
                if back:
                    scores(i, 0)
                    scores(i, 1)
                    p_transposes(i, 0)
                if front:
                    project(i, 0)
                if back:
                    scores(i, 2)
                    p_transposes(i, 1)
                    values(i, 0)
                if front:
                    project(i, 1)
                if back:
                    scores(i, 3)
                    p_transposes(i, 2)
                    values(i, 1)
                if front:
                    project(i, 2)
                if back:
                    p_transposes(i, 3)
                    values(i, 2)
                if front:
                    project(i, 3)
                if back:
                    values(i, 3)
                if not front:
                    W.b1_products(pe, 0, stage1, psT)
                if front:
                    qk_transposes(i, 0)
                    qk_transposes(i, 1)
                    project(i, TT)
                    qk_transposes(i, 2)
                    project(i, TT + 1)
                    qk_transposes(i, 3)
                    project(i, TT + 2)
                    project(i, TT + 3)
            pipeline(pe, step)


def layers_block(nc, outer, io, W, xT, ident, identb, ones, epsc):
    ctx, stack = ExitStack(), ExitStack()
    with ctx, stack:
        def sb(name, shape, dt=F32):
            return ctx.enter_context(nc.sbuf_tensor("l_" + name, shape, dt))

        def pb(name, n=1):
            return ctx.enter_context(nc.psum_tensor("l_" + name, [P, 512 * n], F32))

        def sem(name):
            return outer.enter_context(nc.semaphore("l_" + name))

        QKW = 2 * INNER
        wq_hi, wq_lo, w1_hi, w1_lo, wo, w2 = W.wq_hi, W.wq_lo, W.w1_hi, W.w1_lo, W.wo, W.w2
        b1col, b2col = W.b1col, W.b2col
        cosT, sinT, maskT = W.cosT, W.sinT, W.maskT
        att = sb("att", [P, 2, B * TT * D])

        def part(half, quarter, quarters=1):
            return att[:, half, quarter * 2 * QKW:(quarter + quarters) * 2 * QKW]
        raw = part(0, 0).rearrange("p (a c) -> p a c", a=2)
        Pr = raw
        tmp = part(0, 1).rearrange("p (a c) -> p a c", a=2)
        sq, t2 = tmp[:, 0, :], tmp[:, 1, :]
        OT = tmp[:, :, :].rearrange("p a (b c) -> p (a b) c", c=N)
        rot = part(1, 0, 2).rearrange("p (a c) -> p a c", a=TT)
        PT = rot
        ssq = sb("ssq", [P, TT, 2 * HEADS])
        lnq = sb("lnq", [P, TT, 2 * HEADS])
        rn = sb("rn", [P, TT, 2 * HEADS])
        sc8 = sb("sc8", [P, TT, HEADS])
        nsc8 = sb("nsc8", [P, TT, HEADS])
        hhi = sb("hhi", [P, KD, N], F32R)
        hlo = sb("hlo", [P, KD, N], F32R)
        ffn_buf = sb("ffn", [P, 6 + HT, N])
        FW = ffn_buf[:, 0:6, :]
        stage1 = FW[:, :, :].rearrange("p a b -> p (a b)")[:, 0:KD * W1T * P].rearrange("p (k n) -> p k n", k=KD)
        dF, sqF, G = FW[:, 0:2, :], FW[:, 2:4, :], FW[:, 4:6, :]
        fhi = sb("fhi", [P, KD, N], F32R)
        flo = sb("flo", [P, KD, N], F32R)
        rstdF = sb("rstdF", [P, N])
        U = ffn_buf[:, 6:6 + HT, :]
        QT = part(1, 2, 2).rearrange("p (a b c) -> p a b c", a=2, b=INNER // P)
        stage = QT[:, :, :, :].rearrange("p a b c -> p (a b c)")[:, 0:KD * 3 * INNER].rearrange("p (k n) -> p k n", k=KD)
        KT = part(0, 2).rearrange("p (b c) -> p b c", b=INNER // P)
        V = part(0, 3).rearrange("p (t c) -> p t c", t=TT)
        mx = sb("mx", [P, 2, TT])
        nb = sb("nb", [P, 2, TT])
        sums = sb("sums", [P, 2, TT])
        rinv = sb("rinv", [P, 2, TT])

        ring = [pb("ring0"), pb("ring1")]
        psS = pb("psS", 2)
        psP = pb("psP", 2)
        psF = pb("psF", 2)
        scores_of = (psS, psF)
        down_of = (psP[:, 0:N], psS[:, 0:N])
        hidden_of = ((psF[:, 0:N], psF[:, N:2 * N]), (ring[0][:, :], ring[1][:, :]))

        names = ("h_ready zeroed "
                 "h_hi h_lo proj_ps proj_sb sq_done ssq_done t1_done t2_done rot_done clamped lnq_done rn_done "
                 "k_scaled sc_done qT_ps qT_sb kT_ps kT_sb s_ps m_red m_bias exp_done rinv_done p_done pT_ps "
                 "pT_sb0 pT_sb1 o_ps o_sb wo_ps x_attn mean_ps d_done sqF_done var_ps lnF_done rstdF_done hn_done "
                 "f_hi f_lo w1_ps gelu_done u_done w2_ps x_ffn").split()
        S = {n: sem(n) for n in names}
        WS = W.S
        xs = att[:, :, :].rearrange("p j (b t d) -> p j b t d", b=B, t=TT)
        xs_in = [sem("xs_in0"), sem("xs_in1")]
        block = stack.enter_context(nc.Block())

        def heads_of(ap, n):
            return ap.rearrange("p (h d) -> p h d", h=n)

        def pipeline(e, step):
            step(0, 0, None)
            with e.Fori(1, B) as i:
                step(i, 0, 0)
            step(B, 1, 0)
            with e.Fori(B + 1, 2 * B) as i:
                step(i, 1, 1)
            step(2 * B, None, 1)

        @block.sync
        def _(sp):
            sp.wait_ge(S["s_ps"], HEADS * B)
            W.load_wqkv(sp, 1, stage)
            sp.wait_ge(S["wo_ps"], B)
            W.load_wo(sp, 1)
            W.load_w1(sp, 1, stage1)
            sp.wait_ge(S["w2_ps"], KD * B)
            W.load_w2(sp, 1)
            sp.wait_ge(S["wo_ps"], LAYERS * B)
            for half in range(2):
                few = slice(half * B // 2, (half + 1) * B // 2)
                for j, n in enumerate(("x", "s")):
                    sp.dma_start(xs[:, j, few], io[n][few].rearrange("b (t p) d -> p b t d", p=P)).then_inc(xs_in[half], 16)

        @block.gpsimd
        def _(pool):

            def rotate(i, t, l):
                ge(pool, S["proj_sb"], 3 * (TT * i + t) + 2)
                ge(pool, S["rot_done"], TT * i + t)
                for j in range(2):
                    src = raw[:, t % 2, j * INNER:(j + 1) * INNER].rearrange("p (h s d) -> p h s d", h=HEADS, s=2)
                    dst = t2[:, j * INNER:(j + 1) * INNER].rearrange("p (h s d) -> p h s d", h=HEADS, s=2)
                    tab = sinT[:, l, t, j, :].rearrange("p (s d) -> p s d", s=2)
                    for s in range(2):
                        pool.tensor_tensor(dst[:, :, s, :], src[:, :, 1 - s, :],
                                           tab[:, s, :].unsqueeze(1).broadcast_to([P, HEADS, DH // 2]), ALU.mult).then_inc(S["t2_done"], 1)

            def scale_k(i, t):
                n = TT * i + t + 1
                ge(pool, S["rot_done"], n)
                ge(pool, S["rn_done"], n)
                kr = heads_of(rot[:, t, INNER:QKW], HEADS)
                pool.tensor_tensor(kr, kr, along(rn[:, t, HEADS:2 * HEADS], DH), ALU.mult).then_inc(S["k_scaled"], 1)

            def step(i, la, lf):
                attn, ffn = la is not None, lf is not None
                turn = attn and ffn and la != lf
                def normalize():
                    ge(pool, S["rstdF_done"], i)
                    pool.tensor_tensor(dF, dF, rstdF[:, :].unsqueeze(1).broadcast_to([P, KD, N]), ALU.mult).then_inc(S["hn_done"], 1)

                if attn and la != lf:
                    ge(pool, WS["wq_lo"], KD * (la + 1))
                    pool.memset(QT[DH:P, 0, :, :], 0.0)
                    pool.memset(QT[0:DH, 1, :, :], 0.0).then_inc(S["zeroed"], 1)
                    pool.wait_ge(S["zeroed"], la + 1)
                if attn:
                    rotate(i, 0, la)
                    scale_k(i, 0)
                    rotate(i, 1, la)
                if attn and ffn:
                    normalize()
                if attn:
                    scale_k(i, 1)
                    rotate(i, 2, la)
                    scale_k(i, 2)
                    rotate(i, 3, la)
                    scale_k(i, 3)
                    for h in range(HEADS):
                        ge(pool, S["rinv_done"], HEADS * i + h + 1)
                        pr = Pr[:, h % 2, :].rearrange("p (t c) -> p t c", t=TT)
                        pool.tensor_tensor(pr[:, 0, P:2 * P], pr[:, 0, P:2 * P], rinv[:, h % 2, 0:1].broadcast_to([P, P]), ALU.mult)
                        pool.tensor_tensor(pr[:, 1:TT, :], pr[:, 1:TT, :], along(rinv[:, h % 2, 1:TT], 2 * P), ALU.mult).then_inc(S["p_done"], 1)
            pipeline(pool, step)

        @block.scalar
        def _(act):
            act.preload_act_table_set(NLE)

            def copies(i, t, after_q=None):
                for c in range(3):
                    n = 3 * (TT * i + t) + c
                    ge(act, S["proj_ps"], n + 1)
                    if c == 0 and t >= 2:
                        ge(act, S["rot_done"], TT * i + t - 1)
                    if c == 1 and after_q:
                        after_q()
                    dst = raw[:, t % 2, c * INNER:(c + 1) * INNER] if c < 2 else V[:, t, :]
                    act.activation(dst, ring[(t + c) % 2][:, :], ACT.Copy).then_inc(S["proj_sb"], 1)
                    if c == 1:
                        ge(act, S["proj_sb"], n + 1)
                        ge(act, S["ssq_done"], TT * i + t)
                        act.activation(sq, raw[:, t % 2, :], ACT.Square).then_inc(S["sq_done"], 1)
                ge(act, S["clamped"], TT * i + t + 1)
                act.activation(lnq[:, t, :], ssq[:, t, :], ACT.Ln).then_inc(S["lnq_done"], 1)
                ge(act, S["lnq_done"], TT * i + t + 1)
                act.activation(rn[:, t, :], lnq[:, t, :], ACT.Exp, scale=-0.5).then_inc(S["rn_done"], 1)

            def high(b, n):
                ge(act, S["proj_ps"], 3 * TT * (n - 1))
                act.activation(hhi[:, :, :], h_view(xT, b), ACT.Copy).then_inc(S["h_hi"], 1)

            def q_evac(i, t):
                ge(act, S["qT_ps"], TT * i + t + 1)
                for par in range(2):
                    rows = slice(par * DH, (par + 1) * DH)
                    last = act.activation(QT[rows, par, :, t * P:(t + 1) * P], psS[rows, 0:512].rearrange("p (a c) -> p a c", c=P), ACT.Copy)
                last.then_inc(S["qT_sb"], 1)

            def gelu(i, j, l):
                u = i - 1
                ge(act, S["w1_ps"], HT * u + j + 1)
                if j >= 2:
                    ge(act, S["u_done"], HT * u + j - 1)
                gate = hidden_of[j % 2][0]
                if j < HFULL:
                    act.activation(G[:, j % 2, :], gate, ACT.Gelu, bias=b1col[:, l, HFULL + j:HFULL + j + 1]).then_inc(S["gelu_done"], 1)
                else:
                    act.activation(G[0:HREM, j % 2, :], gate[GATE0:GATE0 + HREM, :], ACT.Gelu,
                                   bias=b1col[GATE0:GATE0 + HREM, l, 2 * HFULL:W1T]).then_inc(S["gelu_done"], 1)

            def p_evac(i, h):
                ge(act, S["pT_ps"], HEADS * i + h + 1)
                act.activation(PT[:, h % 2, 0:512], psP[:, 0:512], ACT.Copy).then_inc(S["pT_sb0"], 1)

            def softmax(i, h):
                ge(act, S["m_bias"], HEADS * i + h + 1)
                ge(act, S["pT_ps"], HEADS * i + h - 1)
                ps = scores_of[h % 2]
                for t in range(TT):
                    c0 = P if t == 0 else 0
                    last = act.activation(Pr[:, h % 2, t * 2 * P + c0:(t + 1) * 2 * P], ps[:, t * 2 * P + c0:(t + 1) * 2 * P], ACT.Exp,
                                          bias=nb[:, h % 2, t:t + 1], scale=sc8[:, t, h:h + 1], accum_out=sums[:, h % 2, t:t + 1])
                last.then_inc(S["exp_done"], 1)

            def step(i, la, lf):
                attn, ffn = la is not None, lf is not None
                turn = attn and ffn and la != lf
                def square():
                    ge(act, S["d_done"], i)
                    act.activation(sqF[:, :, :], dF, ACT.Square).then_inc(S["sqF_done"], 1)

                def inverse_deviation():
                    ge(act, S["var_ps"], i)
                    act.activation(rstdF[:, :], psF[:, N:2 * N], ACT.Ln, bias=epsc[:, 0:1]).then_inc(S["lnF_done"], 1)
                    ge(act, S["lnF_done"], i)
                    act.activation(rstdF[:, :], rstdF[:, :], ACT.Exp, scale=-0.5).then_inc(S["rstdF_done"], 1)

                if not attn:
                    square()
                    inverse_deviation()
                if turn:
                    act.wait_ge(S["proj_ps"], 3 * TT * B)
                    for k in range(KD):
                        W.high_wqkv(act, 1, stage, k)
                if attn:
                    copies(i, 0)
                    copies(i, 1, square if ffn else None)
                if attn and ffn:
                    inverse_deviation()
                if attn:
                    copies(i, 2, lambda: q_evac(i, 0))
                if attn:
                    q_evac(i, 1)
                    copies(i, 3)
                    q_evac(i, 2)
                if ffn:
                    gelu(i, 0, lf)
                    gelu(i, 1, lf)
                if attn:
                    q_evac(i, 3)
                if ffn:
                    for j in range(2, HT):
                        gelu(i, j, lf)
                if attn:
                    act.preload_act_table_set(NLE)
                    high((i + 1) % B, i + 2)
                    for h in range(HEADS + 3):
                        if 2 <= h < HEADS + 2:
                            p_evac(i, h - 2)
                        if h < HEADS:
                            softmax(i, h)
                        if turn and 4 <= h < 4 + KD:
                            act.wait_ge(S["w1_ps"], HT * B)
                            W.high_w1(act, 1, stage1, h - 4)
                        if h >= 3 and h % 2 == 0:
                            pair = (h - 3) // 2
                            ge(act, S["o_ps"], HEADS // 2 * i + pair + 1)
                            act.activation(OT[:, pair, :], ring[pair % 2][:, :], ACT.Copy).then_inc(S["o_sb"], 1)
            high(0, 1)
            pipeline(act, step)

        @block.vector
        def _(dve):
            dve.memset(U[:, HFULL, :], 0.0)

            def rotate(i, t, l, between=None):
                n = TT * i + t
                ge(dve, S["sq_done"], n + 1)
                dve.tensor_reduce(ssq[:, t, :], sq.rearrange("p (h d) -> p h d", d=DH), AX.X, ALU.add).then_inc(S["ssq_done"], 1)
                ge(dve, S["ssq_done"], n + 1)
                dve.tensor_scalar(ssq[:, t, :], ssq[:, t, :], 1e-24, None, ALU.max).then_inc(S["clamped"], 1)
                for j in range(2):
                    last = dve.tensor_tensor(heads_of(rot[:, t, j * INNER:(j + 1) * INNER], HEADS),
                                             heads_of(raw[:, t % 2, j * INNER:(j + 1) * INNER], HEADS),
                                             cosT[:, l, t, j, :].unsqueeze(1).broadcast_to([P, HEADS, DH]), ALU.mult)
                last.then_inc(S["t1_done"], 1)
                if between:
                    between()
                ge(dve, S["t1_done"], n + 1)
                ge(dve, S["t2_done"], 4 * (n + 1))
                dve.tensor_tensor(rot[:, t, :], rot[:, t, :], t2, ALU.add).then_inc(S["rot_done"], 1)

            def gated(i, j, l):
                u = i - 1
                ge(dve, S["gelu_done"], HT * u + j + 1)
                gate, value = hidden_of[j % 2]
                if j < HFULL:
                    dve.scalar_tensor_tensor(out=U[:, j, :], in0=value, scalar=b1col[:, l, j:j + 1], in1=G[:, j % 2, :],
                                             op0=ALU.add, op1=ALU.mult).then_inc(S["u_done"], 1)
                else:
                    dve.scalar_tensor_tensor(out=U[0:HREM, j, :], in0=gate[0:HREM, :], scalar=b1col[0:HREM, l, 2 * HFULL:W1T],
                                             in1=G[0:HREM, j % 2, :], op0=ALU.add, op1=ALU.mult).then_inc(S["u_done"], 1)

            def low(b, n):
                ge(dve, S["h_hi"], n)
                dve.tensor_tensor(hlo[:, :, :], h_view(xT, b), hhi[:, :, :].bitcast(F32), ALU.subtract).then_inc(S["h_lo"], 1)

            def add_ffn(i, c, l):
                ge(dve, S["w2_ps"], KD * (i - 1) + c + 1)
                xk = xT[:, bass.ds(i - 1 - B * l, 1), c * X1:c * X1 + N]
                dve.scalar_tensor_tensor(out=xk, in0=down_of[c].unsqueeze(1), scalar=b2col[:, l, c:c + 1], in1=xk,
                                         op0=ALU.add, op1=ALU.add).then_inc(S["x_ffn"], 1)

            def k_evac(i, t):
                ge(dve, S["kT_ps"], TT * i + t + 1)
                dve.tensor_copy(KT[:, :, t * P:(t + 1) * P], psS[:, 512:1024].rearrange("p (a c) -> p a c", c=P)).then_inc(S["kT_sb"], 1)

            def step(i, la, lf):
                attn, ffn = la is not None, lf is not None
                turn = attn and ffn and la != lf
                def less_mean():
                    ge(dve, S["mean_ps"], i)
                    for k in range(KD):
                        last = dve.tensor_tensor(dF[:, k], dF[:, k], psF[:, 0:N], ALU.subtract)
                    last.then_inc(S["d_done"], 1)

                def high():
                    ge(dve, S["hn_done"], i)
                    dve.tensor_scalar(fhi[:, :, :], dF, 1.0, None, ALU.mult).then_inc(S["f_hi"], 1)

                def low_f():
                    ge(dve, S["f_hi"], i)
                    dve.tensor_tensor(flo[:, :, :], dF, fhi[:, :, :].bitcast(F32), ALU.subtract).then_inc(S["f_lo"], 1)

                if turn:
                    for k in range(KD):
                        W.low_wqkv(dve, 1, stage, k)
                if not attn:
                    less_mean()
                    dve.wait_ge(S["rstdF_done"], i)
                    dve.wait_ge(S["d_done"], i)
                    dve.tensor_tensor(dF, dF, rstdF[:, :].unsqueeze(1).broadcast_to([P, KD, N]), ALU.mult).then_inc(S["hn_done"], 1)
                    high()
                    low_f()
                if attn:
                    rotate(i, 0, la, less_mean if ffn else None)
                    rotate(i, 1, la)
                    k_evac(i, 0)
                if attn and ffn:
                    high()
                if attn:
                    rotate(i, 2, la, low_f if ffn else None)
                    k_evac(i, 1)
                    rotate(i, 3, la)
                    k_evac(i, 2)
                if ffn:
                    gated(i, 0, lf)
                    gated(i, 1, lf)
                if attn:
                    k_evac(i, 3)
                    ge(dve, S["rn_done"], TT * (i + 1))
                    dve.tensor_scalar(sc8[:, :, :], rn[:, :, 0:HEADS], QK_SCALE, None, ALU.mult)
                    dve.tensor_scalar(nsc8[:, :, :], rn[:, :, 0:HEADS], -QK_SCALE, None, ALU.mult).then_inc(S["sc_done"], 1)
                if ffn:
                    for j in range(2, HT):
                        gated(i, j, lf)
                if turn:
                    ge(dve, S["u_done"], HT * i)
                    dve.memset(stage1[:, :, 2 * HFULL * P:], 0.0).then_inc(WS["w1pad"], 1)
                if not attn:
                    add_ffn(i, 0, lf)
                else:
                    ge(dve, S["sc_done"], i + 1)
                    for h in range(HEADS + 2):
                        ps = scores_of[h % 2]
                        if h < HEADS:
                            n = HEADS * i + h + 1
                            ge(dve, S["s_ps"], n)
                            dve.reduce_max(mx[:, h % 2, 0:1], ps[:, P:2 * P], AX.X)
                            dve.reduce_max(mx[:, h % 2, 1:TT], ps[:, 2 * P:].rearrange("p (t c) -> p t c", c=2 * P), AX.X).then_inc(S["m_red"], 1)
                            ge(dve, S["m_red"], n)
                            dve.tensor_tensor(nb[:, h % 2, :], mx[:, h % 2, :], nsc8[:, :, h], ALU.mult).then_inc(S["m_bias"], 1)
                        if h == 0:
                            low((i + 1) % B, i + 2)
                        if h == 1 and ffn:
                            add_ffn(i, 0, lf)
                        if h >= 2:
                            ge(dve, S["pT_ps"], HEADS * i + h - 1)
                            dve.tensor_copy(PT[:, h % 2, 512:896], psP[:, 512:896]).then_inc(S["pT_sb1"], 1)
                        if h < HEADS:
                            ge(dve, S["exp_done"], HEADS * i + h + 1)
                            dve.reciprocal(rinv[:, h % 2, :], sums[:, h % 2, :]).then_inc(S["rinv_done"], 1)
                        if turn and 4 <= h < 4 + KD:
                            W.low_w1(dve, 1, stage1, h - 4)
                if ffn:
                    add_ffn(i, 1, lf)
                if attn:
                    ge(dve, S["wo_ps"], i + 1)
                    for k in range(KD):
                        xk = xT[:, bass.ds(i - B * la, 1), k * X1:k * X1 + N]
                        dve.tensor_tensor(xk, xk, psP[:, k * N:(k + 1) * N].unsqueeze(1), ALU.add).then_inc(S["x_attn"], 1)
                    if turn:
                        W.b1_columns(dve, 1, psF)
                    ge(dve, S["x_attn"], KD * (i + 1))
                    dve.tensor_scalar(dF, h_view(xT, i - B * la), 1.0, None, ALU.mult).then_inc(S["h_ready"], 1)
            low(0, 1)
            pipeline(dve, step)

        @block.tensor
        def _(pe):
            def project(i, t):
                for c in range(3):
                    n = 3 * (TT * i + t) + c
                    if t == 0 and c == 0:
                        ge(pe, S["h_lo"], i + 1)
                    elif t or c > 1:
                        ge(pe, S["proj_sb"], n - 1)
                    m = 0
                    for k in range(KD):
                        for a, w in ((hhi, wq_hi), (hhi, wq_lo), (hlo, wq_hi)):
                            last = pe.matmul(ring[(t + c) % 2][:, :], a[:, k, t * P:(t + 1) * P], w[:, k, c * INNER:(c + 1) * INNER],
                                             start=(m == 0), stop=(m == 3 * KD - 1))
                            m += 1
                    last.then_inc(S["proj_ps"], 1)

            def mean(i):
                ge(pe, S["h_ready"], i)
                for k in range(KD):
                    last = pe.matmul(psF[:, 0:N], ones[:, :], dF[:, k], start=(k == 0), stop=(k == KD - 1))
                last.then_inc(S["mean_ps"], 1)

            def variance(i):
                ge(pe, S["sqF_done"], i)
                for k in range(KD):
                    last = pe.matmul(psF[:, N:2 * N], ones[:, :], sqF[:, k, :], start=(k == 0), stop=(k == KD - 1))
                last.then_inc(S["var_ps"], 1)

            def hidden(i, j, attn):
                u = i - 1
                ge(pe, S["f_lo"], i)
                if j == 1 and attn:
                    ge(pe, S["proj_sb"], 3 * TT * (i + 1))
                if j >= 2:
                    ge(pe, S["u_done"], HT * u + j - 1)
                tiles = ((HFULL + j, 0), (j, 1)) if j < HFULL else ((2 * HFULL, 0),)
                for tile, bank in tiles:
                    m = 0
                    for k in range(KD):
                        for w, a in ((w1_hi, fhi), (w1_lo, fhi), (w1_hi, flo)):
                            last = pe.matmul(hidden_of[j % 2][bank], w[:, k, tile * P:(tile + 1) * P], a[:, k, :], start=(m == 0), stop=(m == 3 * KD - 1))
                            m += 1
                last.then_inc(S["w1_ps"], 1)

            def down(i, c, tiles):
                for k in tiles:
                    if c == 0 and k >= HFULL - 1:
                        ge(pe, S["u_done"], HT * (i - 1) + k + 1)
                    last = pe.matmul(down_of[c], w2[:, k, c * P:(c + 1) * P], U[:, k, :], start=(k == 0), stop=(k == HT - 1))
                if HT - 1 in tiles:
                    last.then_inc(S["w2_ps"], 1)

            def transposes(i, t):
                n = TT * i + t
                for j, (there, free, done) in enumerate((("rot_done", "qT_sb", "qT_ps"), ("k_scaled", "kT_sb", "kT_ps"))):
                    ge(pe, S[there], n + 1)
                    if t:
                        ge(pe, S[free], n)
                    for a in range(INNER // P):
                        last = pe.transpose(psS[:, j * 512 + a * P:j * 512 + (a + 1) * P],
                                            rot[:, t, j * INNER + a * P:j * INNER + (a + 1) * P], ident[:, :])
                    last.then_inc(S[done], 1)

            def scores(i, h):
                if h == 0:
                    ge(pe, S["qT_sb"], TT * (i + 1))
                    ge(pe, S["kT_sb"], TT * (i + 1))
                if h >= 2:
                    ge(pe, S["exp_done"], HEADS * i + h - 1)
                for t in range(TT):
                    c0 = P if t == 0 else 0
                    out = scores_of[h % 2][:, t * 2 * P + c0:(t + 1) * 2 * P]
                    pe.matmul(out, identb[:, :], maskT[:, c0:2 * P], start=True, stop=False)
                    last = pe.matmul(out, QT[:, h % 2, h // 2, t * P:(t + 1) * P], KT[:, h // 2, max(t - 1, 0) * P:(t + 1) * P], start=False, stop=True)
                last.then_inc(S["s_ps"], 1)

            def p_transposes(i, h, ffn):
                ge(pe, S["p_done"], HEADS * i + h + 1)
                if h:
                    ge(pe, S["pT_sb0"], HEADS * i + h)
                    ge(pe, S["pT_sb1"], HEADS * i + h)
                elif ffn:
                    ge(pe, S["x_ffn"], KD * (i - 1) + 1)
                for t in range(TT):
                    last = pe.transpose(psP[:, t * 2 * P:t * 2 * P + P], Pr[:, h % 2, t * 2 * P + P:(t + 1) * 2 * P], ident[:, :])
                    if t:
                        last = pe.transpose(psP[:, (t - 1) * 2 * P + P:t * 2 * P], Pr[:, h % 2, t * 2 * P:t * 2 * P + P], ident[:, :])
                last.then_inc(S["pT_ps"], 1)

            def values(i, h):
                pair, rows = h // 2, slice(h % 2 * DH, (h % 2 + 1) * DH)
                ge(pe, S["pT_sb0"], HEADS * i + h + 1)
                ge(pe, S["pT_sb1"], HEADS * i + h + 1)
                if h == 0:
                    ge(pe, S["proj_sb"], 3 * TT * (i + 1))
                if h % 2 == 0 and pair >= 2:
                    ge(pe, S["o_sb"], HEADS // 2 * i + pair - 1)
                for t in range(TT):
                    w = 2 * P if t < TT - 1 else P
                    last = pe.matmul(ring[pair % 2][rows, t * P:t * P + w], V[:, t, h * DH:(h + 1) * DH], PT[:, h % 2, t * 2 * P:t * 2 * P + w],
                                     start=(t == 0), stop=(t == TT - 1), skip_group_check=True)
                if h % 2:
                    last.then_inc(S["o_ps"], 1)

            def output(i):
                for a in range(INNER // P):
                    ge(pe, S["o_sb"], HEADS // 2 * i + a + 1)
                    for c in range(KD):
                        last = pe.matmul(psP[:, c * N:(c + 1) * N], wo[:, a, c * P:(c + 1) * P], OT[:, a, :],
                                         start=(a == 0), stop=(a == INNER // P - 1))
                last.then_inc(S["wo_ps"], 1)

            def step(i, la, lf):
                attn, ffn = la is not None, lf is not None
                turn = attn and ffn and la != lf
                if ffn and la != lf:
                    mean(i)
                if not attn:
                    variance(i)
                if turn:
                    pe.wait_ge(WS["wq_lo"], KD * LAYERS)
                if attn:
                    project(i, 0)
                if ffn and la == lf:
                    mean(i)
                if attn:
                    project(i, 1)
                if attn and ffn:
                    variance(i)
                if attn:
                    transposes(i, 0)
                    project(i, 2)
                    transposes(i, 1)
                    project(i, 3)
                if ffn:
                    hidden(i, 0, attn)
                if attn:
                    transposes(i, 2)
                if ffn:
                    hidden(i, 1, attn)
                if attn:
                    transposes(i, 3)
                if ffn:
                    for j in range(2, HT):
                        hidden(i, j, attn)
                if attn and la != lf:
                    pe.wait_ge(S["zeroed"], la + 1)
                if attn:
                    scores(i, 0)
                    if ffn:
                        ge(pe, S["u_done"], HT * (i - 1) + HFULL)
                    scores(i, 1)
                if ffn:
                    ge(pe, S["x_attn"], KD * i)
                    down(i, 0, range(HT))
                if attn:
                    for h in range(2, HEADS + 3):
                        if 2 <= h < HEADS:
                            scores(i, h)
                        if 2 <= h < HEADS + 2:
                            if ffn and h == HEADS:
                                ge(pe, S["exp_done"], HEADS * i + HEADS - 1)
                                down(i, 1, range(0, 2))
                            if ffn and h == HEADS + 1:
                                down(i, 1, range(2, HT))
                            p_transposes(i, h - 2, ffn)
                        if h >= 3:
                            values(i, h - 3)
                    if turn:
                        pe.wait_ge(WS["wo_in"], 16 * LAYERS)
                    output(i)
                    if turn:
                        ge(pe, S["exp_done"], HEADS * (i + 1))
                        W.b1_products(pe, 1, stage1, psF)
                        pe.wait_ge(WS["w1_lo"], KD * LAYERS)
                        pe.wait_ge(WS["w2_in"], 32 * LAYERS)
                else:
                    down(i, 1, range(HT))
            pe.wait_ge(WS["wq_lo"], KD)
            pe.wait_ge(WS["w1_lo"], KD)
            pe.wait_ge(WS["wo_in"], 16)
            pe.wait_ge(WS["w2_in"], 32)
            pipeline(pe, step)
        stack.close()
        combine_block(nc, outer, io, xT, ident, xs, xs_in, ffn_buf, (psS, psP))


def combine_block(nc, outer, io, xT, ident, xs, xs_in, buffers, banks):
    ctx = ExitStack()
    with ctx:
        x_in, s_in = xs[:, 0], xs[:, 1]
        yT = buffers[:, 0:2 * KD, :].rearrange("p (a k) n -> p a k n", a=2)
        E = buffers[:, 2 * KD:4 * KD, :].rearrange("p a n -> p (a n)").rearrange("p (a t d) -> p a t d", a=2, t=TT)
        Q = buffers[:, 4 * KD:6 * KD, :].rearrange("p a n -> p (a n)").rearrange("p (a t d) -> p a t d", a=2, t=TT)
        ps = [bank[:, :].rearrange("p (t d) -> p t d", t=TT) for bank in banks]
        names = "yT tr silu prod sum out".split()
        S = {n: outer.enter_context(nc.semaphore("c_" + n)) for n in names}
        block = ctx.enter_context(nc.Block())
        o_v = io["out"].rearrange("b (t p) d -> b p t d", p=P)

        def pairs(e, body):
            for par in range(2):
                body(0, par)
            with e.Fori(1, B // 2) as i:
                for par in range(2):
                    body(i, par)

        @block.sync
        def _(sp):
            def store(i, par):
                b = 2 * i + par
                ge(sp, S["sum"], b + 1)
                sp.dma_start(o_v[bass.ds(b, 1)].rearrange("b p t d -> p b t d"), x_in[:, bass.ds(b, 1)]).then_inc(S["out"], 16)
            pairs(sp, store)
            sp.wait_ge(S["out"], 16 * B)

        @block.gpsimd
        def _(pool):
            for half in range(2):
                pool.wait_ge(xs_in[half], 32)

            def body(i, par):
                b = 2 * i + par
                ge(pool, S["silu"], b + 1)
                ge(pool, S["sum"], b - 1)
                pool.tensor_tensor(Q[:, par].unsqueeze(1), E[:, par].unsqueeze(1), s_in[:, bass.ds(b, 1)], ALU.mult).then_inc(S["prod"], 1)
            pairs(pool, body)

        @block.scalar
        def _(act):
            def silu(i, par):
                b = 2 * i + par
                ge(act, S["tr"], b + 1)
                ge(act, S["prod"], b - 1)
                act.activation(E[:, par], ps[par][:, :, :], ACT.Silu).then_inc(S["silu"], 1)

            pairs(act, silu)

        @block.vector
        def _(dve):
            def copy(i, par):
                b = 2 * i + par
                ge(dve, S["tr"], b - 1)
                dve.tensor_scalar(yT[:, par], x_view(xT, b), 1.0, None, ALU.mult).then_inc(S["yT"], 1)

            def add_x(i, par):
                b = 2 * i + par
                ge(dve, S["prod"], b + 1)
                xb = x_in[:, bass.ds(b, 1)]
                dve.tensor_tensor(xb, Q[:, par].unsqueeze(1), xb, ALU.add).then_inc(S["sum"], 1)

            for half in range(2):
                dve.wait_ge(xs_in[half], 32)
            for par in range(2):
                copy(0, par)
            with dve.Fori(1, B // 2) as i:
                for par in range(2):
                    copy(i, par)
                    add_x(i - 1, par)
            for par in range(2):
                add_x(B // 2 - 1, par)

        @block.tensor
        def _(pe):
            def body(i, par):
                b = 2 * i + par
                ge(pe, S["yT"], b + 1)
                ge(pe, S["silu"], b - 1)
                for t in range(TT):
                    for k in range(KD):
                        last = pe.transpose(ps[par][:, t, k * P:(k + 1) * P], yT[:, par, k, t * P:(t + 1) * P], ident[:, :])
                last.then_inc(S["tr"], 1)
            pairs(pe, body)


def build(nc, io):
    with ExitStack() as ctx:
        xT = ctx.enter_context(nc.sbuf_tensor("xT", [P, B, XW], F32))
        ident = ctx.enter_context(nc.sbuf_tensor("ident", [P, P], F32))
        identb = ctx.enter_context(nc.sbuf_tensor("identb", [P, P], BF16))
        ones = ctx.enter_context(nc.sbuf_tensor("ones", [P, P], F32))
        epsc = ctx.enter_context(nc.sbuf_tensor("eps", [P, 1], F32))
        W = Weights(ctx, nc, io)
        attention_block(nc, ctx, io, W, xT, ident, identb, ones, epsc)
        layers_block(nc, ctx, io, W, xT, ident, identb, ones, epsc)


def shape_constants():
    f = np.float32
    i = np.arange(D // 2, dtype=f)
    theta = np.power(f(10000.0), f(-2.0) * (i - f(1.0)) / f(D)).astype(f)
    pos = np.arange(N, dtype=f)
    ang = pos[:, None] * theta[None, :]
    c, s = np.cos(ang).astype(f), np.sin(ang).astype(f)
    acos = np.repeat(c, 2, axis=1)
    asin = np.stack((s, -s), axis=-1).reshape(N, D)
    half = np.arange(0, DH, 2, dtype=f)
    inv = (f(1.0) / np.power(f(10000.0), half / f(DH))).astype(f)
    fr = pos[:, None] * inv[None, :]
    fr = np.concatenate([fr, fr], axis=-1)
    base = (half + f(0.4 * DH)) / f(1.4 * DH)
    power = (pos - f(N // 2)) / f(P // 2)
    xs = np.power(base[None, :], power[:, None]).astype(f)
    xs = np.concatenate([xs, xs], axis=-1)
    c, s = np.cos(fr).astype(f), np.sin(fr).astype(f)
    sign = np.concatenate([-np.ones(DH // 2, f), np.ones(DH // 2, f)])
    fcos = np.stack([c * xs, c / xs], axis=1)
    fsin = np.stack([s * xs * sign, s / xs * sign], axis=1)

    def rows(a):
        return np.ascontiguousarray(a.reshape(TT, P, *a.shape[1:]).swapaxes(0, 1).astype(f))
    q, k = np.arange(P)[:, None], np.arange(P)[None, :]
    own = np.where(k <= q, f(0), f(-3e38))
    prev = np.where(k >= q, f(0), f(-3e38))
    amask = np.concatenate([np.zeros((P, N - P), f), own], axis=1)
    fmask = np.concatenate([prev, own], axis=1)
    return dict(acos=rows(acos), asin=rows(asin), fcos=rows(fcos), fsin=rows(fsin), amask=amask, fmask=fmask, ident=np.eye(P, dtype=f))


NAMES = dict(x="L0_attn_x", wq="L0_attn_w_q", wk="L0_attn_w_k", wv="L0_attn_w_v", wqkv="L0_ffn_wqkv", q_scale="L0_ffn_q_scale",
             k_scale="L0_ffn_k_scale", wo="L0_ffn_wo", ln_g="L0_ffn_ln_g", ln_b="L0_ffn_ln_b", w1="L0_ffn_w1", b1="L0_ffn_b1",
             w2="L0_ffn_w2", b2="L0_ffn_b2")


def kernel(**inputs):
    import ml_dtypes
    import concourse.bacc as _bacc
    from concourse.bass_utils import run_bass_kernel_spmd as _run

    nc = _bacc.Bacc("TRN2", target_bir_lowering=False, num_devices=1)
    arrays, io = {}, {}
    for short, name in NAMES.items():
        arrays[f"in_{short}"] = np.ascontiguousarray(inputs[name])
    for short, a in shape_constants().items():
        arrays[f"in_{short}"] = a.astype(ml_dtypes.bfloat16) if short.endswith("mask") else a
    for key, a in arrays.items():
        io[key[3:]] = nc.dram_tensor(key, a.shape, mybir.dt.from_np(a.dtype), kind="ExternalInput").ap()
    io["s"] = nc.dram_tensor("scratch_s", (B, N, D), F32, kind="Internal").ap()
    io["out"] = nc.dram_tensor("out_dram", (B, N, D), F32, kind="ExternalOutput").ap()
    build(nc, io)
    r = _run(nc, [arrays], core_ids=[0])
    return r.results[0]["out_dram"]
```
